# Optimizing a Trainium2 kernel written in Bass

```python
import numpy as np
import jax
import jax.numpy as jnp

def _softmax(x, axis=-1):
    return jax.nn.softmax(x, axis=axis)

def _gelu(x):
    return jax.nn.gelu(x, approximate=True)

def _silu(x):
    return jax.nn.silu(x)

def _sigmoid(x):
    return jax.nn.sigmoid(x)

def _layernorm(x, axis=-1, eps=1e-05):
    m = jnp.mean(x, axis=axis, keepdims=True)
    v = jnp.var(x, axis=axis, keepdims=True)
    return (x - m) / jnp.sqrt(v + eps)

def _scatter_add(tgt, idx, src, axis=0):
    return tgt.at[idx].add(src)

def _segment_sum(src, seg, n):
    return jax.ops.segment_sum(src, seg, n)
kernel_name = 'mk_gps_d1_gnn_r8_55468f'

def setup_inputs(seed: int=0):
    np.random.seed(seed)
    _w = jnp.asarray

    def _rec_inputs():
        import jax
        import jax.numpy as jnp
        _gk = jax.random.key(seed)
        x = -8.776e-05 + 1 * jax.random.normal(jax.random.fold_in(_gk, 1), (1250, 512), jnp.float32)
        src = jax.random.randint(jax.random.fold_in(_gk, 2), (20000,), 0, 1250, jnp.int32)
        dst = jnp.minimum((1250 * jax.random.uniform(jax.random.fold_in(_gk, 3), (20000,)) ** 2.0).astype(jnp.int32), 9999)
        _o = jnp.argsort(dst, stable=True)
        src = src[_o]
        dst = dst[_o]
        edge_weight = jax.random.uniform(jax.random.fold_in(_gk, 12), (20000,), jnp.float32, 0.0, 0.999996)
        return (x, src, dst, edge_weight)
    x, src, dst, edge_weight = _rec_inputs()

    def _L0_gnn_setup():
        import jax, jax.numpy as jnp
        import numpy as np
        N = 1250
        E = 20000
        D_IN = 512
        D_OUT = 512
        key = jax.random.key(seed)
        k1, k2, k3, k4, k5 = jax.random.split(key, 5)
        x = jax.random.normal(k1, (N, D_IN), dtype=jnp.float32)
        edge_index = jax.random.randint(k2, (2, E), 0, N, dtype=jnp.int64)
        edge_attr = jax.random.uniform(k3, (E,), dtype=jnp.float32)
        W = jax.random.normal(k4, (D_IN, D_OUT), dtype=jnp.float32) * 0.05
        b = jax.random.normal(k5, (D_OUT,), dtype=jnp.float32) * 0.05
        return {'x': x, 'edge_index': edge_index, 'edge_attr': edge_attr, 'W': W, 'b': b}
    _L0_gnn_all = _L0_gnn_setup()
    _L0_gnn_in = {k: v for k, v in _L0_gnn_all.items() if k in ('W', 'b')}
    del _L0_gnn_all

    def _L0_mix_setup():
        import jax, jax.numpy as jnp
        import numpy as np
        DIM = 512
        HEADS = 8
        HEAD_DIM = DIM // HEADS
        key = jax.random.key(seed)
        ks = jax.random.split(key, 9)
        B, T, C = (8, 1024, DIM)
        s = 1.0 / np.sqrt(C)
        x = jax.random.normal(ks[0], (B, T, C), dtype=jnp.float32)
        Wq = jax.random.uniform(ks[1], (C, C), jnp.float32, -s, s)
        bq = jax.random.uniform(ks[2], (C,), jnp.float32, -s, s)
        Wk = jax.random.uniform(ks[3], (C, C), jnp.float32, -s, s)
        bk = jax.random.uniform(ks[4], (C,), jnp.float32, -s, s)
        Wv = jax.random.uniform(ks[5], (C, C), jnp.float32, -s, s)
        bv = jax.random.uniform(ks[6], (C,), jnp.float32, -s, s)
        Wo = jax.random.uniform(ks[7], (C, C), jnp.float32, -s, s)
        bo = jax.random.uniform(ks[8], (C,), jnp.float32, -s, s)
        return {'x': x, 'Wq': Wq, 'bq': bq, 'Wk': Wk, 'bk': bk, 'Wv': Wv, 'bv': bv, 'Wo': Wo, 'bo': bo}
    _L0_mix_all = _L0_mix_setup()
    _L0_mix_in = {k: v for k, v in _L0_mix_all.items() if k in ('Wq', 'bq', 'Wk', 'bk', 'Wv', 'bv', 'Wo', 'bo')}
    del _L0_mix_all

    def _L0_ffn_setup():
        import jax, jax.numpy as jnp
        import numpy as np
        B, N, D, E = (8, 1024, 512, 8)
        H = 2 * D
        key = jax.random.key(seed)
        ks = jax.random.split(key, 7)
        s = 0.02
        return {'x': jax.random.normal(ks[0], (B, N, D), dtype=jnp.float32), 'W1': jax.random.normal(ks[1], (E, D, H), dtype=jnp.float32) * s, 'b1': jnp.zeros((E, H), dtype=jnp.float32), 'W2': jax.random.normal(ks[2], (E, H, D), dtype=jnp.float32) * s, 'b2': jnp.zeros((E, D), dtype=jnp.float32), 'Wg': jax.random.normal(ks[3], (D, E), dtype=jnp.float32) * s, 'bg': jnp.zeros((E,), dtype=jnp.float32)}
    _L0_ffn_all = _L0_ffn_setup()
    _L0_ffn_in = {k: v for k, v in _L0_ffn_all.items() if k in ('W1', 'b1', 'W2', 'b2', 'Wg', 'bg')}
    del _L0_ffn_all
    return {'x': x, 'src': src, 'dst': dst, 'edge_weight': edge_weight, 'L0_gnn_W': _L0_gnn_in['W'], 'L0_gnn_b': _L0_gnn_in['b'], 'L0_mix_Wq': _L0_mix_in['Wq'], 'L0_mix_bq': _L0_mix_in['bq'], 'L0_mix_Wk': _L0_mix_in['Wk'], 'L0_mix_bk': _L0_mix_in['bk'], 'L0_mix_Wv': _L0_mix_in['Wv'], 'L0_mix_bv': _L0_mix_in['bv'], 'L0_mix_Wo': _L0_mix_in['Wo'], 'L0_mix_bo': _L0_mix_in['bo'], 'L0_ffn_W1': _L0_ffn_in['W1'], 'L0_ffn_b1': _L0_ffn_in['b1'], 'L0_ffn_W2': _L0_ffn_in['W2'], 'L0_ffn_b2': _L0_ffn_in['b2'], 'L0_ffn_Wg': _L0_ffn_in['Wg'], 'L0_ffn_bg': _L0_ffn_in['bg']}

def reference(x, src, dst, edge_weight, L0_gnn_W, L0_gnn_b, L0_mix_Wq, L0_mix_bq, L0_mix_Wk, L0_mix_bk, L0_mix_Wv, L0_mix_bv, L0_mix_Wo, L0_mix_bo, L0_ffn_W1, L0_ffn_b1, L0_ffn_W2, L0_ffn_b2, L0_ffn_Wg, L0_ffn_bg):
    import jax
    import jax.numpy as jnp

    def _L0_gnn_ref(x, edge_index, edge_attr, W, b):
        import jax, jax.numpy as jnp
        import numpy as np
        N = 1250
        E = 20000
        D_IN = 512
        D_OUT = 512
        n = x.shape[0]
        row, col = (edge_index[0], edge_index[1])
        loop = jnp.arange(n, dtype=edge_index.dtype)
        row_f = jnp.concatenate([row, loop])
        col_f = jnp.concatenate([col, loop])
        ew = jnp.concatenate([edge_attr, jnp.ones((n,), dtype=edge_attr.dtype)])
        deg = jax.ops.segment_sum(ew, col_f, num_segments=n)
        dinv = jnp.where(deg > 0, jax.lax.rsqrt(deg), 0.0)
        norm = dinv[row_f] * ew * dinv[col_f]
        h = x @ W
        msg = h[row_f] * norm[:, None]
        out = jax.ops.segment_sum(msg, col_f, num_segments=n)
        return out + b

    def _L0_mix_ref(x, Wq, bq, Wk, bk, Wv, bv, Wo, bo):
        import jax, jax.numpy as jnp
        import numpy as np
        DIM = 512
        HEADS = 8
        HEAD_DIM = DIM // HEADS
        B, T, C = x.shape
        H, D = (HEADS, HEAD_DIM)

        def proj(W, b):
            return (x @ W.T + b).reshape(B, T, H, D).transpose(0, 2, 1, 3)
        Q = proj(Wq, bq)
        K = proj(Wk, bk)
        V = proj(Wv, bv)
        Q = jax.nn.elu(Q) + 1.0
        K = jax.nn.elu(K) + 1.0
        KV = jnp.einsum('bhnd,bhne->bhde', K, V)
        Q_KV = jnp.einsum('bhnd,bhde->bhne', Q, KV)
        K_sum = K.sum(axis=2)
        normalizer = jnp.einsum('bhnd,bhd->bhn', Q, K_sum)
        out = Q_KV / (normalizer[..., None] + 1e-06)
        out = out.transpose(0, 2, 1, 3).reshape(B, T, C)
        out = out @ Wo.T + bo
        return out

    def _L0_ffn_ref(x, W1, b1, W2, b2, Wg, bg):
        import jax, jax.numpy as jnp
        import numpy as np
        B, N, D, E = (8, 1024, 512, 8)
        H = 2 * D
        Bs, Ns, Ds = x.shape
        xf = x.reshape(Bs * Ns, Ds)
        logits = xf @ Wg + bg
        idx = jnp.argmax(logits, axis=-1)
        out = jnp.zeros_like(xf)
        num_experts = W1.shape[0]
        for e in range(num_experts):
            h = jax.nn.relu(xf @ W1[e] + b1[e])
            y = h @ W2[e] + b2[e]
            out = jnp.where((idx == e)[:, None], y, out)
        return out.reshape(Bs, Ns, Ds)
    edge_index = jnp.stack([src, dst])
    xn = _layernorm(x, axis=-1)
    x = x + _L0_gnn_ref(xn, edge_index, edge_weight, L0_gnn_W, L0_gnn_b) + _L0_mix_ref(xn[None], L0_mix_Wq, L0_mix_bq, L0_mix_Wk, L0_mix_bk, L0_mix_Wv, L0_mix_bv, L0_mix_Wo, L0_mix_bo)[0]
    x = x + _L0_ffn_ref(_layernorm(x, axis=-1)[None], L0_ffn_W1, L0_ffn_b1, L0_ffn_W2, L0_ffn_b2, L0_ffn_Wg, L0_ffn_bg)[0]
    return x

_drawn_inputs = setup_inputs


def setup_inputs(seed=0):
    import zlib

    import numpy as np

    out = dict(_drawn_inputs(seed))
    spreads = {'L0_ffn_b1': (0.0, 0.1), 'L0_ffn_b2': (0.0, 0.1), 'L0_ffn_bg': (0.0, 0.1)}
    factors = {'L0_mix_Wq': 8.0, 'L0_mix_bq': 8.0, 'L0_mix_Wk': 8.0, 'L0_mix_bk': 8.0, 'L0_mix_Wv': 3.206}
    for name, (base, spread) in spreads.items():
        noise = np.random.default_rng([zlib.crc32(name.encode()), seed]).standard_normal(out[name].shape)
        drawn = base * np.exp(spread * noise) if base else spread * noise
        out[name] = jnp.asarray(drawn.astype(out[name].dtype))
    for name, factor in factors.items():
        out[name] = (out[name] * factor).astype(out[name].dtype)
    return out
```

```python
from contextlib import ExitStack

import concourse.bass as bass
from concourse import mybir

F32 = mybir.dt.float32
I32 = mybir.dt.int32
U32 = mybir.dt.uint32
ALU = mybir.AluOpType
ACT = mybir.ActivationFunctionType
AX_X = mybir.AxisListType.X

P = 128
N = 1250
D = 512
HEAD = 64
E = 20000
NE = 8
H = 2 * D
T = -(-N // P)
LAST = N - (T - 1) * P
KC = D // P
HC = H // P
NP = T * P
EC = 160
G = 4
DG = 8
BLK = 192
B2ND = BLK - P
BLOCKS = (N + NE * (BLK - 1)) // BLK
PAIRS = BLOCKS // 2
MIN_BLOCKS = -(-N // BLK)
WROW = KC * H + HC * D + HC + KC
EPS = 1e-5
QG = KC * 3
VW = P + 2
assert G == KC and EC * P >= E + 3 * P and EC % (2 * DG) == 0 and BLOCKS % 2 == 0


def n_blocks():
    return [(0, 512), (512, 512), (1024, NP - 1024)]


def transformer_layer(nc, x, src, dst, ew, wq, wk, wv, wo, wg_nn, bq, brow, gate_w, gate_b, experts, out):
    scaled_rows = nc.dram_tensor("scaled_rows", [NP, D], F32)
    token_rows = nc.dram_tensor("token_rows", [NP, 2 * D], F32)
    slot_tokens = nc.dram_tensor("slot_tokens", [BLK * BLOCKS, 1], I32)

    with ExitStack() as ctx:
        def sb(name, shape, dt=F32):
            return ctx.enter_context(nc.sbuf_tensor(name, shape, dt))

        def sem(name):
            return ctx.enter_context(nc.semaphore(name))

        xres = sb("xres", [P, T, D])
        xn = sb("xn", [P, T, D])
        xT_ = sb("xT_", [P, KC * NP])
        xnT = xT_[:, :].rearrange("p (c n) -> p c n", c=KC)
        qT_ = sb("qT_", [P, KC * NP])
        qT = qT_[:, :].rearrange("p (c n) -> p c n", c=KC)
        ffw = sb("ffw", [P, 2, WROW])
        early = ffw[:, :, :].rearrange("p a n -> p (a n)")
        wk_sb = early[:, 0:KC * D].rearrange("p (c n) -> p c n", c=KC)
        wv_sb = early[:, KC * D:2 * KC * D].rearrange("p (c n) -> p c n", c=KC)
        k_sb = early[:, 2 * KC * D:2 * KC * D + T * D].rearrange("p (t n) -> p t n", t=T)
        v_at = 2 * KC * D + T * D
        wq_sb = early[:, v_at:v_at + KC * D].rearrange("p (c n) -> p c n", c=KC)
        v_sb = early[:, v_at:v_at + T * KC * VW].rearrange("p (t c n) -> p t c n", t=T, c=KC)
        spare = early[0:1, v_at + T * KC * VW:v_at + T * KC * VW + T * EC]
        late = sb("late", [P, 3 * KC * D])
        w_sb = late[:, 0:KC * D].rearrange("p (c n) -> p c n", c=KC)
        wo_sb = late[:, KC * D:2 * KC * D].rearrange("p (c n) -> p c n", c=KC)
        m_sb = late[:, 2 * KC * D:3 * KC * D].rearrange("p (c n) -> p c n", c=KC)
        in_tile = late[:, 0:T * EC].rearrange("p (t c) -> p t c", t=T)
        deg_coef = late[:, T * EC:2 * T * EC].rearrange("p (c t) -> p c t", t=T)
        deg_hot = late[:, 2 * T * EC:2 * T * EC + 2 * DG * P].rearrange("p (b c n) -> p b c n", b=2, c=DG)
        dst_sb, dst_hi, dst_lo, dst_hif, dst_lof = (
            late[:, 2 * T * EC + 2 * DG * P + n * EC:2 * T * EC + 2 * DG * P + (n + 1) * EC] for n in range(5))
        dst_sb, dst_hi, dst_lo = (a.bitcast(I32) for a in (dst_sb, dst_hi, dst_lo))
        assert 2 * T * EC + 2 * DG * P + 5 * EC <= 3 * KC * D

        ring = sb("ring", [P, G, D])
        hot = sb("hot", [P, G, P])
        src_sb = sb("src_sb", [P, EC], I32)
        edge = sb("edge", [P, 2, EC])
        edge_now = sb("edge_now", [P, 2, G])
        src_now = sb("src_now", [P, G], I32)
        col_i = sb("col_i", [P, P], I32)
        col_f = sb("col_f", [P, P])
        col_t = sb("col_t", [P, P])
        token_i = sb("token_i", [P, T], I32)
        token_f = sb("token_f", [P, T])
        valid = sb("valid", [P, T])
        falling_i = sb("falling_i", [P, NE], I32)
        falling = sb("falling", [P, NE])
        chunk_i = early[0:1, v_at + T * KC * VW + T * EC:][:, 0:EC].bitcast(I32)
        chunk_f = early[0:1, v_at + T * KC * VW + T * EC:][:, EC:2 * EC]
        blk_i = sb("blk_i", [P, BLOCKS], I32)
        blk_f = sb("blk_f", [P, BLOCKS])
        ident = sb("ident", [P, P])
        before = sb("before", [P, P])
        ones = sb("ones", [P, P])
        same_head = sb("same_head", [P, P])
        zrow = sb("zrow", [1, D], mybir.dt.bfloat16)
        bq_sb = sb("bq_sb", [P, KC])
        brow_sb = sb("brow_sb", [P, 3, D])
        gw_sb = sb("gw_sb", [P, KC, NE])
        gb_sb = sb("gb_sb", [P, NE])
        stat = sb("stat", [P, 2, 6])
        mv = sb("mv", [P, T, 2])
        veps = sb("veps", [P, T])
        std = sb("std", [P, T])
        rstd = sb("rstd", [P, T])
        deg = sb("deg", [P, T])
        degpos = sb("degpos", [P, T])
        degroot = sb("degroot", [P, T])
        dinv = sb("dinv", [P, T])
        dinv2 = sb("dinv2", [P, T])
        seenk = sb("seenk", [1, T])
        first_f = sb("first_f", [1, T])
        end_f = sb("end_f", [1, T])
        any_f = sb("any_f", [1, T])
        len_i = sb("len_i", [1, T], I32)
        len_f = sb("len_f", [1, T])
        zero_t = sb("zero_t", [P, T])
        walk = sb("walk", [1, 2 * T + 2], I32)
        halves = sb("halves", [P, 6 * D])
        biased, low, expd = (halves[:, n * 2 * D:(n + 1) * 2 * D].rearrange("p (b n) -> p b n", b=2) for n in range(3))
        rows2 = halves[:, 0:4 * D].rearrange("p (b n) -> p b n", b=2)
        x2T = halves[:, 4 * D:6 * D].rearrange("p (b c n) -> p b c n", b=2, c=KC)
        kvm, ksm = (halves[:, n * D:(n + 1) * D].rearrange("p (c n) -> p c n", c=KC) for n in range(2))
        kvT = hot
        seen = ring[0:1, :, :].rearrange("p j n -> p (j n)")[:, 0:T * EC].rearrange("p (t c) -> p t c", t=T)
        seen2 = spare.rearrange("p (t c) -> p t c", t=T)
        logit = sb("logit", [P, T, NE])
        best = sb("best", [P, T])
        top = sb("top", [P, T, NE])
        choice = sb("choice", [P, T, NE])
        rank = sb("rank", [P, T, NE])
        count = sb("count", [P, NE])
        countT = sb("countT", [P, NE])
        nblk = sb("nblk", [P, NE])
        blk_end = sb("blk_end", [P, NE])
        blk_start = sb("blk_start", [P, NE])
        pick = sb("pick", [P, T, NE])
        rank_t = sb("rank_t", [P, T])
        start_t = sb("start_t", [P, T])
        over_t = sb("over_t", [P, T])
        slot_f = sb("slot_f", [P, T])
        slot_i = sb("slot_i", [P, T], I32)
        blk_e = sb("blk_e", [P, BLOCKS])
        plan = sb("plan", [1, BLOCKS + 1], I32)
        empty = sb("empty", [P, BLK * BLOCKS // P], I32)
        slots_a = sb("slots_a", [P, BLOCKS + 2], I32)
        slots_b = sb("slots_b", [B2ND, BLOCKS + 2], I32)
        now_a = sb("now_a", [P, 2], I32)
        now_b = sb("now_b", [B2ND, 2], I32)
        xg = xT_[:, 0:2 * 2 * 2 * D].rearrange("p (b s n) -> p b s n", b=2, s=2)
        xgT = qT_[:, 0:KC * BLK].rearrange("p (c n) -> p c n", c=KC)
        hT = qT_[:, KC * BLK:(KC + HC) * BLK].rearrange("p (c n) -> p c n", c=HC)
        yT = qT_[:, (KC + HC) * BLK:(2 * KC + HC) * BLK].rearrange("p (c n) -> p c n", c=KC)
        yo = xn[:, 0:4, :].rearrange("p (b s) n -> p b s n", b=2)
        w1 = [ffw[:, b, 0:KC * H].rearrange("p (c n) -> p c n", c=KC) for b in range(2)]
        w2 = [ffw[:, b, KC * H:KC * H + HC * D].rearrange("p (c n) -> p c n", c=HC) for b in range(2)]
        b1 = [ffw[:, b, KC * H + HC * D:KC * H + HC * D + HC] for b in range(2)]
        b2 = [ffw[:, b, KC * H + HC * D + HC:WROW] for b in range(2)]

        ps = ctx.enter_context(nc.psum_tensor("ps", [P, 8, 512], F32))
        TRB, PRB = (0, 1), (2, 3, 4, 5)

        x_in = [sem(f"x_in{t}") for t in range(T)]
        edges_in, wq_in, wk_in, wv_in, wwo_in, small_in = (sem(s) for s in
            ("edges_in", "wq_in", "wk_in", "wv_in", "wwo_in", "small_in"))
        bo_in = sem("bo_in")
        pool_passed = sem("pool_passed")
        const_set, x_pad_set = sem("const_set"), sem("x_pad_set")
        dve_step, act_step, pool_step = sem("dve_step"), sem("act_step"), sem("pool_step")
        var_ready, std_ready = sem("var_ready"), sem("std_ready")
        xn_ready = sem("xn_ready")
        tr_done, tr_free = sem("tr_done"), sem("tr_free")
        mm_done, mm_free = sem("mm_done"), sem("mm_free")
        q_free, elu_done = sem("q_free"), sem("elu_done")
        low_ready, exp_done = sem("low_ready"), sem("exp_done")
        seen_done, coef_ready, hot8_ready, hot8_used, deg_done = (sem(s) for s in
            ("seen_done", "coef_ready", "hot8_ready", "hot8_used", "deg_done"))
        root_ask, root_ready = sem("root_ask"), sem("root_ready")
        walk_ready = sem("walk_ready")
        late_free = sem("late_free")
        scaled_ready = sem("scaled_ready")
        scaled_out = [sem(f"scaled_out{s}") for s in range(G)]
        kv_done, kv_masked = sem("kv_done"), sem("kv_masked")
        gathered = [sem(f"gathered{j}") for j in range(G)]
        hot_ready = [sem(f"hot_ready{j}") for j in range(G)]
        summed = [sem(f"summed{j}") for j in range(G)]
        tile_summed, agg_ready = sem("tile_summed"), sem("agg_ready")
        it_dve = sem("it_dve")
        it_pool = sem("it_pool")
        var2_ready, std2_ready, rows2_ready, x2_ready = (sem(s) for s in ("var2_ready", "std2_ready", "rows2_ready", "x2_ready"))
        rows2_out = [sem(f"rows2_out{b}") for b in range(2)]
        logits_done, choice_ready, rank_done, plan_ready = (sem(s) for s in
            ("logits_done", "choice_ready", "rank_done", "plan_ready"))
        empty_set, empty_out, ids_out, slots_in, now_set = (sem(s) for s in ("empty_set", "empty_out", "ids_out", "slots_in", "now_set"))
        w_in = [sem(f"w_in{b}") for b in range(2)]
        xg_in = [sem(f"xg_in{b}") for b in range(2)]
        out_done = [sem(f"out_done{b}") for b in range(2)]
        xgT_done, xgT_act, xgT_dve, h_done, h_ready, y_done, y_ready, yr_done, yo_ready = (sem(s) for s in
            ("xgT_done", "xgT_act", "xgT_dve", "h_done", "h_ready", "y_done", "y_ready", "yr_done", "yo_ready"))

        NB = n_blocks()
        groups = ([("q", m, b) for m in range(KC) for b in range(3)]
                  + [("k", t, 0) for t in range(T)] + [("v", t, 0) for t in range(T)]
                  + [("m", j, 0) for j in range(KC)] + [("norm", j, b) for j in range(KC) for b in range(3)]
                  + [("out", t, 0) for t in range(T)])
        group_no = {g: i for i, g in enumerate(groups)}
        turns = [("xn", t) for t in range(T)] + [("kv", 0), ("agg", 0)]
        for t in range(T):
            if t + 1 < T:
                turns.append(("agg", t + 1))
            if t >= 1:
                turns.append(("x2", t - 1))
        turns.append(("x2", T - 1))
        turn_no = {g: i for i, g in enumerate(turns)}

        block = ctx.enter_context(nc.Block())

        @block.sync
        def _(sp):
            for t in range(T - 1):
                sp.dma_start(xres[:, t, :], x[t * P:(t + 1) * P, :]).then_inc(x_in[t], 16)
            sp.wait_ge(x_pad_set, 1)
            sp.dma_start(xres[0:LAST, T - 1, :], x[(T - 1) * P:N, :]).then_inc(x_in[T - 1], 16)
            sp.dma_start(wk_sb, wk).then_inc(wk_in, 16)
            sp.dma_start(wv_sb, wv).then_inc(wv_in, 16)
            sp.wait_ge(mm_free, T)
            sp.dma_start(brow_sb[:, 0, :], brow[3:4, :].to_broadcast([P, D])).then_inc(bo_in, 16)
            sp.wait_ge(late_free, 1)
            sp.dma_start(w_sb, wg_nn).then_inc(wwo_in, 16)
            sp.dma_start(wo_sb, wo).then_inc(wwo_in, 16)
            for t in range(T):
                sp.wait_ge(scaled_ready, t + 1)
                sp.dma_start(scaled_rows[t * P:(t + 1) * P, :], ring[:, t % G, :]).then_inc(scaled_out[t % G], 16)
            for t in range(T):
                sp.wait_ge(rows2_ready, t + 1)
                sp.dma_start(token_rows[t * P:(t + 1) * P, :], rows2[:, t % 2, :]).then_inc(rows2_out[t % 2], 16)
            sp.wait_ge(plan_ready, 1)
            sp.wait_ge(mm_done, len(groups))
            blocks = sp.value_load(plan[0:1, BLOCKS:BLOCKS + 1], min_val=MIN_BLOCKS, max_val=BLOCKS)
            e0 = sp.value_load(plan[0:1, 0:1], min_val=0, max_val=NE - 1)
            sp.dma_start(ffw[:, 0, :], experts[bass.ds(e0, 1), :, :].rearrange("a p n -> p (a n)")).then_inc(w_in[0], 16)
            e1 = sp.value_load(plan[0:1, 1:2], min_val=0, max_val=NE - 1)
            sp.dma_start(ffw[:, 1, :], experts[bass.ds(e1, 1), :, :].rearrange("a p n -> p (a n)")).then_inc(w_in[1], 16)
            with sp.Fori(0, PAIRS - 1) as q:
                for b in range(2):
                    with sp.If(q * 2 + (2 + b) < blocks):
                        sp.wait_ge(y_ready, q * (2 * KC) + (b + 1) * KC)
                        e = sp.value_load(plan[0:1, bass.ds(q * 2 + (2 + b), 1)], min_val=0, max_val=NE - 1)
                        sp.dma_start(ffw[:, b, :], experts[bass.ds(e, 1), :, :].rearrange("a p n -> p (a n)")).then_inc(w_in[b], 16)

        @block.scalar
        def _(act):
            act.dma_start(dst_sb[:, :], dst).then_inc(edges_in, 16)
            act.dma_start(edge[:, 1, :], ew).then_inc(edges_in, 16)
            act.dma_start(src_sb[:, :], src).then_inc(edges_in, 16)
            act.dma_start(wq_sb, wq).then_inc(wq_in, 16)
            act.dma_start(bq_sb[:, :], bq).then_inc(small_in, 16)
            for n in range(3):
                act.dma_start(brow_sb[:, n, :], brow[n:n + 1, :].to_broadcast([P, D])).then_inc(small_in, 16)
            act.dma_start(gw_sb[:, :, :], gate_w).then_inc(small_in, 16)
            act.dma_start(gb_sb[:, :], gate_b.to_broadcast([P, NE])).then_inc(small_in, 16)

            def empty_turn(kind, t, to):
                n = turn_no[(kind, t)]
                act.wait_ge(tr_done, n + 1)
                nc.scalar.activation(to, ps[:, TRB[n % 2], :].rearrange("p (c n) -> p c n", c=KC), ACT.Copy).then_inc(tr_free, 1)

            act.wait_ge(var_ready, 1)
            nc.scalar.activation(std[:, :], veps[:, :], ACT.Sqrt).then_inc(std_ready, 1)
            for t in range(T):
                empty_turn("xn", t, xnT[:, :, t * P:(t + 1) * P])
            act.wait_ge(small_in, 16 * 6)
            def q_bias(n):
                m, cols = n // 3, NB[n % 3][1]
                act.wait_ge(mm_done, n + 1)
                if n >= 2:
                    act.wait_ge(elu_done, n - 1)
                nc.scalar.activation(biased[:, n % 2, 0:cols], ps[:, PRB[n % 4], 0:cols], ACT.Identity,
                                     bias=bq_sb[:, m:m + 1]).then_inc(q_free, 1)

            def exp_low(n):
                cols = NB[n % 3][1] if n < QG else D
                act.wait_ge(low_ready, n + 1)
                if n >= 2:
                    act.wait_ge(elu_done, n - 1)
                nc.scalar.activation(expd[:, n % 2, 0:cols], low[:, n % 2, 0:cols], ACT.Exp).then_inc(exp_done, 1)

            for n in range(QG + T):
                if n < QG:
                    q_bias(n)
                if n:
                    exp_low(n - 1)
            exp_low(QG + T - 1)
            act.wait_ge(root_ask, 1)
            nc.scalar.activation(degroot[:, :], deg[:, :], ACT.Sqrt).then_inc(root_ready, 1)
            empty_turn("kv", 0, kvT[:, :, :])
            empty_turn("agg", 0, xnT[:, :, 0:P])
            for t in range(T):
                if t + 1 < T:
                    empty_turn("agg", t + 1, xnT[:, :, (t + 1) * P:(t + 2) * P])
                if t >= 1:
                    if t >= 3:
                        act.wait_ge(logits_done, t - 2)
                    empty_turn("x2", t - 1, x2T[:, (t - 1) % 2, :, :])
                act.wait_ge(var2_ready, t + 1)
                nc.scalar.activation(std[:, t:t + 1], veps[:, t:t + 1], ACT.Sqrt).then_inc(std2_ready, 1)
            act.wait_ge(logits_done, T - 2)
            empty_turn("x2", T - 1, x2T[:, (T - 1) % 2, :, :])
            act.wait_ge(plan_ready, 1)
            blocks = act.value_load(plan[0:1, BLOCKS:BLOCKS + 1], min_val=MIN_BLOCKS, max_val=BLOCKS)
            with act.Fori(0, PAIRS) as q:
                for b in range(2):
                    with act.If(q * 2 + b < blocks):
                        act.wait_ge(xgT_done, q * 2 + (b + 1))
                        nc.scalar.activation(xgT[:, 0:2, :], ps[:, 0, 0:2 * BLK].rearrange("p (c n) -> p c n", c=2),
                                             ACT.Copy).then_inc(xgT_act, 1)
                        act.wait_ge(w_in[b], q * 16 + 16)
                        for m in range(HC):
                            act.wait_ge(h_done, q * (2 * HC) + (b * HC + m + 1))
                            nc.scalar.activation(hT[:, m, :], ps[:, PRB[m % 4], 0:BLK], ACT.Relu,
                                                 bias=b1[b][:, m:m + 1]).then_inc(h_ready, 1)

        @block.gpsimd
        def _(pool):
            steps = [0]

            def step(ins):
                steps[0] += 1
                ins.then_inc(pool_step, 1)
                pool.wait_ge(pool_step, steps[0])

            step(nc.gpsimd.memset(xres[96:P, T - 1, :], 0.0))
            pool.sem_inc(x_pad_set, 1)
            nc.gpsimd.iota(col_i[:, :], [[1, P]], base=0, channel_multiplier=0)
            nc.gpsimd.iota(chunk_i[:, :], [[1, EC]], base=0, channel_multiplier=0)
            nc.gpsimd.iota(token_i[:, :], [[P, T]], base=0, channel_multiplier=1)
            nc.gpsimd.iota(falling_i[:, :], [[-1, NE]], base=NE, channel_multiplier=0)
            nc.gpsimd.iota(blk_i[:, :], [[1, BLOCKS]], base=0, channel_multiplier=0)
            nc.gpsimd.memset(empty[:, :], N)
            nc.gpsimd.memset(ident[:, :], 0.0)
            nc.gpsimd.memset(before[:, :], 1.0)
            nc.gpsimd.memset(ones[:, :], 1.0)
            nc.gpsimd.memset(zrow[:, :], 0.0)
            nc.gpsimd.memset(same_head[:, :], 0.0)
            step(nc.gpsimd.memset(zero_t[:, :], 0.0))
            step(nc.gpsimd.memset(same_head[0:HEAD, 0:HEAD], 1.0))
            step(nc.gpsimd.memset(same_head[HEAD:P, HEAD:P], 1.0))
            nc.gpsimd.affine_select(out=ident[:, :], in_=ident[:, :], compare_op=ALU.not_equal, fill=1.0,
                                    base=0, pattern=[[-1, P]], channel_multiplier=1)
            step(nc.gpsimd.affine_select(out=before[:, :], in_=before[:, :], compare_op=ALU.is_gt, fill=0.0,
                                         base=0, pattern=[[1, P]], channel_multiplier=-1))
            pool.sem_inc(const_set, 1)
            pool.dma_start(slot_tokens[:, :].rearrange("(p s) a -> p (s a)", p=P), empty[:, :]).then_inc(empty_out, 16)
            pool.wait_ge(walk_ready, 1)
            for s in range(G):
                pool.wait_ge(scaled_out[s], 16 * len(range(s, T, G)))
            with pool.Fori(0, T) as t:
                first = pool.value_load(walk[0:1, bass.ds(t, 1)], min_val=0, max_val=EC)
                g0 = pool.value_load(walk[0:1, bass.ds(t + T, 1)], min_val=0, max_val=T * EC // G)
                g1 = pool.value_load(walk[0:1, bass.ds(t + (T + 1), 1)], min_val=1, max_val=T * EC // G)
                with pool.Fori(g0, g1) as g:
                    c = nc.s_assert_within((g - g0) * G + first, 0, EC - G, skip_runtime_bounds_check_because="DEG makes the ranges end before EC")
                    for j in range(G):
                        pool.wait_ge(summed[j], g + 1)
                        pool.sem_inc(pool_passed, 1)
                        nc.gpsimd.tensor_copy(src_now[:, j:j + 1], src_sb[:, bass.ds(c + j, 1)]).then_inc(it_pool, 1)
                        pool.wait_ge(it_pool, g * G + (j + 1))
                        pool.sem_inc(pool_passed, 1)
                        nc.gpsimd.indirect_dma_start(
                            out=ring[:, j, :], out_offset=None, in_=scaled_rows[:, :],
                            in_offset=bass.IndirectOffsetOnAxis(ap=src_now[:, j:j + 1].bitcast(U32), axis=0),
                        ).then_inc(gathered[j], 16)
            pool.wait_ge(plan_ready, 1)
            pool.wait_ge(empty_out, 16)
            for t in range(T):
                r = P if t < T - 1 else LAST
                nc.gpsimd.indirect_dma_start(
                    out=slot_tokens[:, :], out_offset=bass.IndirectOffsetOnAxis(ap=slot_i[0:r, t:t + 1].bitcast(U32), axis=0),
                    in_=token_i[0:r, t:t + 1], in_offset=None).then_inc(ids_out, 16)
            pool.wait_ge(ids_out, 16 * T)
            pool.dma_start(slots_a[:, 0:BLOCKS], slot_tokens[0:P * BLOCKS, :].rearrange("(s b) a -> s (b a)", s=P)).then_inc(slots_in, 16)
            pool.dma_start(slots_b[:, 0:BLOCKS], slot_tokens[P * BLOCKS:BLK * BLOCKS, :].rearrange("(s b) a -> s (b a)", s=B2ND)).then_inc(slots_in, 16)
            pool.wait_ge(slots_in, 32)
            for b in range(2):
                pool.wait_ge(rows2_out[b], 16 * len(range(b, T, 2)))
            blocks = pool.value_load(plan[0:1, BLOCKS:BLOCKS + 1], min_val=MIN_BLOCKS, max_val=BLOCKS)

            def fetch(i, b, n):
                nc.gpsimd.tensor_copy(now_a[:, b:b + 1], slots_a[:, bass.ds(i, 1)]).then_inc(now_set, 1)
                nc.gpsimd.tensor_copy(now_b[:, b:b + 1], slots_b[:, bass.ds(i, 1)]).then_inc(now_set, 1)
                pool.wait_ge(now_set, n * 2 + 2)
                pool.sem_inc(pool_passed, 1)
                for s, now in enumerate((now_a, now_b)):
                    nc.gpsimd.indirect_dma_start(
                        out=xg[0:now.shape[0], b, s, :], out_offset=None, in_=token_rows[:, :],
                        in_offset=bass.IndirectOffsetOnAxis(ap=now[:, b:b + 1].bitcast(U32), axis=0),
                    ).then_inc(xg_in[b], 16)

            pool.wait_ge(mm_done, len(groups))
            fetch(0, 0, 0)
            fetch(1, 1, 1)
            with pool.Fori(0, PAIRS) as q:
                for b in range(2):
                    with pool.If(q * 2 + b < blocks):
                        pool.wait_ge(yo_ready, q * 4 + (2 * b + 3))
                        pool.sem_inc(pool_passed, 1)
                        for s, now in enumerate((now_a, now_b)):
                            nc.gpsimd.indirect_dma_start(
                                out=out, out_offset=bass.IndirectOffsetOnAxis(ap=now[:, b:b + 1].bitcast(U32), axis=0),
                                in_=yo[0:now.shape[0], b, s, :], in_offset=None,
                                bounds_check=N - 1, oob_is_err=False).then_inc(out_done[b], 16)
                        pool.wait_ge(out_done[b], q * 32 + 32)
                    with pool.If(q * 2 + (b + 2) < blocks):
                        fetch(q * 2 + (b + 2), b, q * 2 + (b + 2))

        @block.vector
        def _(dve):
            steps = [0]

            def step(ins):
                steps[0] += 1
                ins.then_inc(dve_step, 1)
                dve.wait_ge(dve_step, steps[0])

            v = nc.vector
            dve.wait_ge(edges_in, 48)
            v.tensor_scalar(dst_hi[:, :], dst_sb[:, :], 7, None, ALU.arith_shift_right)
            v.tensor_scalar(dst_lo[:, :], dst_sb[:, :], P - 1, None, ALU.bitwise_and)
            step(v.tensor_copy(edge[:, 0, :], dst_sb[:, :]))
            v.tensor_copy(dst_hif[:, :], dst_hi[:, :])
            dve.wait_ge(const_set, 1)
            v.tensor_copy(col_f[:, :], col_i[:, :])
            v.tensor_copy(col_t[:, :], col_i[:, :])
            v.tensor_copy(chunk_f[:, :], chunk_i[:, :])
            v.tensor_copy(token_f[:, :], token_i[:, :])
            v.tensor_copy(falling[:, :], falling_i[:, :])
            v.tensor_copy(blk_f[:, :], blk_i[:, :])
            step(v.tensor_copy(dst_lof[:, :], dst_lo[:, :]))
            for t in range(T):
                ins = v.tensor_scalar(in_tile[:, t, :], dst_hif[:, :], float(t), None, ALU.is_equal)
            step(ins)
            v.tensor_tensor(deg_coef, in_tile.rearrange("p t c -> p c t"),
                            edge[:, 1, :][:, :, None].to_broadcast([P, EC, T]), ALU.mult).then_inc(coef_ready, 1)
            for t in range(T):
                dve.wait_ge(x_in[t], 16)
                step(v.bn_stats(stat[:, t % 2, :], xres[:, t, :]))
                step(v.bn_aggr(mv[:, t, :], stat[:, t % 2, :]))
            v.tensor_scalar(veps[:, :], mv[:, :, 1], EPS, None, ALU.add).then_inc(var_ready, 1)
            dve.wait_ge(std_ready, 1)
            step(v.reciprocal(rstd[:, :], std[:, :]))
            for t in range(T):
                v.tensor_scalar(xn[:, t, :], xres[:, t, :], mv[:, t, 0:1], rstd[:, t:t + 1], ALU.subtract,
                                ALU.mult).then_inc(xn_ready, 1)

            def out_of(kind, m, b=0):
                n = group_no[(kind, m, b)]
                dve.wait_ge(mm_done, n + 1)
                return n, ps[:, PRB[n % 4], :]

            dve.wait_ge(small_in, 16 * 6)
            def q_low(m, b):
                n = group_no[("q", m, b)]
                cols = NB[b][1]
                dve.wait_ge(q_free, n + 1)
                if n >= 2:
                    dve.wait_ge(exp_done, n - 1)
                v.tensor_scalar(low[:, n % 2, 0:cols], biased[:, n % 2, 0:cols], 0.0, None, ALU.min).then_inc(low_ready, 1)

            def q_sum(m, b):
                n = group_no[("q", m, b)]
                first, cols = NB[b]
                dve.wait_ge(exp_done, n + 1)
                v.scalar_tensor_tensor(out=qT[:, m, first:first + cols], in0=biased[:, n % 2, 0:cols], scalar=0.0,
                                       in1=expd[:, n % 2, 0:cols], op0=ALU.max, op1=ALU.add).then_inc(elu_done, 1)

            qs = [(m, b) for m in range(KC) for b in range(3)]
            for i, (m, b) in enumerate(qs):
                q_low(m, b)
                if i:
                    q_sum(*qs[i - 1])
            q_sum(*qs[-1])
            dve.wait_ge(seen_done, 1)
            per = T * EC // 4
            for n in range(4):
                ins = v.tensor_scalar(ring[0:1, :, :].rearrange("p j n -> p (j n)")[:, n * per:(n + 1) * per],
                                      ps[0:1, 4 + n, 0:per], 1.0, None, ALU.min)
            step(ins)
            dve.sem_inc(seen_done, 1)
            step(v.tensor_scalar(seen2[:, 0, :], chunk_f[:, :], 1.0, None, ALU.add))
            step(v.tensor_tensor(seen2[:, 1:T, :], seen[:, 1:T, :], seen2[:, 0:1, :].to_broadcast([1, T - 1, EC]), ALU.mult))
            step(v.tensor_tensor(seen2[:, 0, :], seen[:, 0, :], seen2[:, 0, :], ALU.mult))
            step(v.tensor_reduce(end_f[:, :], seen2[:, :, :], AX_X, ALU.max))
            step(v.tensor_scalar(seen2[:, 0, :], chunk_f[:, :], -1.0, float(EC), ALU.mult, ALU.add))
            step(v.tensor_tensor(seen2[:, 1:T, :], seen[:, 1:T, :], seen2[:, 0:1, :].to_broadcast([1, T - 1, EC]), ALU.mult))
            step(v.tensor_tensor(seen2[:, 0, :], seen[:, 0, :], seen2[:, 0, :], ALU.mult))
            step(v.tensor_reduce(seenk[:, :], seen2[:, :, :], AX_X, ALU.max))
            v.tensor_scalar(any_f[:, :], seenk[:, :], 0.0, None, ALU.is_gt)
            step(v.tensor_scalar(first_f[:, :], seenk[:, :], -1.0, float(EC), ALU.mult, ALU.add))
            step(v.tensor_tensor(first_f[:, :], first_f[:, :], any_f[:, :], ALU.mult))
            step(v.tensor_tensor(len_f[:, :], end_f[:, :], first_f[:, :], ALU.subtract))
            step(v.tensor_scalar(len_i[:, :], len_f[:, :], float(G - 1), float(G), ALU.add, ALU.max))
            step(v.tensor_scalar(len_i[:, :], len_i[:, :], G.bit_length() - 1, None, ALU.arith_shift_right))
            step(v.tensor_copy(len_f[:, :], len_i[:, :]))
            step(v.tensor_tensor_scan(end_f[:, :], len_f[:, :], zero_t[0:1, :], 0.0, ALU.add, ALU.add))
            v.tensor_copy(walk[:, 0:T], first_f[:, :])
            v.memset(walk[:, T:T + 1], 0)
            step(v.tensor_copy(walk[:, T + 1:2 * T + 1], end_f[:, :]))
            dve.sem_inc(walk_ready, 1)
            with dve.Fori(0, EC // (2 * DG)) as i:
                for b in range(2):
                    dve.wait_ge(hot8_used, i * 2 + 1)
                    v.tensor_tensor(
                        deg_hot[:, b, :, :], col_f[:, None, :].to_broadcast([P, DG, P]),
                        dst_lof[:, bass.ds(i * (2 * DG) + b * DG, DG)][:, :, None].to_broadcast([P, DG, P]),
                        ALU.is_equal).then_inc(hot8_ready, 1)
            dve.wait_ge(deg_done, 1)
            step(v.tensor_scalar(deg[:, :], ps[:, 7, 0:T], 1.0, None, ALU.add))
            step(v.tensor_scalar(degpos[:, :], deg[:, :], 0.0, None, ALU.is_gt))
            step(v.tensor_scalar(deg[:, :], deg[:, :], 1e-37, None, ALU.max))

            def k_low(t):
                n, bank = out_of("k", t)
                v.tensor_tensor(k_sb[:, t, :], bank, brow_sb[:, 0, :], ALU.add).then_inc(mm_free, 1)
                dve.wait_ge(mm_free, n + 1 - QG)
                if n >= 2:
                    dve.wait_ge(exp_done, n - 1)
                v.tensor_scalar(low[:, n % 2, :], k_sb[:, t, :], 0.0, None, ALU.min).then_inc(low_ready, 1)

            def k_sum(t):
                n = group_no[("k", t, 0)]
                dve.wait_ge(exp_done, n + 1)
                v.scalar_tensor_tensor(out=k_sb[:, t, :], in0=k_sb[:, t, :], scalar=0.0, in1=expd[:, n % 2, :],
                                       op0=ALU.max, op1=ALU.add).then_inc(elu_done, 1)

            for t in range(T):
                k_low(t)
                if t:
                    k_sum(t - 1)
            k_sum(T - 1)
            dve.sem_inc(root_ask, 1)
            step(v.memset(v_sb[:, :, :, P:VW], 1.0))
            for t in range(T):
                n, bank = out_of("v", t)
                v.tensor_tensor(v_sb[:, t, :, 0:P], bank.rearrange("p (c n) -> p c n", c=KC),
                                brow_sb[:, 1, :].rearrange("p (c n) -> p c n", c=KC), ALU.add).then_inc(mm_free, 1)
            dve.wait_ge(root_ready, 1)
            step(v.reciprocal(dinv[:, :], degroot[:, :]))
            step(v.tensor_tensor(dinv[:, :], dinv[:, :], degpos[:, :], ALU.mult))
            step(v.tensor_tensor(dinv2[:, :], dinv[:, :], dinv[:, :], ALU.mult))
            for t in range(T):
                if t >= G:
                    dve.wait_ge(scaled_out[t % G], 16 * (t // G))
                v.tensor_scalar(ring[:, t % G, :], xn[:, t, :], dinv[:, t:t + 1], None, ALU.mult).then_inc(scaled_ready, 1)
            dve.wait_ge(kv_done, 1)
            for j in range(KC):
                kv = ps[:, 6 + j // 2, (j % 2) * 256:(j % 2) * 256 + VW]
                v.tensor_tensor(kvm[:, j, :], kv[:, 0:P], same_head[:, :], ALU.mult)
                ins = v.tensor_scalar(ksm[:, j, :], same_head[:, :], kv[:, P:P + 1], None, ALU.mult)
            ins.then_inc(kv_masked, 1)
            for t in range(T):
                v.tensor_scalar(xn[:, t, :], xn[:, t, :], dinv2[:, t:t + 1], None, ALU.mult)
            dve.wait_ge(bo_in, 16)
            step(v.tensor_tensor(brow_sb[:, 2, :], brow_sb[:, 2, :], brow_sb[:, 0, :], ALU.add))
            for t in range(T):
                ins = v.tensor_tensor(xres[:, t, :], xres[:, t, :], brow_sb[:, 2, :], ALU.add)
            step(ins)
            for j in range(KC):
                n, bank = out_of("m", j)
                v.tensor_copy(m_sb[:, j, :], bank).then_inc(mm_free, 1)
            for j in range(KC):
                for b, (first, cols) in enumerate(NB):
                    n, bank = out_of("norm", j, b)
                    step(v.tensor_scalar(low[:, n % 2, 0:cols], bank[:, 0:cols], 1e-6, None, ALU.add))
                    step(v.reciprocal(low[:, n % 2, 0:cols], low[:, n % 2, 0:cols]))
                    v.tensor_tensor(qT[:, j, first:first + cols], qT[:, j, first:first + cols], low[:, n % 2, 0:cols],
                                    ALU.mult).then_inc(mm_free, 1)
            for j in range(G):
                dve.sem_inc(hot_ready[j], 1)
            dve.sem_inc(agg_ready, 1)
            with dve.Fori(0, T) as t:
                first = dve.value_load(walk[0:1, bass.ds(t, 1)], min_val=0, max_val=EC)
                g0 = dve.value_load(walk[0:1, bass.ds(t + T, 1)], min_val=0, max_val=T * EC // G)
                g1 = dve.value_load(walk[0:1, bass.ds(t + (T + 1), 1)], min_val=1, max_val=T * EC // G)
                with dve.Fori(g0, g1) as g:
                    c = nc.s_assert_within((g - g0) * G + first, 0, EC - G, skip_runtime_bounds_check_because="DEG makes the ranges end before EC")
                    dve.wait_ge(hot_ready[G - 1], g + 1)
                    v.tensor_copy(edge_now[:, :, :], edge[:, :, bass.ds(c, G)]).then_inc(it_dve, 1)
                    dve.wait_ge(it_dve, g * 1 + t + 1)
                    for j in range(G):
                        dve.wait_ge(summed[j], g + 1)
                        v.tensor_scalar(hot[:, j, :], col_t[:, :], edge_now[:, 0, j:j + 1], edge_now[:, 1, j:j + 1],
                                        ALU.is_equal, ALU.mult).then_inc(hot_ready[j], 1)
                dve.wait_ge(tile_summed, t + 1)
                v.scalar_tensor_tensor(out=xn[:, bass.ds(t, 1), :].rearrange("p a n -> p (a n)"), in0=ps[:, 6, :],
                                       scalar=dinv[:, bass.ds(t, 1)], in1=xn[:, bass.ds(t, 1), :].rearrange("p a n -> p (a n)"),
                                       op0=ALU.mult, op1=ALU.add).then_inc(agg_ready, 1)
                v.tensor_scalar(col_t[:, :], col_t[:, :], float(P), None, ALU.add).then_inc(it_dve, 1)
            for t in range(T):
                n, bank = out_of("out", t)
                if t >= 2:
                    dve.wait_ge(rows2_out[t % 2], 16 * (t // 2))
                ins = v.tensor_tensor(rows2[:, t % 2, 0:D], bank, xres[:, t, :], ALU.add)
                step(ins)
                dve.sem_inc(mm_free, 1)
                step(v.bn_stats(stat[:, t % 2, :], rows2[:, t % 2, 0:D]))
                step(v.bn_aggr(mv[:, t, :], stat[:, t % 2, :]))
                v.tensor_scalar(veps[:, t:t + 1], mv[:, t, 1:2], EPS, None, ALU.add).then_inc(var2_ready, 1)
                dve.wait_ge(std2_ready, t + 1)
                step(v.reciprocal(rstd[:, t:t + 1], std[:, t:t + 1]))
                if t >= 2:
                    dve.wait_ge(tr_done, turn_no[("x2", t - 2)] + 1)
                v.tensor_scalar(rows2[:, t % 2, D:2 * D], rows2[:, t % 2, 0:D], mv[:, t, 0:1], rstd[:, t:t + 1],
                                ALU.subtract, ALU.mult).then_inc(rows2_ready, 1)
            v.tensor_scalar(valid[:, :], token_f[:, :], float(N), None, ALU.is_lt)
            dve.wait_ge(logits_done, T)
            step(v.tensor_tensor(logit[:, :, :], ps[:, 6, 0:T * NE].rearrange("p (t e) -> p t e", t=T),
                                 gb_sb[:, None, :].to_broadcast([P, T, NE]), ALU.add))
            step(v.tensor_reduce(best[:, :], logit[:, :, :], AX_X, ALU.max))
            step(v.tensor_tensor(top[:, :, :], logit[:, :, :], best[:, :][:, :, None].to_broadcast([P, T, NE]), ALU.is_equal))
            step(v.tensor_tensor(top[:, :, :], top[:, :, :], falling[:, None, :].to_broadcast([P, T, NE]), ALU.mult))
            step(v.tensor_reduce(best[:, :], top[:, :, :], AX_X, ALU.max))
            step(v.tensor_tensor(choice[:, :, :], best[:, :][:, :, None].to_broadcast([P, T, NE]),
                                 falling[:, None, :].to_broadcast([P, T, NE]), ALU.is_equal))
            v.tensor_tensor(choice[:, :, :], choice[:, :, :], valid[:, :][:, :, None].to_broadcast([P, T, NE]), ALU.mult).then_inc(choice_ready, 1)
            dve.wait_ge(rank_done, 1)
            step(v.memset(count[:, :], 0.0))
            for t in range(T):
                v.tensor_tensor(rank[:, t, :], ps[:, 7, t * NE:(t + 1) * NE], count[:, :], ALU.add)
                step(v.tensor_tensor(count[:, :], ps[:, 7, 256 + t * NE:256 + (t + 1) * NE], count[:, :], ALU.add))
            step(v.memset(nblk[:, :], 0.0))
            for i in range(-(-N // BLK)):
                step(v.scalar_tensor_tensor(out=nblk[:, :], in0=count[:, :], scalar=float(i * BLK), in1=nblk[:, :],
                                            op0=ALU.is_gt, op1=ALU.add))
            step(v.tensor_tensor_scan(blk_end[:, :], nblk[:, :], zero_t[:, 0:NE], 0.0, ALU.add, ALU.add))
            step(v.tensor_tensor(blk_start[:, :], blk_end[:, :], nblk[:, :], ALU.subtract))
            step(v.tensor_tensor(pick[:, :, :], choice[:, :, :], rank[:, :, :], ALU.mult))
            step(v.tensor_reduce(rank_t[:, :], pick[:, :, :], AX_X, ALU.add))
            step(v.tensor_tensor(pick[:, :, :], choice[:, :, :], blk_start[:, None, :].to_broadcast([P, T, NE]), ALU.mult))
            step(v.tensor_reduce(start_t[:, :], pick[:, :, :], AX_X, ALU.add))
            step(v.memset(over_t[:, :], 0.0))
            for i in range(1, -(-N // BLK)):
                step(v.scalar_tensor_tensor(out=over_t[:, :], in0=rank_t[:, :], scalar=float(i * BLK), in1=over_t[:, :],
                                            op0=ALU.is_ge, op1=ALU.add))
            step(v.tensor_tensor(start_t[:, :], start_t[:, :], over_t[:, :], ALU.add))
            step(v.scalar_tensor_tensor(out=slot_f[:, :], in0=over_t[:, :], scalar=float(-BLK), in1=rank_t[:, :],
                                        op0=ALU.mult, op1=ALU.add))
            step(v.scalar_tensor_tensor(out=slot_f[:, :], in0=slot_f[:, :], scalar=float(BLOCKS), in1=start_t[:, :],
                                        op0=ALU.mult, op1=ALU.add))
            step(v.tensor_copy(slot_i[:, :], slot_f[:, :]))
            step(v.memset(blk_e[:, :], 0.0))
            for e in range(NE - 1):
                step(v.scalar_tensor_tensor(out=blk_e[:, :], in0=blk_f[:, :], scalar=blk_end[:, e:e + 1], in1=blk_e[:, :],
                                            op0=ALU.is_ge, op1=ALU.add))
            v.tensor_copy(plan[:, 0:BLOCKS], blk_e[0:1, :])
            step(v.tensor_copy(plan[:, BLOCKS:BLOCKS + 1], blk_end[0:1, NE - 1:NE]))
            dve.sem_inc(plan_ready, 1)
            dve.sem_inc(yo_ready, 1)
            blocks = dve.value_load(plan[0:1, BLOCKS:BLOCKS + 1], min_val=MIN_BLOCKS, max_val=BLOCKS)
            with dve.Fori(0, PAIRS) as q:
                for b in range(2):
                    with dve.If(q * 2 + b < blocks):
                        dve.wait_ge(xgT_done, q * 2 + (b + 1))
                        v.tensor_copy(xgT[:, 2:4, :], ps[:, 1, 0:2 * BLK].rearrange("p (c n) -> p c n", c=2)).then_inc(xgT_dve, 1)
                        dve.wait_ge(w_in[b], q * 16 + 16)
                        for j in range(KC):
                            dve.wait_ge(y_done, q * (2 * KC) + (b * KC + j + 1))
                            v.tensor_scalar(yT[:, j, :], ps[:, 6 + j % 2, 0:BLK], b2[b][:, j:j + 1], None, ALU.add).then_inc(y_ready, 1)
                        dve.wait_ge(yr_done, q * 2 + (b + 1))
                        dve.wait_ge(xg_in[b], q * 32 + 32)
                        v.tensor_tensor(yo[:, b, 0, :], ps[:, 0, :], xg[:, b, 0, 0:D], ALU.add).then_inc(yo_ready, 1)
                        v.tensor_tensor(yo[0:B2ND, b, 1, :], ps[0:B2ND, 1, :], xg[0:B2ND, b, 1, 0:D], ALU.add).then_inc(yo_ready, 1)

        @block.tensor
        def _(pe):
            mm = nc.tensor.matmul

            def turn(kind, t, block_of):
                n = turn_no[(kind, t)]
                if n >= 2:
                    pe.wait_ge(tr_free, n - 1)
                for c in range(KC):
                    ins = nc.tensor.transpose(ps[:, TRB[n % 2], c * P:(c + 1) * P], block_of(c), ident[:, :])
                ins.then_inc(tr_done, 1)

            def group(kind, m, b, cols, parts):
                n = group_no[(kind, m, b)]
                if n >= 4 and n - 4 < QG:
                    pe.wait_ge(q_free, n - 3)
                elif n >= 4:
                    pe.wait_ge(mm_free, n - 3 - QG)
                for i, (left, right) in enumerate(parts):
                    ins = mm(ps[:, PRB[n % 4], 0:cols], left, right, start=(i == 0), stop=(i == len(parts) - 1))
                ins.then_inc(mm_done, 1)

            pe.wait_ge(const_set, 1)
            for t in range(T):
                pe.wait_ge(xn_ready, t + 1)
                turn("xn", t, lambda c: xn[:, t, c * P:(c + 1) * P])
            pe.wait_ge(wq_in, 16)
            pe.wait_ge(tr_free, T)
            for m in range(KC):
                for b, (first, cols) in enumerate(NB):
                    group("q", m, b, cols, [(wq_sb[:, c, m * P:(m + 1) * P], xnT[:, c, first:first + cols]) for c in range(KC)])
            pe.wait_ge(coef_ready, 1)
            pe.wait_ge(q_free, QG)
            per = T * EC // 4
            for n in range(4):
                ins = mm(ps[0:1, 4 + n, 0:per], ones[:, 0:1], late[:, n * per:(n + 1) * per], start=True, stop=True)
            ins.then_inc(seen_done, 1)
            pe.wait_ge(seen_done, 2)
            mm(ps[:, 7, 0:T], zrow[:, 0:P], zrow[:, 0:T], start=True, stop=False)
            pe.sem_inc(hot8_used, 1)
            with pe.Fori(0, EC // (2 * DG)) as i:
                for b in range(2):
                    pe.wait_ge(hot8_ready, i * 2 + (b + 1))
                    for c in range(DG):
                        ins = mm(ps[:, 7, 0:T], deg_hot[:, b, c, :],
                                 deg_coef[:, bass.ds(i * (2 * DG) + (b * DG + c), 1), :].rearrange("p a t -> p (a t)"),
                                 start=False, stop=False)
                    ins.then_inc(hot8_used, 1)
            mm(ps[:, 7, 0:T], zrow[:, 0:P], zrow[:, 0:T], start=False, stop=True).then_inc(deg_done, 1)
            pe.wait_ge(deg_done, 1)
            pe.sem_inc(late_free, 1)
            pe.wait_ge(wk_in, 16)
            for t in range(T):
                group("k", t, 0, D, [(xnT[:, c, t * P:(t + 1) * P], wk_sb[:, c, :]) for c in range(KC)])
            pe.wait_ge(wv_in, 16)
            for t in range(T):
                group("v", t, 0, D, [(xnT[:, c, t * P:(t + 1) * P], wv_sb[:, c, :]) for c in range(KC)])
            pe.wait_ge(elu_done, QG + T)
            pe.wait_ge(mm_free, 2 * T)
            pe.wait_ge(root_ready, 1)
            for j in range(KC):
                for t in range(T):
                    r = P if t < T - 1 else LAST
                    ins = mm(ps[:, 6 + j // 2, (j % 2) * 256:(j % 2) * 256 + VW], k_sb[0:r, t, j * P:(j + 1) * P],
                             v_sb[0:r, t, j, :], start=(t == 0), stop=(t == T - 1))
            ins.then_inc(kv_done, 1)
            pe.wait_ge(kv_masked, 1)
            turn("kv", 0, lambda c: kvm[:, c, :])
            pe.wait_ge(wwo_in, 32)
            pe.wait_ge(tr_free, turn_no[("kv", 0)] + 1)
            pe.wait_ge(elu_done, QG + T)
            for j in range(KC):
                group("m", j, 0, D, [(kvT[:, j, :], wo_sb[:, j, :])])
            for j in range(KC):
                for b, (first, cols) in enumerate(NB):
                    group("norm", j, b, cols, [(ksm[:, j, :], qT[:, j, first:first + cols])])
            for j in range(G):
                pe.sem_inc(summed[j], 1)
            with pe.Fori(0, T) as t:
                g0 = pe.value_load(walk[0:1, bass.ds(t + T, 1)], min_val=0, max_val=T * EC // G)
                g1 = pe.value_load(walk[0:1, bass.ds(t + (T + 1), 1)], min_val=1, max_val=T * EC // G)
                pe.wait_ge(agg_ready, t + 1)
                mm(ps[:, 6, :], zrow[:, 0:P], zrow[:, :], start=True, stop=False)
                with pe.Fori(g0, g1) as g:
                    for j in range(G):
                        pe.wait_ge(gathered[j], g * 16 + 16)
                        pe.wait_ge(hot_ready[j], g + 2)
                        mm(ps[:, 6, :], hot[:, j, :], ring[:, j, :], start=False, stop=False).then_inc(summed[j], 1)
                mm(ps[:, 6, :], zrow[:, 0:P], zrow[:, :], start=False, stop=True).then_inc(tile_summed, 1)
            def agg_turn(t):
                pe.wait_ge(agg_ready, t + 2)
                turn("agg", t, lambda c: xn[:, t, c * P:(c + 1) * P])

            def x2_turn(t):
                pe.wait_ge(rows2_ready, t + 1)
                turn("x2", t, lambda c: rows2[:, t % 2, D + c * P:D + (c + 1) * P])

            def gate(t):
                pe.wait_ge(tr_free, turn_no[("x2", t)] + 1)
                for c in range(KC):
                    ins = mm(ps[:, 6, t * NE:(t + 1) * NE], x2T[:, t % 2, c, :], gw_sb[:, c, :], start=(c == 0), stop=(c == KC - 1))
                ins.then_inc(logits_done, 1)

            agg_turn(0)
            for t in range(T):
                if t + 1 < T:
                    agg_turn(t + 1)
                pe.wait_ge(tr_free, turn_no[("agg", t)] + 1)
                group("out", t, 0, D, [(xnT[:, c, t * P:(t + 1) * P], w_sb[:, c, :]) for c in range(KC)]
                      + [(qT[:, c, t * P:(t + 1) * P], m_sb[:, c, :]) for c in range(KC)])
                if t >= 1:
                    x2_turn(t - 1)
                    gate(t - 1)
            x2_turn(T - 1)
            gate(T - 1)
            pe.wait_ge(choice_ready, 1)
            every = choice[:, :, :].rearrange("p t e -> p (t e)")
            mm(ps[:, 7, 0:T * NE], before[:, :], every, start=True, stop=True)
            mm(ps[:, 7, 256:256 + T * NE], ones[:, :], every, start=True, stop=True).then_inc(rank_done, 1)
            pe.wait_ge(plan_ready, 1)
            blocks = pe.value_load(plan[0:1, BLOCKS:BLOCKS + 1], min_val=MIN_BLOCKS, max_val=BLOCKS)
            with pe.Fori(0, PAIRS) as q:
                for b in range(2):
                    with pe.If(q * 2 + b < blocks):
                        pe.wait_ge(xg_in[b], q * 32 + 32)
                        pe.wait_ge(yo_ready, q * 4 + 2 * b + 1)
                        for c in range(KC):
                            at = (c % 2) * BLK
                            nc.tensor.transpose(ps[:, c // 2, at:at + P], xg[:, b, 0, D + c * P:D + (c + 1) * P], ident[:, :])
                            ins = nc.tensor.transpose(ps[:, c // 2, at + P:at + BLK],
                                                      xg[0:B2ND, b, 1, D + c * P:D + (c + 1) * P], ident[0:B2ND, 0:B2ND])
                        ins.then_inc(xgT_done, 1)
                        pe.wait_ge(w_in[b], q * 16 + 16)
                        pe.wait_ge(xgT_act, q * 2 + (b + 1))
                        pe.wait_ge(xgT_dve, q * 2 + (b + 1))
                        for m in range(HC):
                            if m >= 4:
                                pe.wait_ge(h_ready, q * (2 * HC) + (b * HC + m - 3))
                            for c in range(KC):
                                ins = mm(ps[:, PRB[m % 4], 0:BLK], w1[b][:, c, m * P:(m + 1) * P], xgT[:, c, :],
                                         start=(c == 0), stop=(c == KC - 1))
                            ins.then_inc(h_done, 1)
                        for j in range(KC):
                            if j >= 2:
                                pe.wait_ge(y_ready, q * (2 * KC) + (b * KC + j - 1))
                            for m in range(HC):
                                if j == 0:
                                    pe.wait_ge(h_ready, q * (2 * HC) + (b * HC + m + 1))
                                ins = mm(ps[:, 6 + j % 2, 0:BLK], w2[b][:, m, j * P:(j + 1) * P], hT[:, m, :],
                                         start=(m == 0), stop=(m == HC - 1))
                            ins.then_inc(y_done, 1)
                        for j in range(KC):
                            pe.wait_ge(y_ready, q * (2 * KC) + (b * KC + j + 1))
                            nc.tensor.transpose(ps[:, 0, j * P:(j + 1) * P], yT[:, j, 0:P], ident[:, :])
                            ins = nc.tensor.transpose(ps[0:B2ND, 1, j * P:(j + 1) * P], yT[:, j, P:BLK], ident[:, :])
                        ins.then_inc(yr_done, 1)


def kernel(**inputs):
    import numpy as np
    import concourse.bacc as bacc
    from concourse.bass_utils import run_bass_kernel_spmd

    a = {k: np.asarray(v) for k, v in inputs.items()}

    def chunks(e):
        return np.ascontiguousarray(e.reshape(EC, P).T)

    def rows(w):
        return np.ascontiguousarray(w.reshape(-1, P, w.shape[-1]).transpose(1, 0, 2))

    pad = EC * P - E
    experts = np.concatenate([
        a["L0_ffn_W1"].reshape(NE, KC, P, H).transpose(0, 2, 1, 3).reshape(NE, P, KC * H),
        a["L0_ffn_W2"].reshape(NE, HC, P, D).transpose(0, 2, 1, 3).reshape(NE, P, HC * D),
        a["L0_ffn_b1"].reshape(NE, HC, P).transpose(0, 2, 1),
        a["L0_ffn_b2"].reshape(NE, KC, P).transpose(0, 2, 1)], axis=2)
    arrays = {
        "x": a["x"],
        "src": chunks(np.concatenate([a["src"], np.zeros(pad, a["src"].dtype)])),
        "dst": chunks(np.concatenate([a["dst"], np.full(pad, -1, a["dst"].dtype)])),
        "ew": chunks(np.concatenate([a["edge_weight"], np.zeros(pad, a["edge_weight"].dtype)])),
        "wq": rows(a["L0_mix_Wq"].T), "wk": rows(a["L0_mix_Wk"].T), "wv": rows(a["L0_mix_Wv"].T), "wo": rows(a["L0_mix_Wo"].T),
        "wg_nn": rows(a["L0_gnn_W"]),
        "bq": np.ascontiguousarray(a["L0_mix_bq"].reshape(KC, P).T),
        "brow": np.stack([a["L0_mix_bk"], a["L0_mix_bv"], a["L0_gnn_b"], a["L0_mix_bo"]]),
        "gate_w": rows(a["L0_ffn_Wg"]),
        "gate_b": a["L0_ffn_bg"].reshape(1, NE),
        "experts": np.ascontiguousarray(experts),
    }
    nc = bacc.Bacc("TRN2", target_bir_lowering=False, num_devices=1)
    args = {k: nc.dram_tensor(f"in_{k}", v.shape, mybir.dt.from_np(v.dtype), kind="ExternalInput").ap() for k, v in arrays.items()}
    out = nc.dram_tensor("out_x", (N, D), F32, kind="ExternalOutput").ap()
    transformer_layer(nc, **args, out=out)
    r = run_bass_kernel_spmd(nc, [{f"in_{k}": v for k, v in arrays.items()}], core_ids=[0])
    return r.results[0]["out_x"]
```

```python
from contextlib import ExitStack

import concourse.bass as bass
from concourse import mybir

F32 = mybir.dt.float32
BF16 = mybir.dt.bfloat16
I32 = mybir.dt.int32
U32 = mybir.dt.uint32
ALU = mybir.AluOpType
ACT = mybir.ActivationFunctionType
AX_X = mybir.AxisListType.X

P = 128
N = 1250
D = 512
HEAD = 64
E = 20000
NE = 8
H = 2 * D
T = -(-N // P)
LAST = N - (T - 1) * P
KC = D // P
HC = H // P
NP = T * P
EC = 160
G = 2
W = 64
EG = -(-E // (G * P))
SLOTS = 8
DG = 16
BLK = 176
B2ND = BLK - P
BLOCKS = (N + NE * (BLK - 1)) // BLK // 2 * 2 + 2
PAIRS = BLOCKS // 2
MIN_BLOCKS = -(-N // BLK)
WROW = KC * H + HC * D + HC + KC
EPS = 1e-5
WP = 4
MORE = NP // W
QG = KC * 3
VW = P + 2
assert EC * P >= E and EC % DG == 0 and EC >= EG * G and BLK * BLOCKS % P == 0


def n_blocks():
    return [(0, 512), (512, 512), (1024, NP - 1024)]


def transformer_layer(nc, x, src, dst, ew, wq, wk, wv, wo, wg_nn, bq, brow, gate_w, gate_b, experts, out):
    scaled_rows = nc.dram_tensor("scaled_rows", [NP, D], F32)
    token_rows = nc.dram_tensor("token_rows", [NP, 2 * D], F32)
    slot_tokens = nc.dram_tensor("slot_tokens", [BLK * BLOCKS, 1], I32)

    with ExitStack() as ctx:
        def sb(name, shape, dt=F32):
            return ctx.enter_context(nc.sbuf_tensor(name, shape, dt))

        def sem(name):
            return ctx.enter_context(nc.semaphore(name))

        xn = sb("xn", [P, T, D])
        k_sb = xn
        xT_ = sb("xT_", [P, KC * NP])
        xnT = xT_[:, :].rearrange("p (c n) -> p c n", c=KC)
        qT_ = sb("qT_", [P, KC * NP])
        qT = qT_[:, :].rearrange("p (c n) -> p c n", c=KC)
        sumT = sb("sumT", [P, KC, NP + W])
        ffw = sb("ffw", [P, 2, WROW])
        early = ffw[:, :, :].rearrange("p a n -> p (a n)")
        taken = [0]

        def part(n, rows=P):
            taken[0] += n
            assert taken[0] <= 2 * WROW
            return early[0:rows, taken[0] - n:taken[0]]

        ring = part(SLOTS * D).rearrange("p (s n) -> p s n", s=SLOTS)
        wq_sb, wk_sb, wv_sb = (part(KC * D).rearrange("p (c n) -> p c n", c=KC) for _ in range(3))
        v_sb = part(T * KC * VW).rearrange("p (t c n) -> p t c n", t=T, c=KC)
        dst_sb, dst_hi, dst_lo = (part(EC).bitcast(I32) for _ in range(3))
        dst_lof = part(EC)
        late = sb("late", [P, 3 * KC * D])
        w_sb = late[:, 0:KC * D].rearrange("p (c n) -> p c n", c=KC)
        wo_sb = late[:, KC * D:2 * KC * D].rearrange("p (c n) -> p c n", c=KC)
        m_sb = late[:, 2 * KC * D:3 * KC * D].rearrange("p (c n) -> p c n", c=KC)
        late16 = late[:, :].bitcast(BF16)
        in_tile = late16[:, 0:T * EC].rearrange("p (t c) -> p t c", t=T)
        deg_coef = late16[:, T * EC:4 * T * EC].rearrange("p (c w t) -> p c w t", w=3, t=T)
        deg_hot = late16[:, 4 * T * EC:4 * T * EC + 2 * DG * P].rearrange("p (b c n) -> p b c n", b=2, c=DG)
        assert 4 * T * EC + 2 * DG * P <= 6 * KC * D

        hot = sb("hot", [P, SLOTS, W])
        src_sb = sb("src_sb", [P, EC], I32)
        dst_f = sb("dst_f", [P, EC])
        ew_sb = sb("ew_sb", [P, EC])
        rel = sb("rel", [P, EC])
        src_now = sb("src_now", [P, G], I32)
        edge_now = sb("edge_now", [P, 2, G])
        col_i = sb("col_i", [P, P], I32)
        col_f = sb("col_f", [P, P])
        col_h = sb("col_h", [P, P], BF16)
        token_i = sb("token_i", [P, T], I32)
        token_f = sb("token_f", [P, T])
        valid = sb("valid", [P, T])
        falling_i = sb("falling_i", [P, NE], I32)
        falling = sb("falling", [P, NE])
        blk_i = sb("blk_i", [P, BLOCKS], I32)
        blk_f = sb("blk_f", [P, BLOCKS])
        ident = sb("ident", [P, P])
        ends = sb("ends", [P, 2, 2])
        before = sb("before", [P, P])
        ones = sb("ones", [P, P])
        same_head = sb("same_head", [P, P])
        zrow = sb("zrow", [1, P], BF16)
        bq_sb = sb("bq_sb", [P, KC])
        brow_sb = sb("brow_sb", [P, 3, D])
        gw_sb = sb("gw_sb", [P, KC, NE])
        gb_sb = sb("gb_sb", [P, NE])
        stat = sb("stat", [P, T, 6])
        mv = sb("mv", [P, T, 2])
        veps = sb("veps", [P, T])
        std = sb("std", [P, T])
        rstd = sb("rstd", [P, T])
        deg = sb("deg", [P, T])
        deg3 = sb("deg3", [P, T])
        degpos = sb("degpos", [P, T])
        degroot = sb("degroot", [P, T])
        dinv = sb("dinv", [P, T])
        dinv2 = sb("dinv2", [P, T])
        group_lo = sb("group_lo", [P, EG])
        group_hi = sb("group_hi", [P, EG])
        more_i = sb("more_i", [P, EG], I32)
        more = sb("more", [P, EG])
        after = sb("after", [P, EG])
        zero_g = sb("zero_g", [P, EG])
        window = sb("window", [1, EG], I32)
        rest = sb("rest", [1, EG + 1], I32)
        rest_end = sb("rest_end", [1, 1], I32)
        halves = sb("halves", [P, 6 * D])
        biased, low, expd = (halves[:, n * 2 * D:(n + 1) * 2 * D].rearrange("p (b n) -> p b n", b=2) for n in range(3))
        rows2 = halves[:, 0:4 * D].rearrange("p (b n) -> p b n", b=2)
        x2T = halves[:, 4 * D:6 * D].rearrange("p (b c n) -> p b c n", b=2, c=KC)
        kvm, ksm = (halves[:, n * D:(n + 1) * D].rearrange("p (c n) -> p c n", c=KC) for n in range(2))
        ends_all = expd[:, 1, :].rearrange("p (a n) -> p a n", a=4)
        ew_left = expd[:, 0, 0:2 * EC].rearrange("p (a n) -> p a n", a=2)
        ew_h = biased[:, 1, 0:3 * EC // 2].bitcast(BF16).rearrange("p (a n) -> p a n", a=3)
        hi_h = biased[:, 1, 3 * EC // 2:2 * EC].bitcast(BF16)
        kvT = xT_[:, 0:D].rearrange("p (c n) -> p c n", c=KC)
        xr = xT_[:, D:3 * D].rearrange("p (b n) -> p b n", b=2)
        logit = sb("logit", [P, T, NE])
        best = sb("best", [P, T])
        top = sb("top", [P, T, NE])
        choice = sb("choice", [P, T, NE])
        rank = sb("rank", [P, T, NE])
        count = sb("count", [P, NE])
        countT = sb("countT", [P, NE])
        nblk = sb("nblk", [P, NE])
        blk_end = sb("blk_end", [P, NE])
        blk_start = sb("blk_start", [P, NE])
        pick = sb("pick", [P, T, NE])
        rank_t = sb("rank_t", [P, T])
        start_t = sb("start_t", [P, T])
        over_t = sb("over_t", [P, T])
        slot_f = sb("slot_f", [P, T])
        slot_i = sb("slot_i", [P, T], I32)
        blk_e = sb("blk_e", [P, BLOCKS])
        plan = sb("plan", [1, BLOCKS + 1], I32)
        empty = sb("empty", [P, BLK * BLOCKS // P], I32)
        slots_a = sb("slots_a", [P, BLOCKS + 2], I32)
        slots_b = sb("slots_b", [B2ND, BLOCKS + 2], I32)
        now_a = sb("now_a", [P, 2], I32)
        now_b = sb("now_b", [B2ND, 2], I32)
        xg = xT_[:, 0:2 * 2 * 2 * D].rearrange("p (b s n) -> p b s n", b=2, s=2)
        xgT = qT_[:, 0:KC * BLK].rearrange("p (c n) -> p c n", c=KC)
        hT = qT_[:, KC * BLK:(KC + HC) * BLK].rearrange("p (c n) -> p c n", c=HC)
        yT = qT_[:, (KC + HC) * BLK:(2 * KC + HC) * BLK].rearrange("p (c n) -> p c n", c=KC)
        yo = sumT[:, :, 0:D].rearrange("p (b s) n -> p b s n", b=2)
        w1 = [ffw[:, b, 0:KC * H].rearrange("p (c n) -> p c n", c=KC) for b in range(2)]
        w2 = [ffw[:, b, KC * H:KC * H + HC * D].rearrange("p (c n) -> p c n", c=HC) for b in range(2)]
        b1 = [ffw[:, b, KC * H + HC * D:KC * H + HC * D + HC] for b in range(2)]
        b2 = [ffw[:, b, KC * H + HC * D + HC:WROW] for b in range(2)]

        ps = ctx.enter_context(nc.psum_tensor("ps", [P, 8, 512], F32))
        TRB, PRB = (0, 1), (2, 3, 4, 5)

        x_in = [sem(f"x_in{t}") for t in range(T)]
        xr_in = [sem(f"xr_in{b}") for b in range(2)]
        edges_in, src_in, stats_ready, wq_in, wk_in, wv_in, wwo_in, small_in, bo_in = (sem(s) for s in
            ("edges_in", "src_in", "stats_ready", "wq_in", "wk_in", "wv_in", "wwo_in", "small_in", "bo_in"))
        pool_passed = sem("pool_passed")
        const_set, x_pad_set = sem("const_set"), sem("x_pad_set")
        dve_step, pool_step = sem("dve_step"), sem("pool_step")
        var_ready, std_ready, xn_ready = sem("var_ready"), sem("std_ready"), sem("xn_ready")
        tr_done, tr_free = sem("tr_done"), sem("tr_free")
        mm_done, bank_free = sem("mm_done"), [sem(f"bank_free{b}") for b in range(len((2, 3, 4, 5)))]
        biased_ready, elu_done, deg_done = sem("biased_ready"), sem("elu_done"), sem("deg_done")
        low_ready, exp_done = sem("low_ready"), sem("exp_done")
        dst_ready, dst_turned, ends_ready, ends_done = (sem(s) for s in ("dst_ready", "dst_turned", "ends_ready", "ends_done"))
        coef_ready, deg_hot_ready, deg_hot_used = (sem(s) for s in ("coef_ready", "deg_hot_ready", "deg_hot_used"))
        root_ask, root_ready = sem("root_ask"), sem("root_ready")
        scaled_ready, scaled_out = sem("scaled_ready"), sem("scaled_out")
        windows_ready, rel_ready = sem("windows_ready"), sem("rel_ready")
        kv_masked, m_ready, qn_ready = sem("kv_masked"), sem("m_ready"), sem("qn_ready")
        gathered = [sem(f"gathered{s}") for s in range(SLOTS)]
        hot_ready, sum_done, sum_added = sem("hot_ready"), sem("sum_done"), sem("sum_added")
        rest_set, rest_in, rest_now, rest_hot, rest_done, rest_added = (sem(s) for s in
            ("rest_set", "rest_in", "rest_now", "rest_hot", "rest_done", "rest_added"))
        xr_ready, xr_used = sem("xr_ready"), sem("xr_used")
        var2_ready, std2_ready, rows2_ready = (sem(s) for s in ("var2_ready", "std2_ready", "rows2_ready"))
        rows2_out = [sem(f"rows2_out{b}") for b in range(2)]
        logits_done, choice_ready, rank_done, plan_ready = (sem(s) for s in
            ("logits_done", "choice_ready", "rank_done", "plan_ready"))
        empty_out, ids_out, slots_in, now_set = (sem(s) for s in ("empty_out", "ids_out", "slots_in", "now_set"))
        w_in = [sem(f"w_in{b}") for b in range(2)]
        xg_in = [sem(f"xg_in{b}") for b in range(2)]
        out_done = [sem(f"out_done{b}") for b in range(2)]
        xgT_done, xgT_act, xgT_dve, h_done, h_ready, y_done, y_ready, yr_done, yo_ready = (sem(s) for s in
            ("xgT_done", "xgT_act", "xgT_dve", "h_done", "h_ready", "y_done", "y_ready", "yr_done", "yo_ready"))

        NB = n_blocks()
        dense = ([("q", m, b) for m in range(KC) for b in range(3)]
                 + [("k", t, 0) for t in range(T)] + [("v", t, 0) for t in range(T)]
                 + [("kv", j, 0) for j in range(KC)] + [("kvT", 0, 0)] + [("m", j, 0) for j in range(KC)]
                 + [("norm", j, b) for j in range(KC) for b in range(3)])
        order = [("xnT", t, 0) for t in range(T)]
        for n, item in enumerate(dense[0:8]):
            order.append(item)
            if n < EC // DG // 2:
                order += [("deg", 2 * n, 0), ("deg", 2 * n + 1, 0)]
            if n == EC // DG // 2:
                order.append(("deg_end", 0, 0))
        order += [("xsT", t, 0) for t in range(T)]
        cost = {"q": 3.4, "k": 3.4, "v": 3.4, "kv": 2.2, "kvT": 1.2, "m": 0.9, "norm": 0.9}
        now, g = 0.0, 0
        for item in dense[8:]:
            order.append(item)
            now += cost[item[0]]
            while g < EG and 4.0 + 2.2 * g < now:
                order.append(("agg", g, 0))
                now += 0.9
                g += 1
        order += [("agg", n, 0) for n in range(g, EG)] + [("rest", 0, 0)]
        for t in range(T):
            order += [("outA", t, 0), ("outB", t, 0)] + ([("x2T", t - 1, 0)] if t else [])
        order.append(("x2T", T - 1, 0))
        group_no = {g: i for i, g in enumerate([i for i in order if i[0] in ("q", "k", "v", "kv", "m", "norm", "outA", "outB")])}
        turn_no = {g: i for i, g in enumerate([i for i in order if i[0] in ("xnT", "xsT", "kvT", "x2T")])}

        block = ctx.enter_context(nc.Block())

        @block.sync
        def _(sp):
            for t in range(0, T - 1, 2):
                sp.dma_start(xn[:, t, :], x[t * P:(t + 1) * P, :]).then_inc(x_in[t], 16)
            sp.wait_ge(x_pad_set, 1)
            sp.dma_start(xn[0:LAST, T - 1, :], x[(T - 1) * P:N, :]).then_inc(x_in[T - 1], 16)
            sp.dma_start(wk_sb, wk).then_inc(wk_in, 16)
            sp.dma_start(wv_sb, wv).then_inc(wv_in, 16)
            for t in range(T):
                sp.wait_ge(scaled_ready, t + 1)
                sp.dma_start(scaled_rows[t * P:(t + 1) * P, :], xn[:, t, :]).then_inc(scaled_out, 16)
            sp.wait_ge(deg_done, 1)
            sp.dma_start(wo_sb, wo).then_inc(wwo_in, 16)
            sp.dma_start(w_sb, wg_nn).then_inc(wwo_in, 16)
            sp.wait_ge(elu_done, QG + T)
            sp.dma_start(brow_sb[:, 0, :], brow[3:4, :].to_broadcast([P, D])).then_inc(bo_in, 16)

            def load_x(t):
                if t >= 2:
                    sp.wait_ge(xr_used, t - 1)
                r = P if t < T - 1 else LAST
                sp.dma_start(xr[0:r, t % 2, :], x[t * P:t * P + r, :]).then_inc(xr_in[t % 2], 16)

            def load_expert(e, b, parts=range(WP)):
                for p in parts:
                    sp.dma_start(ffw[:, b, p * (WROW // WP):(p + 1) * (WROW // WP)],
                                 experts[bass.ds(e, 1), :, p * (WROW // WP):(p + 1) * (WROW // WP)].rearrange("a p n -> p (a n)")
                                 ).then_inc(w_in[b], 16)

            sp.wait_ge(mm_done, group_no[("v", T - 1, 0)] + 1)
            load_x(0)
            load_x(1)
            for t in range(T):
                sp.wait_ge(mm_done, group_no[("outA", t, 0)] + 1)
                if t < 2 * WP:
                    load_expert(t // WP, t // WP, [t % WP])
                sp.wait_ge(rows2_ready, t + 1)
                sp.dma_start(token_rows[t * P:(t + 1) * P, :], rows2[:, t % 2, :]).then_inc(rows2_out[t % 2], 16)
                if t + 2 < T:
                    load_x(t + 2)
            sp.wait_ge(plan_ready, 1)
            blocks = sp.value_load(plan[0:1, BLOCKS:BLOCKS + 1], min_val=MIN_BLOCKS, max_val=BLOCKS)
            for b in range(2):
                e = sp.value_load(plan[0:1, b:b + 1], min_val=0, max_val=NE - 1)
                with sp.If(e != b):
                    sp.wait_ge(w_in[b], WP * 16)
                    load_expert(e, b)
                with sp.If(e == b):
                    sp.sem_inc(w_in[b], WP * 16)
            with sp.Fori(0, PAIRS - 1) as q:
                for b in range(2):
                    with sp.If(q * 2 + (2 + b) < blocks):
                        sp.wait_ge(y_ready, q * (2 * KC) + (b + 1) * KC)
                        e = sp.value_load(plan[0:1, bass.ds(q * 2 + (2 + b), 1)], min_val=0, max_val=NE - 1)
                        load_expert(e, b)

        @block.scalar
        def _(act):
            act.dma_start(dst_sb, dst).then_inc(edges_in, 16)
            act.dma_start(ew_sb[:, :], ew).then_inc(edges_in, 16)
            for t in range(1, T - 1, 2):
                act.dma_start(xn[:, t, :], x[t * P:(t + 1) * P, :]).then_inc(x_in[t], 16)
            act.dma_start(wq_sb, wq).then_inc(wq_in, 16)
            act.dma_start(bq_sb[:, :], bq).then_inc(small_in, 16)
            for n in range(3):
                act.dma_start(brow_sb[:, n, :], brow[n:n + 1, :].to_broadcast([P, D])).then_inc(small_in, 16)
            act.dma_start(gw_sb[:, :, :], gate_w).then_inc(small_in, 16)
            act.dma_start(gb_sb[:, :], gate_b.to_broadcast([P, NE])).then_inc(small_in, 16)
            act.dma_start(src_sb[:, :], src).then_inc(src_in, 16)

            def empty_turn(kind, t, to):
                n = turn_no[(kind, t, 0)]
                act.wait_ge(tr_done, n + 1)
                nc.scalar.activation(to, ps[:, TRB[n % 2], :].rearrange("p (c n) -> p c n", c=KC), ACT.Copy).then_inc(tr_free, 1)

            def q_bias(m, b):
                n, e, cols = group_no[("q", m, b)], 3 * m + b, NB[b][1]
                act.wait_ge(mm_done, n + 1)
                if e >= 2:
                    act.wait_ge(elu_done, e - 1)
                nc.scalar.activation(biased[:, e % 2, 0:cols], ps[:, PRB[n % 4], 0:cols], ACT.Identity,
                                     bias=bq_sb[:, m:m + 1]).then_inc(bank_free[n % 4], 1)
                act.wait_ge(bank_free[n % 4], n // 4 + 1)
                act.sem_inc(biased_ready, 1)

            def exp_low(e):
                cols = NB[e % 3][1] if e < QG else D
                act.wait_ge(low_ready, e + 1)
                if e >= 2:
                    act.wait_ge(elu_done, e - 1)
                nc.scalar.activation(expd[:, e % 2, 0:cols], low[:, e % 2, 0:cols], ACT.Exp).then_inc(exp_done, 1)

            act.wait_ge(var_ready, 1)
            nc.scalar.activation(std[:, :], veps[:, :], ACT.Sqrt).then_inc(std_ready, 1)
            for kind, m, b in order:
                if kind == "xnT":
                    empty_turn(kind, m, xnT[:, :, m * P:(m + 1) * P])
                if kind == "q":
                    if (m, b) == (0, 0):
                        act.wait_ge(small_in, 16 * 6)
                    q_bias(m, b)
                    if 3 * m + b:
                        exp_low(3 * m + b - 1)
                if kind == "k":
                    exp_low(QG + m - 1)
                if kind == "v" and m == 0:
                    exp_low(QG + T - 1)
                if kind == "deg_end":
                    act.wait_ge(root_ask, 1)
                    nc.scalar.activation(degroot[:, :], deg[:, :], ACT.Sqrt).then_inc(root_ready, 1)
                if kind == "xsT":
                    empty_turn(kind, m, sumT[:, :, m * P:(m + 1) * P])
                if kind == "kvT":
                    empty_turn(kind, m, kvT)
                if kind == "outB":
                    act.wait_ge(var2_ready, m + 1)
                    nc.scalar.activation(std[:, m:m + 1], veps[:, m:m + 1], ACT.Sqrt).then_inc(std2_ready, 1)
                if kind == "x2T":
                    if m >= 2:
                        act.wait_ge(logits_done, m - 1)
                    empty_turn(kind, m, x2T[:, m % 2, :, :])
            act.wait_ge(plan_ready, 1)
            blocks = act.value_load(plan[0:1, BLOCKS:BLOCKS + 1], min_val=MIN_BLOCKS, max_val=BLOCKS)
            with act.Fori(0, PAIRS) as q:
                for b in range(2):
                    with act.If(q * 2 + b < blocks):
                        act.wait_ge(xgT_done, q * 2 + (b + 1))
                        nc.scalar.activation(xgT[:, 0:2, :], ps[:, 0, 0:2 * BLK].rearrange("p (c n) -> p c n", c=2),
                                             ACT.Copy).then_inc(xgT_act, 1)
                        act.wait_ge(w_in[b], q * (16 * WP) + 32 * WP)
                        for m in range(HC):
                            act.wait_ge(h_done, q * (2 * HC) + (b * HC + m + 1))
                            nc.scalar.activation(hT[:, m, :], ps[:, PRB[m % 4], 0:BLK], ACT.Relu,
                                                 bias=b1[b][:, m:m + 1]).then_inc(h_ready, 1)


        @block.gpsimd
        def _(pool):
            steps = [0]

            def step(ins):
                steps[0] += 1
                ins.then_inc(pool_step, 1)
                pool.wait_ge(pool_step, steps[0])

            step(nc.gpsimd.memset(xn[96:P, T - 1, :], 0.0))
            pool.sem_inc(x_pad_set, 1)
            nc.gpsimd.iota(col_i[:, :], [[1, P]], base=0, channel_multiplier=0)
            nc.gpsimd.iota(token_i[:, :], [[P, T]], base=0, channel_multiplier=1)
            nc.gpsimd.iota(falling_i[:, :], [[-1, NE]], base=NE, channel_multiplier=0)
            nc.gpsimd.iota(blk_i[:, :], [[1, BLOCKS]], base=0, channel_multiplier=0)
            nc.gpsimd.memset(empty[:, :], N)
            nc.gpsimd.memset(ident[:, :], 0.0)
            nc.gpsimd.memset(before[:, :], 1.0)
            nc.gpsimd.memset(ones[:, :], 1.0)
            nc.gpsimd.memset(zrow[:, :], 0.0)
            nc.gpsimd.memset(sumT[:, :, NP:NP + W], 0.0)
            nc.gpsimd.memset(same_head[:, :], 0.0)
            step(nc.gpsimd.memset(zero_g[:, :], 0.0))
            step(nc.gpsimd.memset(same_head[0:HEAD, 0:HEAD], 1.0))
            step(nc.gpsimd.memset(same_head[HEAD:P, HEAD:P], 1.0))
            nc.gpsimd.affine_select(out=ident[:, :], in_=ident[:, :], compare_op=ALU.not_equal, fill=1.0,
                                    base=0, pattern=[[-1, P]], channel_multiplier=1)
            step(nc.gpsimd.affine_select(out=before[:, :], in_=before[:, :], compare_op=ALU.is_gt, fill=0.0,
                                         base=0, pattern=[[1, P]], channel_multiplier=-1))
            pool.sem_inc(const_set, 1)
            pool.dma_start(slot_tokens[:, :].rearrange("(p s) a -> p (s a)", p=P), empty[:, :]).then_inc(empty_out, 16)
            step(nc.gpsimd.memset(v_sb[:, :, :, P:VW], 1.0))
            pool.sem_inc(const_set, 1)

            def gather(to, idx, done):
                nc.gpsimd.indirect_dma_start(
                    out=to, out_offset=None, in_=scaled_rows[:, :],
                    in_offset=bass.IndirectOffsetOnAxis(ap=idx.bitcast(U32), axis=0)).then_inc(done, 16)

            pool.wait_ge(src_in, 16)
            pool.wait_ge(scaled_out, 16 * T)
            for c in range(EG * G):
                if c >= SLOTS:
                    pool.wait_ge(sum_done, (c - SLOTS) // G + 1)
                gather(ring[:, c % SLOTS, :], src_sb[:, c:c + 1], gathered[c % SLOTS])
            pool.wait_ge(sum_done, EG)
            total = pool.value_load(rest_end[0:1, 0:1], min_val=0, max_val=EG * MORE)
            with pool.If(total > 0):
                with pool.Fori(0, EG) as g:
                    r0 = pool.value_load(rest[0:1, bass.ds(g, 1)], min_val=0, max_val=EG * MORE)
                    r1 = pool.value_load(rest[0:1, bass.ds(g + 1, 1)], min_val=0, max_val=EG * MORE)
                    with pool.If(r0 < r1):
                        with pool.Fori(r0, r1) as r:
                            pool.wait_ge(rest_done, r + 1)
                            pool.sem_inc(pool_passed, 1)
                            nc.gpsimd.tensor_copy(src_now[:, :], src_sb[:, bass.ds(g * G, G)]).then_inc(rest_now, 1)
                            pool.wait_ge(rest_now, r + 1)
                            pool.sem_inc(pool_passed, 1)
                            for j in range(G):
                                gather(ring[:, j, :], src_now[:, j:j + 1], rest_in)
            pool.wait_ge(bo_in, 16)
            step(nc.gpsimd.tensor_tensor(brow_sb[:, 2, :], brow_sb[:, 2, :], brow_sb[:, 0, :], ALU.add))
            for t in range(T):
                pool.wait_ge(xr_in[t % 2], 16 * (t // 2 + 1))
                nc.gpsimd.tensor_tensor(xr[:, t % 2, :], xr[:, t % 2, :], brow_sb[:, 2, :], ALU.add).then_inc(xr_ready, 1)
            pool.wait_ge(plan_ready, 1)
            pool.wait_ge(empty_out, 16)
            for t in range(T):
                r = P if t < T - 1 else LAST
                nc.gpsimd.indirect_dma_start(
                    out=slot_tokens[:, :], out_offset=bass.IndirectOffsetOnAxis(ap=slot_i[0:r, t:t + 1].bitcast(U32), axis=0),
                    in_=token_i[0:r, t:t + 1], in_offset=None).then_inc(ids_out, 16)
            pool.wait_ge(ids_out, 16 * T)
            pool.dma_start(slots_a[:, 0:BLOCKS], slot_tokens[0:P * BLOCKS, :].rearrange("(s b) a -> s (b a)", s=P)).then_inc(slots_in, 16)
            pool.dma_start(slots_b[:, 0:BLOCKS], slot_tokens[P * BLOCKS:BLK * BLOCKS, :].rearrange("(s b) a -> s (b a)", s=B2ND)).then_inc(slots_in, 16)
            pool.wait_ge(slots_in, 32)
            for b in range(2):
                pool.wait_ge(rows2_out[b], 16 * len(range(b, T, 2)))
            blocks = pool.value_load(plan[0:1, BLOCKS:BLOCKS + 1], min_val=MIN_BLOCKS, max_val=BLOCKS)

            def fetch(i, b, n):
                nc.gpsimd.tensor_copy(now_a[:, b:b + 1], slots_a[:, bass.ds(i, 1)]).then_inc(now_set, 1)
                nc.gpsimd.tensor_copy(now_b[:, b:b + 1], slots_b[:, bass.ds(i, 1)]).then_inc(now_set, 1)
                pool.wait_ge(now_set, n * 2 + 2)
                pool.sem_inc(pool_passed, 1)
                for s, now in enumerate((now_a, now_b)):
                    nc.gpsimd.indirect_dma_start(
                        out=xg[0:now.shape[0], b, s, :], out_offset=None, in_=token_rows[:, :],
                        in_offset=bass.IndirectOffsetOnAxis(ap=now[:, b:b + 1].bitcast(U32), axis=0),
                    ).then_inc(xg_in[b], 16)

            fetch(0, 0, 0)
            fetch(1, 1, 1)
            with pool.Fori(0, PAIRS) as q:
                for b in range(2):
                    with pool.If(q * 2 + b < blocks):
                        pool.wait_ge(yo_ready, q * 4 + (2 * b + 3))
                        pool.sem_inc(pool_passed, 1)
                        for s, now in enumerate((now_a, now_b)):
                            nc.gpsimd.indirect_dma_start(
                                out=out, out_offset=bass.IndirectOffsetOnAxis(ap=now[:, b:b + 1].bitcast(U32), axis=0),
                                in_=yo[0:now.shape[0], b, s, :], in_offset=None,
                                bounds_check=N - 1, oob_is_err=False).then_inc(out_done[b], 16)
                        pool.wait_ge(out_done[b], q * 32 + 32)
                    with pool.If(q * 2 + (b + 2) < blocks):
                        fetch(q * 2 + (b + 2), b, q * 2 + (b + 2))


        @block.vector
        def _(dve):
            steps = [0]

            def step(ins):
                steps[0] += 1
                ins.then_inc(dve_step, 1)
                dve.wait_ge(dve_step, steps[0])

            v = nc.vector
            dve.wait_ge(edges_in, 32)
            v.tensor_scalar(dst_hi, dst_sb, 7, None, ALU.arith_shift_right)
            v.tensor_scalar(dst_lo, dst_sb, P - 1, None, ALU.bitwise_and)
            step(v.tensor_copy(ew_h[:, 0, :], ew_sb[:, :]))
            step(v.tensor_tensor(ew_left[:, 0, :], ew_sb[:, :], ew_h[:, 0, :], ALU.subtract))
            v.tensor_copy(hi_h, dst_hi)
            v.tensor_copy(dst_lof, dst_lo)
            step(v.tensor_copy(ew_h[:, 1, :], ew_left[:, 0, :]))
            step(v.tensor_tensor(ew_left[:, 1, :], ew_left[:, 0, :], ew_h[:, 1, :], ALU.subtract))
            for t in range(T):
                v.tensor_scalar(in_tile[:, t, :], hi_h, float(t), None, ALU.is_equal)
            step(v.tensor_copy(ew_h[:, 2, :], ew_left[:, 1, :]))
            for w in range(3):
                ins = v.tensor_tensor(deg_coef[:, :, w, :], in_tile.rearrange("p t c -> p c t"),
                                      ew_h[:, w, :][:, :, None].to_broadcast([P, EC, T]), ALU.mult)
            ins.then_inc(coef_ready, 1)
            dve.wait_ge(const_set, 1)
            v.tensor_copy(col_f[:, :], col_i[:, :])
            v.tensor_copy(col_h[:, :], col_i[:, :])
            v.tensor_copy(token_f[:, :], token_i[:, :])
            v.tensor_copy(falling[:, :], falling_i[:, :])
            v.tensor_copy(blk_f[:, :], blk_i[:, :])
            v.tensor_copy(dst_f[:, :], dst_sb).then_inc(dst_ready, 1)
            for t in range(T):
                dve.wait_ge(x_in[t], 16)
                v.bn_stats(stat[:, t, :], xn[:, t, :]).then_inc(stats_ready, 1)
            for t in range(T):
                dve.wait_ge(stats_ready, t + 1)
                ins = v.bn_aggr(mv[:, t, :], stat[:, t, :])
            step(ins)
            v.tensor_scalar(veps[:, :], mv[:, :, 1], EPS, None, ALU.add).then_inc(var_ready, 1)
            dve.wait_ge(std_ready, 1)
            step(v.reciprocal(rstd[:, :], std[:, :]))
            for t in range(T):
                v.tensor_scalar(xn[:, t, :], xn[:, t, :], mv[:, t, 0:1], rstd[:, t:t + 1], ALU.subtract,
                                ALU.mult).then_inc(xn_ready, 1)

            def deg_hots(n):
                if n >= 2:
                    dve.wait_ge(deg_hot_used, n - 1)
                for c in range(DG):
                    ins = v.tensor_scalar(deg_hot[:, n % 2, c, :], col_h[:, :], dst_lof[:, n * DG + c:n * DG + c + 1], None,
                                          ALU.is_equal)
                ins.then_inc(deg_hot_ready, 1)

            deg_hots(0)
            dve.wait_ge(dst_turned, 1)
            for a, r in ((0, P), (1, EC - P)):
                v.tensor_reduce(ends[0:r, a, 0:1], ps[0:r, 7, a * P:(a + 1) * P], AX_X, ALU.min)
                ins = v.tensor_reduce(ends[0:r, a, 1:2], ps[0:r, 7, a * P:(a + 1) * P], AX_X, ALU.max)
            step(ins)
            for a, r in ((0, P), (1, EC - P)):
                for w in range(2):
                    ins = v.tensor_scalar(ends_all[0:r, 2 * a + w, :], ones[0:r, :], ends[0:r, a, w:w + 1], None, ALU.mult)
            ins.then_inc(ends_ready, 1)
            deg_hots(1)

            def windows():
                dve.wait_ge(ends_done, 1)
                v.tensor_reduce(group_lo[:, :], ps[:, 7, 0:EG * G].rearrange("p (g c) -> p g c", c=G), AX_X, ALU.min)
                step(v.tensor_reduce(group_hi[:, :], ps[:, 7, 256:256 + EG * G].rearrange("p (g c) -> p g c", c=G), AX_X, ALU.max))
                v.tensor_tensor(rel[:, 0:EG * G].rearrange("p (g c) -> p g c", c=G), dst_f[:, 0:EG * G].rearrange("p (g c) -> p g c", c=G),
                                group_lo[:, :][:, :, None].to_broadcast([P, EG, G]), ALU.subtract)
                v.tensor_copy(window[:, :], group_lo[0:1, :])
                step(v.tensor_tensor(more_i[:, :], group_hi[:, :], group_lo[:, :], ALU.subtract))
                step(v.tensor_scalar(more_i[:, :], more_i[:, :], W.bit_length() - 1, None, ALU.arith_shift_right))
                step(v.tensor_copy(more[:, :], more_i[:, :]))
                step(v.tensor_tensor_scan(after[:, :], more[:, :], zero_g[:, :], 0.0, ALU.add, ALU.add))
                v.memset(rest[:, 0:1], 0)
                v.tensor_copy(rest[:, 1:EG + 1], after[0:1, :])
                step(v.tensor_copy(rest_end[:, :], after[0:1, EG - 1:EG]))
                dve.sem_inc(windows_ready, 1)

            def degrees():
                dve.wait_ge(deg_done, 1)
                step(v.tensor_scalar(deg3[:, :], ps[:, 6, 0:T], 1.0, None, ALU.add))
                step(v.tensor_tensor(deg3[:, :], deg3[:, :], ps[:, 6, T:2 * T], ALU.add))
                step(v.tensor_tensor(deg3[:, :], deg3[:, :], ps[:, 6, 2 * T:3 * T], ALU.add))
                v.tensor_scalar(degpos[:, :], deg3[:, :], 0.0, None, ALU.is_gt)
                v.tensor_scalar(deg[:, :], deg3[:, :], 1e-37, None, ALU.max).then_inc(root_ask, 1)
                dve.wait_ge(root_ready, 1)
                step(v.reciprocal(dinv[:, :], degroot[:, :]))
                step(v.tensor_tensor(dinv[:, :], dinv[:, :], degpos[:, :], ALU.mult))
                dve.wait_ge(tr_done, T)
                for t in range(T):
                    v.tensor_scalar(xn[:, t, :], xn[:, t, :], dinv[:, t:t + 1], None, ALU.mult).then_inc(scaled_ready, 1)

            def bank_of(kind, m, b=0):
                n = group_no[(kind, m, b)]
                dve.wait_ge(mm_done, n + 1)
                return bank_free[n % 4], ps[:, PRB[n % 4], :]

            def low_of(e, y, cols):
                if e >= 2:
                    dve.wait_ge(exp_done, e - 1)
                v.tensor_scalar(low[:, e % 2, 0:cols], y, 0.0, None, ALU.min).then_inc(low_ready, 1)

            def q_low(m, b):
                e, cols = 3 * m + b, NB[b][1]
                dve.wait_ge(biased_ready, e + 1)
                low_of(e, biased[:, e % 2, 0:cols], cols)

            def k_low(t):
                if t == 0:
                    dve.wait_ge(scaled_out, 16 * T)
                    dve.wait_ge(tr_done, turn_no[("xsT", T - 1, 0)] + 1)
                free, bank = bank_of("k", t)
                step(v.tensor_tensor(k_sb[:, t, :], bank, brow_sb[:, 0, :], ALU.add))
                dve.sem_inc(free, 1)
                low_of(QG + t, k_sb[:, t, :], D)

            def elu(e):
                if e < QG:
                    first, cols = NB[e % 3]
                    y, to = biased[:, e % 2, 0:cols], qT[:, e // 3, first:first + cols]
                else:
                    cols = D
                    y = to = k_sb[:, e - QG, :]
                dve.wait_ge(exp_done, e + 1)
                v.scalar_tensor_tensor(out=to, in0=y, scalar=0.0, in1=expd[:, e % 2, 0:cols],
                                       op0=ALU.max, op1=ALU.add).then_inc(elu_done, 1)

            def hots(g):
                if g >= EG:
                    return
                if g >= SLOTS // G:
                    dve.wait_ge(sum_done, g - SLOTS // G + 1)
                for c in range(g * G, (g + 1) * G):
                    ins = v.tensor_scalar(hot[:, c % SLOTS, :], col_f[:, 0:W], rel[:, c:c + 1], ew_sb[:, c:c + 1],
                                          ALU.is_equal, ALU.mult)
                ins.then_inc(hot_ready, 1)

            def add_window(bank, start):
                to = sumT[:, :, bass.ds(start, W)]
                return v.tensor_tensor(to, ps[:, bank, 0:KC * W].rearrange("p (c n) -> p c n", c=KC), to, ALU.add)

            def rest_windows():
                total = dve.value_load(rest_end[0:1, 0:1], min_val=0, max_val=EG * MORE)
                dve.sem_inc(rest_hot, 1)
                dve.sem_inc(rest_set, 1)
                dve.sem_inc(rest_added, 1)
                dve.wait_ge(sum_added, EG)
                with dve.If(total > 0):
                    with dve.Fori(0, EG) as g:
                        r0 = dve.value_load(rest[0:1, bass.ds(g, 1)], min_val=0, max_val=EG * MORE)
                        r1 = dve.value_load(rest[0:1, bass.ds(g + 1, 1)], min_val=0, max_val=EG * MORE)
                        start = dve.value_load(window[0:1, bass.ds(g, 1)], min_val=0, max_val=NP - 1)
                        dve.wait_ge(rest_hot, r0 + 1)
                        dve.wait_ge(rest_set, r0 + g + 1)
                        v.tensor_copy(edge_now[:, 0, :], rel[:, bass.ds(g * G, G)])
                        v.tensor_copy(edge_now[:, 1, :], ew_sb[:, bass.ds(g * G, G)]).then_inc(rest_set, 1)
                        with dve.If(r0 < r1):
                            with dve.Fori(r0, r1) as r:
                                dve.wait_ge(rest_hot, r + 1)
                                dve.wait_ge(rest_set, r + g + 2)
                                v.tensor_scalar(edge_now[:, 0, :], edge_now[:, 0, :], float(-W), None, ALU.add).then_inc(rest_set, 1)
                                dve.wait_ge(rest_set, r + g + 3)
                                for j in range(G):
                                    ins = v.tensor_scalar(hot[:, j, :], col_f[:, 0:W], edge_now[:, 0, j:j + 1],
                                                          edge_now[:, 1, j:j + 1], ALU.is_equal, ALU.mult)
                                ins.then_inc(rest_hot, 1)
                                dve.wait_ge(rest_done, r + 2)
                                dve.wait_ge(rest_added, r + 1)
                                at = nc.s_assert_within(start + (r - r0 + 1) * W, 0, NP - 1,
                                                        skip_runtime_bounds_check_because="further windows start at or before the group's greatest destination")
                                add_window(6, at).then_inc(rest_added, 1)

            def out_rows(t):
                b = t % 2
                free, bank = bank_of("outA", t)
                if t >= 2:
                    dve.wait_ge(rows2_out[b], 16 * (t // 2))
                dve.wait_ge(xr_ready, t + 1)
                step(v.scalar_tensor_tensor(out=xr[:, b, :], in0=bank, scalar=dinv[:, t:t + 1], in1=xr[:, b, :],
                                            op0=ALU.mult, op1=ALU.add))
                dve.sem_inc(free, 1)
                free, bank = bank_of("outB", t)
                if t >= 2:
                    dve.wait_ge(tr_done, turn_no[("x2T", t - 2, 0)] + 1)
                step(v.tensor_tensor(rows2[:, b, 0:D], bank, xr[:, b, :], ALU.add))
                dve.sem_inc(free, 1)
                dve.sem_inc(xr_used, 1)
                step(v.bn_stats(stat[:, t, :], rows2[:, b, 0:D]))
                step(v.bn_aggr(mv[:, t, :], stat[:, t, :]))
                v.tensor_scalar(veps[:, t:t + 1], mv[:, t, 1:2], EPS, None, ALU.add).then_inc(var2_ready, 1)
                dve.wait_ge(std2_ready, t + 1)
                step(v.reciprocal(rstd[:, t:t + 1], std[:, t:t + 1]))
                v.tensor_scalar(rows2[:, b, D:2 * D], rows2[:, b, 0:D], mv[:, t, 0:1], rstd[:, t:t + 1],
                                ALU.subtract, ALU.mult).then_inc(rows2_ready, 1)

            dve.wait_ge(small_in, 16 * 6)
            dve.wait_ge(const_set, 2)
            for kind, m, b in order:
                if kind == "q":
                    q_low(m, b)
                    if 3 * m + b:
                        elu(3 * m + b - 1)
                if kind == "deg":
                    if m + 2 < EC // DG:
                        deg_hots(m + 2)
                    if m == 2:
                        windows()
                if kind == "deg_end":
                    degrees()
                if kind == "k":
                    k_low(m)
                    elu(QG + m - 1)
                if kind == "v":
                    if m == 0:
                        elu(QG + T - 1)
                    free, bank = bank_of(kind, m)
                    v.tensor_tensor(v_sb[:, m, :, 0:P], bank.rearrange("p (c n) -> p c n", c=KC),
                                    brow_sb[:, 1, :].rearrange("p (c n) -> p c n", c=KC), ALU.add).then_inc(free, 1)
                if kind == "kv":
                    free, bank = bank_of(kind, m)
                    v.tensor_tensor(kvm[:, m, :], bank[:, 0:P], same_head[:, :], ALU.mult)
                    step(v.tensor_scalar(ksm[:, m, :], same_head[:, :], bank[:, P:P + 1], None, ALU.mult))
                    dve.sem_inc(free, 1)
                    dve.sem_inc(kv_masked, 1)
                if kind == "m":
                    free, bank = bank_of(kind, m)
                    step(v.tensor_copy(m_sb[:, m, :], bank))
                    dve.sem_inc(free, 1)
                    dve.sem_inc(m_ready, 1)
                if kind == "norm":
                    first, cols = NB[b]
                    free, bank = bank_of(kind, m, b)
                    step(v.tensor_scalar(low[:, b % 2, 0:cols], bank[:, 0:cols], 1e-6, None, ALU.add))
                    dve.sem_inc(free, 1)
                    step(v.reciprocal(low[:, b % 2, 0:cols], low[:, b % 2, 0:cols]))
                    step(v.tensor_tensor(qT[:, m, first:first + cols], qT[:, m, first:first + cols], low[:, b % 2, 0:cols], ALU.mult))
                    dve.sem_inc(qn_ready, 1)
                if kind == "agg":
                    if m == 0:
                        for g in range(SLOTS // G - 1):
                            hots(g)
                        dve.wait_ge(tr_free, turn_no[("xsT", T - 1, 0)] + 1)
                    hots(m + SLOTS // G - 1)
                    start = dve.value_load(window[0:1, m:m + 1], min_val=0, max_val=NP - 1)
                    dve.wait_ge(sum_done, m + 1)
                    if m:
                        dve.wait_ge(sum_added, m)
                    add_window(6 + m % 2, start).then_inc(sum_added, 1)
                if kind == "rest":
                    rest_windows()
                if kind == "outB":
                    out_rows(m)
            v.tensor_scalar(valid[:, :], token_f[:, :], float(N), None, ALU.is_lt)
            dve.wait_ge(logits_done, T)
            step(v.tensor_tensor(logit[:, :, :], ps[:, 6, 0:T * NE].rearrange("p (t e) -> p t e", t=T),
                                 gb_sb[:, None, :].to_broadcast([P, T, NE]), ALU.add))
            step(v.tensor_reduce(best[:, :], logit[:, :, :], AX_X, ALU.max))
            step(v.tensor_tensor(top[:, :, :], logit[:, :, :], best[:, :][:, :, None].to_broadcast([P, T, NE]), ALU.is_equal))
            step(v.tensor_tensor(top[:, :, :], top[:, :, :], falling[:, None, :].to_broadcast([P, T, NE]), ALU.mult))
            step(v.tensor_reduce(best[:, :], top[:, :, :], AX_X, ALU.max))
            step(v.tensor_tensor(choice[:, :, :], best[:, :][:, :, None].to_broadcast([P, T, NE]),
                                 falling[:, None, :].to_broadcast([P, T, NE]), ALU.is_equal))
            v.tensor_tensor(choice[:, :, :], choice[:, :, :], valid[:, :][:, :, None].to_broadcast([P, T, NE]), ALU.mult).then_inc(choice_ready, 1)
            dve.wait_ge(rank_done, 1)
            step(v.memset(count[:, :], 0.0))
            for t in range(T):
                v.tensor_tensor(rank[:, t, :], ps[:, 7, t * NE:(t + 1) * NE], count[:, :], ALU.add)
                step(v.tensor_tensor(count[:, :], ps[:, 7, 256 + t * NE:256 + (t + 1) * NE], count[:, :], ALU.add))
            step(v.memset(nblk[:, :], 0.0))
            for i in range(-(-N // BLK)):
                step(v.scalar_tensor_tensor(out=nblk[:, :], in0=count[:, :], scalar=float(i * BLK), in1=nblk[:, :],
                                            op0=ALU.is_gt, op1=ALU.add))
            step(v.tensor_tensor_scan(blk_end[:, :], nblk[:, :], zero_g[:, 0:NE], 0.0, ALU.add, ALU.add))
            step(v.tensor_tensor(blk_start[:, :], blk_end[:, :], nblk[:, :], ALU.subtract))
            step(v.tensor_tensor(pick[:, :, :], choice[:, :, :], rank[:, :, :], ALU.mult))
            step(v.tensor_reduce(rank_t[:, :], pick[:, :, :], AX_X, ALU.add))
            step(v.tensor_tensor(pick[:, :, :], choice[:, :, :], blk_start[:, None, :].to_broadcast([P, T, NE]), ALU.mult))
            step(v.tensor_reduce(start_t[:, :], pick[:, :, :], AX_X, ALU.add))
            step(v.memset(over_t[:, :], 0.0))
            for i in range(1, -(-N // BLK)):
                step(v.scalar_tensor_tensor(out=over_t[:, :], in0=rank_t[:, :], scalar=float(i * BLK), in1=over_t[:, :],
                                            op0=ALU.is_ge, op1=ALU.add))
            step(v.tensor_tensor(start_t[:, :], start_t[:, :], over_t[:, :], ALU.add))
            step(v.scalar_tensor_tensor(out=slot_f[:, :], in0=over_t[:, :], scalar=float(-BLK), in1=rank_t[:, :],
                                        op0=ALU.mult, op1=ALU.add))
            step(v.scalar_tensor_tensor(out=slot_f[:, :], in0=slot_f[:, :], scalar=float(BLOCKS), in1=start_t[:, :],
                                        op0=ALU.mult, op1=ALU.add))
            step(v.tensor_copy(slot_i[:, :], slot_f[:, :]))
            step(v.memset(blk_e[:, :], 0.0))
            for e in range(NE - 1):
                step(v.scalar_tensor_tensor(out=blk_e[:, :], in0=blk_f[:, :], scalar=blk_end[:, e:e + 1], in1=blk_e[:, :],
                                            op0=ALU.is_ge, op1=ALU.add))
            v.tensor_copy(plan[:, 0:BLOCKS], blk_e[0:1, :])
            step(v.tensor_copy(plan[:, BLOCKS:BLOCKS + 1], blk_end[0:1, NE - 1:NE]))
            dve.sem_inc(plan_ready, 1)
            dve.sem_inc(yo_ready, 1)
            blocks = dve.value_load(plan[0:1, BLOCKS:BLOCKS + 1], min_val=MIN_BLOCKS, max_val=BLOCKS)
            with dve.Fori(0, PAIRS) as q:
                for b in range(2):
                    with dve.If(q * 2 + b < blocks):
                        dve.wait_ge(xgT_done, q * 2 + (b + 1))
                        v.tensor_copy(xgT[:, 2:4, :], ps[:, 1, 0:2 * BLK].rearrange("p (c n) -> p c n", c=2)).then_inc(xgT_dve, 1)
                        dve.wait_ge(w_in[b], q * (16 * WP) + 32 * WP)
                        for j in range(KC):
                            dve.wait_ge(y_done, q * (2 * KC) + (b * KC + j + 1))
                            v.tensor_scalar(yT[:, j, :], ps[:, 6 + j % 2, 0:BLK], b2[b][:, j:j + 1], None, ALU.add).then_inc(y_ready, 1)
                        dve.wait_ge(yr_done, q * 2 + (b + 1))
                        dve.wait_ge(xg_in[b], q * 32 + 32)
                        v.tensor_tensor(yo[:, b, 0, :], ps[:, 0, :], xg[:, b, 0, 0:D], ALU.add).then_inc(yo_ready, 1)
                        v.tensor_tensor(yo[0:B2ND, b, 1, :], ps[0:B2ND, 1, :], xg[0:B2ND, b, 1, 0:D], ALU.add).then_inc(yo_ready, 1)

        @block.tensor
        def _(pe):
            mm = nc.tensor.matmul

            def turn(kind, t, block_of):
                n = turn_no[(kind, t, 0)]
                if n >= 2:
                    pe.wait_ge(tr_free, n - 1)
                for c in range(KC):
                    ins = nc.tensor.transpose(ps[:, TRB[n % 2], c * P:(c + 1) * P], block_of(c), ident[:, :])
                ins.then_inc(tr_done, 1)

            def group(kind, m, b, cols, parts):
                n = group_no[(kind, m, b)]
                if n >= 4:
                    pe.wait_ge(bank_free[n % 4], n // 4)
                for i, (left, right) in enumerate(parts):
                    ins = mm(ps[:, PRB[n % 4], 0:cols], left, right, start=(i == 0), stop=(i == len(parts) - 1))
                ins.then_inc(mm_done, 1)

            def window_sum(bank, rows, hots, done):
                for c in range(KC):
                    for j in range(G):
                        ins = mm(ps[:, bank, c * W:(c + 1) * W], rows[j][:, c * P:(c + 1) * P], hots[j],
                                 start=(j == 0), stop=(j == G - 1))
                ins.then_inc(done, 1)

            def gate(t):
                pe.wait_ge(tr_free, turn_no[("x2T", t, 0)] + 1)
                for c in range(KC):
                    ins = mm(ps[:, 6, t * NE:(t + 1) * NE], x2T[:, t % 2, c, :], gw_sb[:, c, :], start=(c == 0), stop=(c == KC - 1))
                ins.then_inc(logits_done, 1)

            pe.wait_ge(const_set, 1)
            pe.wait_ge(dst_ready, 1)
            nc.tensor.transpose(ps[:, 7, 0:P], dst_f[:, 0:P], ident[:, :])
            nc.tensor.transpose(ps[0:EC - P, 7, P:2 * P], dst_f[:, P:EC], ident[:, :]).then_inc(dst_turned, 1)
            for kind, m, b in order:
                if kind == "xnT":
                    pe.wait_ge(xn_ready, m + 1)
                    turn(kind, m, lambda c: xn[:, m, c * P:(c + 1) * P])
                if kind == "q":
                    first, cols = NB[b]
                    if (m, b) == (0, 0):
                        pe.wait_ge(wq_in, 16)
                        pe.wait_ge(tr_free, T)
                    group(kind, m, b, cols, [(wq_sb[:, c, m * P:(m + 1) * P], xnT[:, c, first:first + cols]) for c in range(KC)])
                if kind == "deg":
                    if m == 0:
                        pe.wait_ge(ends_ready, 1)
                        for w in range(2):
                            mm(ps[:, 7, w * 256:w * 256 + P], ends_all[:, w, :], ident[:, :], start=True, stop=True)
                            ins = mm(ps[:, 7, w * 256 + P:w * 256 + EC], ends_all[0:EC - P, 2 + w, :], ident[0:EC - P, 0:EC - P],
                                     start=True, stop=True)
                        ins.then_inc(ends_done, 1)
                        pe.wait_ge(coef_ready, 1)
                    pe.wait_ge(deg_hot_ready, m + 1)
                    for c in range(DG):
                        ins = mm(ps[:, 6, 0:3 * T], deg_hot[:, m % 2, c, :], deg_coef[:, m * DG + c, :, :].rearrange("p w t -> p (w t)"),
                                 start=(m == 0 and c == 0), stop=(m == EC // DG - 1 and c == DG - 1), skip_group_check=True)
                    ins.then_inc(deg_hot_used, 1)
                if kind == "deg_end":
                    pe.wait_ge(deg_hot_used, EC // DG)
                    pe.sem_inc(deg_done, 1)
                if kind == "xsT":
                    pe.wait_ge(scaled_ready, m + 1)
                    turn(kind, m, lambda c: xn[:, m, c * P:(c + 1) * P])
                if kind == "k":
                    pe.wait_ge(wk_in, 16)
                    group(kind, m, b, D, [(xnT[:, c, m * P:(m + 1) * P], wk_sb[:, c, :]) for c in range(KC)])
                if kind == "v":
                    pe.wait_ge(wv_in, 16)
                    group(kind, m, b, D, [(xnT[:, c, m * P:(m + 1) * P], wv_sb[:, c, :]) for c in range(KC)])
                if kind == "kv":
                    if m == 0:
                        pe.wait_ge(elu_done, QG + T)
                        n = group_no[("v", T - 1, 0)]
                        for last in range(n - 3, n + 1):
                            pe.wait_ge(bank_free[last % 4], last // 4 + 1)
                    rows = [P] * (T - 1) + [LAST]
                    group(kind, m, b, VW, [(k_sb[0:r, t, m * P:(m + 1) * P], v_sb[0:r, t, m, :]) for t, r in enumerate(rows)])
                if kind == "kvT":
                    pe.wait_ge(kv_masked, KC)
                    turn(kind, m, lambda c: kvm[:, c, :])
                if kind == "m":
                    if m == 0:
                        pe.wait_ge(wwo_in, 32)
                        pe.wait_ge(tr_free, turn_no[("kvT", 0, 0)] + 1)
                    group(kind, m, b, D, [(kvT[:, m, :], wo_sb[:, m, :])])
                if kind == "norm":
                    first, cols = NB[b]
                    group(kind, m, b, cols, [(ksm[:, m, :], qT[:, m, first:first + cols])])
                if kind == "agg":
                    if m >= 2:
                        pe.wait_ge(sum_added, m - 1)
                    pe.wait_ge(hot_ready, m + 1)
                    slots = [(m * G + j) % SLOTS for j in range(G)]
                    for s in slots:
                        pe.wait_ge(gathered[s], 16 * (m * G // SLOTS + 1))
                    window_sum(6 + m % 2, [ring[:, s, :] for s in slots], [hot[:, s, :] for s in slots], sum_done)
                if kind == "rest":
                    pe.wait_ge(sum_added, EG)
                    pe.wait_ge(windows_ready, 1)
                    total = pe.value_load(rest_end[0:1, 0:1], min_val=0, max_val=EG * MORE)
                    pe.sem_inc(rest_done, 1)
                    with pe.If(total > 0):
                        with pe.Fori(0, total) as r:
                            pe.wait_ge(rest_in, r * (16 * G) + 16 * G)
                            pe.wait_ge(rest_hot, r + 2)
                            pe.wait_ge(rest_added, r + 1)
                            window_sum(6, [ring[:, j, :] for j in range(G)], [hot[:, j, :] for j in range(G)], rest_done)
                    pe.wait_ge(rest_added, total + 1)
                if kind == "outA":
                    if m == 0:
                        pe.wait_ge(m_ready, KC)
                        pe.wait_ge(qn_ready, QG)
                    group(kind, m, b, D, [(sumT[:, c, m * P:(m + 1) * P], w_sb[:, c, :]) for c in range(KC)])
                if kind == "outB":
                    if m >= 2:
                        gate(m - 2)
                    group(kind, m, b, D, [(qT[:, c, m * P:(m + 1) * P], m_sb[:, c, :]) for c in range(KC)])
                if kind == "x2T":
                    pe.wait_ge(rows2_ready, m + 1)
                    turn(kind, m, lambda c: rows2[:, m % 2, D + c * P:D + (c + 1) * P])
            gate(T - 2)
            gate(T - 1)
            pe.wait_ge(choice_ready, 1)
            every = choice[:, :, :].rearrange("p t e -> p (t e)")
            mm(ps[:, 7, 0:T * NE], before[:, :], every, start=True, stop=True)
            mm(ps[:, 7, 256:256 + T * NE], ones[:, :], every, start=True, stop=True).then_inc(rank_done, 1)
            pe.wait_ge(plan_ready, 1)
            blocks = pe.value_load(plan[0:1, BLOCKS:BLOCKS + 1], min_val=MIN_BLOCKS, max_val=BLOCKS)
            with pe.Fori(0, PAIRS) as q:
                for b in range(2):
                    with pe.If(q * 2 + b < blocks):
                        pe.wait_ge(xg_in[b], q * 32 + 32)
                        pe.wait_ge(yo_ready, q * 4 + 2 * b + 1)
                        for c in range(KC):
                            at = (c % 2) * BLK
                            nc.tensor.transpose(ps[:, c // 2, at:at + P], xg[:, b, 0, D + c * P:D + (c + 1) * P], ident[:, :])
                            ins = nc.tensor.transpose(ps[:, c // 2, at + P:at + BLK],
                                                      xg[0:B2ND, b, 1, D + c * P:D + (c + 1) * P], ident[0:B2ND, 0:B2ND])
                        ins.then_inc(xgT_done, 1)
                        pe.wait_ge(w_in[b], q * (16 * WP) + 32 * WP)
                        pe.wait_ge(xgT_act, q * 2 + (b + 1))
                        pe.wait_ge(xgT_dve, q * 2 + (b + 1))
                        for m in range(HC):
                            if m >= 4:
                                pe.wait_ge(h_ready, q * (2 * HC) + (b * HC + m - 3))
                            for c in range(KC):
                                ins = mm(ps[:, PRB[m % 4], 0:BLK], w1[b][:, c, m * P:(m + 1) * P], xgT[:, c, :],
                                         start=(c == 0), stop=(c == KC - 1))
                            ins.then_inc(h_done, 1)
                        for j in range(KC):
                            if j >= 2:
                                pe.wait_ge(y_ready, q * (2 * KC) + (b * KC + j - 1))
                            for m in range(HC):
                                if j == 0:
                                    pe.wait_ge(h_ready, q * (2 * HC) + (b * HC + m + 1))
                                ins = mm(ps[:, 6 + j % 2, 0:BLK], w2[b][:, m, j * P:(j + 1) * P], hT[:, m, :],
                                         start=(m == 0), stop=(m == HC - 1))
                            ins.then_inc(y_done, 1)
                        for j in range(KC):
                            pe.wait_ge(y_ready, q * (2 * KC) + (b * KC + j + 1))
                            nc.tensor.transpose(ps[:, 0, j * P:(j + 1) * P], yT[:, j, 0:P], ident[:, :])
                            ins = nc.tensor.transpose(ps[0:B2ND, 1, j * P:(j + 1) * P], yT[:, j, P:BLK], ident[:, :])
                        ins.then_inc(yr_done, 1)


def kernel(**inputs):
    import numpy as np
    import concourse.bacc as bacc
    from concourse.bass_utils import run_bass_kernel_spmd

    a = {k: np.asarray(v) for k, v in inputs.items()}

    def chunks(e):
        return np.ascontiguousarray(e.reshape(EC, P).T)

    def rows(w):
        return np.ascontiguousarray(w.reshape(-1, P, w.shape[-1]).transpose(1, 0, 2))

    pad = EC * P - E
    experts = np.concatenate([
        a["L0_ffn_W1"].reshape(NE, KC, P, H).transpose(0, 2, 1, 3).reshape(NE, P, KC * H),
        a["L0_ffn_W2"].reshape(NE, HC, P, D).transpose(0, 2, 1, 3).reshape(NE, P, HC * D),
        a["L0_ffn_b1"].reshape(NE, HC, P).transpose(0, 2, 1),
        a["L0_ffn_b2"].reshape(NE, KC, P).transpose(0, 2, 1)], axis=2)
    arrays = {
        "x": a["x"],
        "src": chunks(np.concatenate([a["src"], np.zeros(pad, a["src"].dtype)])),
        "dst": chunks(np.concatenate([a["dst"], np.full(pad, NP - 1, a["dst"].dtype)])),
        "ew": chunks(np.concatenate([a["edge_weight"], np.zeros(pad, a["edge_weight"].dtype)])),
        "wq": rows(a["L0_mix_Wq"].T), "wk": rows(a["L0_mix_Wk"].T), "wv": rows(a["L0_mix_Wv"].T), "wo": rows(a["L0_mix_Wo"].T),
        "wg_nn": rows(a["L0_gnn_W"]),
        "bq": np.ascontiguousarray(a["L0_mix_bq"].reshape(KC, P).T),
        "brow": np.stack([a["L0_mix_bk"], a["L0_mix_bv"], a["L0_gnn_b"], a["L0_mix_bo"]]),
        "gate_w": rows(a["L0_ffn_Wg"]),
        "gate_b": a["L0_ffn_bg"].reshape(1, NE),
        "experts": np.ascontiguousarray(experts),
    }
    nc = bacc.Bacc("TRN2", target_bir_lowering=False, num_devices=1)
    args = {k: nc.dram_tensor(f"in_{k}", v.shape, mybir.dt.from_np(v.dtype), kind="ExternalInput").ap() for k, v in arrays.items()}
    out = nc.dram_tensor("out_x", (N, D), F32, kind="ExternalOutput").ap()
    transformer_layer(nc, **args, out=out)
    r = run_bass_kernel_spmd(nc, [{f"in_{k}": v for k, v in arrays.items()}], core_ids=[0])
    return r.results[0]["out_x"]
```

```python
from contextlib import ExitStack

import concourse.bass as bass
from concourse import mybir

F32 = mybir.dt.float32
F32R = mybir.dt.float32r
BF16 = mybir.dt.bfloat16
I32 = mybir.dt.int32
U32 = mybir.dt.uint32
ALU = mybir.AluOpType
ACT = mybir.ActivationFunctionType
AX_X = mybir.AxisListType.X

P = 128
N = 1250
D = 512
HEAD = 64
E = 20000
NE = 8
H = 2 * D
T = -(-N // P)
LAST = N - (T - 1) * P
KC = D // P
HC = H // P
NP = T * P
EC = 160
G = 2
W = 64
EG = -(-E // (G * P))
PLAIN_V = 4
SLOTS = 8
DG = 16
BLK = 176
B2ND = BLK - P
BLOCKS = (N + NE * (BLK - 1)) // BLK // 2 * 2 + 2
PAIRS = BLOCKS // 2
WIDTHS = (P, 144, 160, BLK)
MIN_BLOCKS = -(-N // BLK)
WROW1 = KC * H + HC
WROW2 = HC * D + KC
WROW = WROW1 + WROW2
EPS = 1e-5
WP = 2
MORE = NP // W
NORMS = NP // 256
QG = KC * 3
VW = P + 2
assert EC * P >= E and EC % DG == 0 and EC >= EG * G and BLK * BLOCKS % P == 0


def n_blocks():
    return [(0, 512), (512, 512), (1024, NP - 1024)]


def transformer_layer(nc, x, src, dst, ew, wq, wk, wv, wo, wg_nn, bq, brow, gate_w, gate_b, experts, out):
    scaled_rows = nc.dram_tensor("scaled_rows", [NP, D], F32)
    token_rows = nc.dram_tensor("token_rows", [NP, 2 * D], F32)

    with ExitStack() as ctx:
        place = {}

        def sb(name, shape, dt=F32):
            place[name] = -(-nc.sbuf_base // 32) * 32
            return ctx.enter_context(nc.sbuf_tensor(name, shape, dt))

        def sem(name):
            return ctx.enter_context(nc.semaphore(name))

        xn = sb("xn", [P, T, D])
        k_sb = xn
        xT_ = sb("xT_", [P, KC * NP])
        xnT = xT_[:, :].rearrange("p (c n) -> p c n", c=KC)
        qT_ = sb("qT_", [P, KC * NP])
        qT = qT_[:, :].rearrange("p (c n) -> p c n", c=KC)
        sumT = sb("sumT", [P, KC, NP + W])
        ffw = sb("ffw", [P, 2, WROW])
        early = ffw[:, :, :].rearrange("p a n -> p (a n)")
        taken = [0]

        def part(n, rows=P):
            taken[0] += n
            assert taken[0] <= 2 * WROW
            return early[0:rows, taken[0] - n:taken[0]]

        ring = part(SLOTS * D).rearrange("p (s n) -> p s n", s=SLOTS)
        wq_sb, wk_sb, wv_sb = (part(KC * D).rearrange("p (c n) -> p c n", c=KC) for _ in range(3))
        v_sb = part(T * KC * VW).rearrange("p (t c n) -> p t c n", t=T, c=KC)
        dst_sb, dst_hi, dst_lo = (part(EC).bitcast(I32) for _ in range(3))
        dst_lof = part(EC // 2).bitcast(BF16)
        late = sb("late", [P, 3 * KC * D])
        w_sb = late[:, 0:KC * D].rearrange("p (c n) -> p c n", c=KC)
        wo_sb = late[:, KC * D:2 * KC * D].rearrange("p (c n) -> p c n", c=KC)
        late16 = late[:, :].bitcast(BF16)
        in_tile = late16[:, 0:T * EC].rearrange("p (t c) -> p t c", t=T)
        deg_coef = late16[:, T * EC:4 * T * EC].rearrange("p (c w t) -> p c w t", w=3, t=T)
        deg_hot = late16[:, 4 * T * EC:4 * T * EC + 2 * DG * P].rearrange("p (b c n) -> p b c n", b=2, c=DG)
        assert 4 * T * EC + 2 * DG * P <= 6 * KC * D

        hot = sb("hot", [P, SLOTS, W])
        src_sb = sb("src_sb", [P, EC], I32)
        dst_f = sb("dst_f", [P, EC])
        ew_sb = sb("ew_sb", [P, EC])
        rel = sb("rel", [P, EC])
        src_now = sb("src_now", [P, G], I32)
        edge_now = sb("edge_now", [P, 2, G])
        col_i = sb("col_i", [P, BLK], I32)
        col_f = sb("col_f", [P, BLK])
        col_h = sb("col_h", [P, P], BF16)
        token_i = sb("token_i", [P, T], I32)
        token_f = sb("token_f", [P, T])
        valid = sb("valid", [P, T])
        falling_i = sb("falling_i", [P, NE], I32)
        falling = sb("falling", [P, NE])
        blk_i = sb("blk_i", [P, BLOCKS], I32)
        blk_f = sb("blk_f", [P, BLOCKS])
        ident = sb("ident", [P, P])
        ends = sb("ends", [P, 2, 2])
        before = sb("before", [P, P])
        ones = sb("ones", [P, P])
        same_head = sb("same_head", [P, P])
        bq_sb = sb("bq_sb", [P, KC])
        brow_sb = sb("brow_sb", [P, 3, D])
        gw_sb = sb("gw_sb", [P, KC, NE])
        gb_sb = sb("gb_sb", [P, NE])
        stat = sb("stat", [P, T, 6])
        mv = sb("mv", [P, T, 2])
        veps = sb("veps", [P, T])
        std = sb("std", [P, T])
        rstd = sb("rstd", [P, T])
        shift = sb("shift", [P, T])
        deg = sb("deg", [P, T])
        deg3 = sb("deg3", [P, T])
        degpos = sb("degpos", [P, T])
        degroot = sb("degroot", [P, T])
        dinv = sb("dinv", [P, T])
        group_lo = sb("group_lo", [P, EG])
        group_hi = sb("group_hi", [P, EG])
        more_i = sb("more_i", [P, EG], I32)
        more = sb("more", [P, EG])
        after = sb("after", [P, EG])
        zero_g = sb("zero_g", [P, EG])
        window = sb("window", [1, EG], I32)
        rest = sb("rest", [1, EG + 1], I32)
        rest_end = sb("rest_end", [1, 1], I32)
        halves = sb("halves", [P, 6 * D])
        biased, low, expd = (halves[:, n * 2 * D:(n + 1) * 2 * D].rearrange("p (b n) -> p b n", b=2) for n in range(3))
        rows2 = halves[:, 0:4 * D].rearrange("p (b n) -> p b n", b=2)
        x2T = halves[:, 4 * D:6 * D].rearrange("p (b c n) -> p b c n", b=2, c=KC)
        ends_all = expd[:, 1, :].rearrange("p (a n) -> p a n", a=4)
        ew_left = expd[:, 0, 0:2 * EC].rearrange("p (a n) -> p a n", a=2)
        ew_h = biased[:, 1, 0:3 * EC // 2].bitcast(BF16).rearrange("p (a n) -> p a n", a=3)
        hi_h = biased[:, 1, 3 * EC // 2:2 * EC].bitcast(BF16)
        wv_place = wv_sb.rearrange("p c n -> p (c n)")
        kvm, kvT, ksm = (wv_place[:, n * D:(n + 1) * D].rearrange("p (c n) -> p c n", c=KC) for n in range(3))
        inv_norm = wk_sb[:, 0:2, :]
        def rounded(name, shape, over, floats):
            return nc.alloc_sbuf_tensor_at(name, shape, F32R, offset=place[over] + 4 * floats)

        w_lo = rounded("w_lo", [P, KC, D], "late", 0)
        w_hi = rounded("w_hi", [P, KC, D], "late", KC * D)
        m_hi = rounded("m_hi", [P, KC, D], "late", 2 * KC * D)
        m_lo = rounded("m_lo", [P, KC, D], "ffw", SLOTS * D)
        out_hi = rounded("out_hi", [P, 2, KC, P], "xT_", 0)
        out_lo = rounded("out_lo", [P, 2, KC, P], "xT_", 2 * D)
        wv_hi = rounded("wv_hi", [P, KC, D], "qT_", 0)
        wv_lo = rounded("wv_lo", [P, KC, D], "ffw", SLOTS * D + 2 * KC * D)
        wk_hi = rounded("wk_hi", [P, KC, D], "qT_", KC * D)
        wk_lo = rounded("wk_lo", [P, KC, D], "ffw", SLOTS * D + KC * D)
        proj_hi = rounded("proj_hi", [P, 2, KC, P], "late", 2 * KC * D)
        proj_lo = rounded("proj_lo", [P, 2, KC, P], "late", 2 * KC * D + 2 * D)
        logit = sb("logit", [P, T, NE])
        best = sb("best", [P, T])
        top = sb("top", [P, T, NE])
        choice = sb("choice", [P, T, NE])
        rank = sb("rank", [P, T, NE])
        count = sb("count", [P, NE])
        nblk = sb("nblk", [P, NE])
        blk_end = sb("blk_end", [P, NE])
        blk_start = sb("blk_start", [P, NE])
        pick = sb("pick", [P, T, NE])
        rank_t = sb("rank_t", [P, T])
        start_t = sb("start_t", [P, T])
        over_t = sb("over_t", [P, T])
        place_t = sb("place_t", [P, T])
        id_t = sb("id_t", [P, T])
        blk_slots = sb("blk_slots", [P, BLOCKS])
        full_e = sb("full_e", [P, NE, MIN_BLOCKS])
        over_all = sb("over_all", [P, T, MIN_BLOCKS - 1])
        blk_e = sb("blk_e", [1, BLOCKS])
        blk_over = sb("blk_over", [1, BLOCKS, NE - 1])
        plan = sb("plan", [1, BLOCKS + 1], I32)
        slots_a = sb("slots_a", [P, BLOCKS + 2], I32)
        slots_b = sb("slots_b", [B2ND, BLOCKS + 2], I32)
        now_a = sb("now_a", [P, 2, 2], I32)
        now_b = sb("now_b", [B2ND, 2, 2], I32)
        size = sb("size", [1, BLOCKS], I32)
        size_f = sb("size_f", [1, BLOCKS])
        size_end = sb("size_end", [1, NE])
        size_e = sb("size_e", [1, BLOCKS, NE])
        size_on = sb("size_on", [1, BLOCKS, NE])
        in_place = qT_[:, 0:T * BLK].rearrange("p (t s) -> p t s", t=T)
        in_block = qT_[:, T * BLK:T * (BLK + BLOCKS)].rearrange("p (t b) -> p t b", t=T)
        xg = xT_[:, 0:2 * 2 * 2 * D].rearrange("p (b s n) -> p b s n", b=2, s=2)
        xgT = qT_[:, 0:2 * KC * BLK].rearrange("p (b c n) -> p b c n", b=2, c=KC)
        hT = qT_[:, 2 * KC * BLK:(2 * KC + HC) * BLK].rearrange("p (c n) -> p c n", c=HC)
        yT = qT_[:, (2 * KC + HC) * BLK:(3 * KC + HC) * BLK].rearrange("p (c n) -> p c n", c=KC)
        yo = sumT[:, :, 0:D].rearrange("p (b s) n -> p b s n", b=2)
        w1 = [ffw[:, b, 0:KC * H].rearrange("p (c n) -> p c n", c=KC) for b in range(2)]
        b1 = [ffw[:, b, KC * H:WROW1] for b in range(2)]
        w2 = [ffw[:, b, WROW1:WROW1 + HC * D].rearrange("p (c n) -> p c n", c=HC) for b in range(2)]
        b2 = [ffw[:, b, WROW1 + HC * D:WROW] for b in range(2)]

        ps = ctx.enter_context(nc.psum_tensor("ps", [P, 8, 512], F32))
        TRB, PRB, SUMB = (0, 1), (2, 3, 4, 5), (6, 7, 1)

        x_in = [sem(f"x_in{t}") for t in range(T)]
        edges_in, src_in, stats_ready, x_again, wq_in, wk_in, wv_in, wwo_in, small_in, bo_in = (sem(s) for s in
            ("edges_in", "src_in", "stats_ready", "x_again", "wq_in", "wk_in", "wv_in", "wwo_in", "small_in", "bo_in"))
        pool_passed, dve_passed, sp_passed = (sem(s) for s in ("pool_passed", "dve_passed", "sp_passed"))
        const_set, x_pad_set = sem("const_set"), sem("x_pad_set")
        dve_step, pool_step = sem("dve_step"), sem("pool_step")
        var_ready, std_ready, rstd_ready, dinv_ready = (sem(s) for s in ("var_ready", "std_ready", "rstd_ready", "dinv_ready"))
        xn_ready, scaled_ready = ([sem(f"{name}_{by}") for by in ("dve", "act")] for name in ("xn_ready", "scaled_ready"))
        tr_done, tr_free = sem("tr_done"), sem("tr_free")
        mm_done, bank_free = sem("mm_done"), [sem(f"bank_free{b}") for b in range(len(PRB))]
        biased_ready, elu_done, deg_done = sem("biased_ready"), sem("elu_done"), sem("deg_done")
        low_ready, exp_done = sem("low_ready"), sem("exp_done")
        dst_ready, dst_turned, ends_ready, ends_done = (sem(s) for s in ("dst_ready", "dst_turned", "ends_ready", "ends_done"))
        coef_ready, deg_hot_ready, deg_hot_used = (sem(s) for s in ("coef_ready", "deg_hot_ready", "deg_hot_used"))
        hi_ready, lo_ready, w_hi_ready, w_lo_ready = (sem(s) for s in ("hi_ready", "lo_ready", "w_hi_ready", "w_lo_ready"))
        edges_split = sem("edges_split")
        root_ask, root_ready = sem("root_ask"), sem("root_ready")
        scaled_out = sem("scaled_out")
        windows_ready = sem("windows_ready")
        kv_masked, m_ready, qn_ready = sem("kv_masked"), sem("m_ready"), sem("qn_ready")
        gathered = [sem(f"gathered{s}") for s in range(SLOTS)]
        hot_ready, sum_done, sum_added = sem("hot_ready"), sem("sum_done"), sem("sum_added")
        rest_set, rest_in, rest_now, rest_hot, rest_done, rest_added = (sem(s) for s in
            ("rest_set", "rest_in", "rest_now", "rest_hot", "rest_done", "rest_added"))
        var2_ready, std2_ready, rows2_ready = (sem(s) for s in ("var2_ready", "std2_ready", "rows2_ready"))
        rows2_out = [sem(f"rows2_out{b}") for b in range(2)]
        logits_done, choice_ready, rank_done, plan_ready = (sem(s) for s in
            ("logits_done", "choice_ready", "rank_done", "plan_ready"))
        slots_asked, slots_done, slots_ready, now_set = (sem(s) for s in ("slots_asked", "slots_done", "slots_ready", "now_set"))
        size_ready, now_out = sem("size_ready"), sem("now_out")
        w1_in, w2_in = ([sem(f"w{a}_in{b}") for b in range(2)] for a in (1, 2))
        xg_in = [sem(f"xg_in{b}") for b in range(2)]
        out_done = [sem(f"out_done{b}") for b in range(2)]
        xgT_done, xgT_act, xgT_dve, h_done, h_ready, y_done, y_ready, yr_done, yo_ready = (sem(s) for s in
            ("xgT_done", "xgT_act", "xgT_dve", "h_done", "h_ready", "y_done", "y_ready", "yr_done", "yo_ready"))

        NB = n_blocks()
        norms = [("norm", j, b) for j in range(KC) for b in range(NORMS)]
        dense = [("v", t, 0) for t in range(T)] + [("k", t, 0) for t in range(T)] + [("q", 0, 0), ("k_end", 0, 0)]
        dense += [("q", 0, 1)] + [("kv", j, 0) for j in range(KC)] + [("q", 0, 2), ("kvT", 0, 0)]
        for m in range(1, KC):
            last = norms[(m - 1) * NORMS:m * NORMS]
            dense += [("q", m, 0)] + last[0:2] + [("q", m, 1)] + last[2:4] + [("q", m, 2)] + last[4:]
        dense += [("q_end", 0, 0), ("m", 0, 0)]
        for j, norm in enumerate(norms[(KC - 1) * NORMS:]):
            dense += [norm] + [("m", j + 1, 0)] * (j < KC - 1)
        order = [("xnT", t, 0) for t in range(T)]
        for n in range(EC // DG):
            if n < 3:
                order.insert(T - 5 + 3 * n, ("deg", n, 0))
            else:
                order.append(("deg", n, 0))
            if n in (2, 5):
                order.append(dense.pop(0))
        order += [("deg_end", 0, 0), dense.pop(0), dense.pop(0)]
        parted = dense[:T - PLAIN_V + T] + [("outB", t, 0) for t in range(T)] + [("outA", t, 0) for t in range(T)]
        first_out = 2 * T - PLAIN_V
        for n in range(first_out - 1, -1, -1):
            dense.insert(max(n - 1, 0), ("split", n, 0))
        at = dense.index(("v", PLAIN_V + 1, 0))
        dense[at:at] = [("splitW", KC + c, 0) for c in range(KC)]
        order += [("splitW", c, 0) for c in range(KC)] + dense[0:2] + [("xsT", t, 0) for t in range(T // 2)]
        order += dense[2:4] + [("xsT", t, 0) for t in range(T // 2, T)]
        dense = dense[4:]
        for t in range(T - 2):
            dense += ([("split", first_out, 0)] * (t == 0) + [("split", first_out + t + 1, 0), ("outB", t, 0)]
                      + [("splitW", 2 * KC + t - 1, 0)] * (1 <= t <= KC))
        share = {"q": 3.4, "k": 2.6, "v": 2.6, "kv": 2.2, "kvT": 1.2, "m": 1.5, "norm": 3.4, "outB": 2.6, "k_end": 0, "q_end": 0, "split": 0, "splitW": 0}
        wait = {("split", first_out, 0): 4.0}
        pace = (sum(share[item[0]] + wait.get(item, 0) for item in dense) - 4.0) / EG
        now, g = 0.0, 0
        for item in dense:
            while g < EG and 4.0 + pace * g < now:
                order.append(("agg", g, 0))
                g += 1
            order.append(item)
            now += share[item[0]] + wait.get(item, 0)
        order += [("agg", n, 0) for n in range(g, EG)] + [("rest", 0, 0)]
        order += [("split", first_out + T - 1, 0), ("outB", T - 2, 0), ("split", first_out + T, 0), ("outB", T - 1, 0)]
        for t in range(T):
            order += [("split", first_out + T + t + 1, 0)] * (t < T - 1) + [("outA", t, 0)] + [("x2T", t - 1, 0)] * (t > 0)
        order.append(("x2T", T - 1, 0))

        group_no = {g: i for i, g in enumerate([i for i in order if i[0] in ("q", "k", "v", "kv", "m", "norm", "outA", "outB")])}
        turn_no = {g: i for i, g in enumerate([i for i in order if i[0] in ("xnT", "xsT", "kvT", "x2T")])}

        def columns(n):
            kind, t, _ = parted[n]
            of = {"v": xnT, "k": xnT, "outB": qT, "outA": sumT}[kind]
            hi, lo = (proj_hi, proj_lo) if n < first_out else (out_hi, out_lo)
            return of[:, :, t * P:(t + 1) * P], hi[:, n % 2, :, :], lo[:, n % 2, :, :]

        def matrix(n):
            whole, hi, lo = ((wv_sb, wv_hi, wv_lo), (wk_sb, wk_hi, wk_lo), (w_sb, w_hi, w_lo))[n // KC]
            return whole[:, n % KC, :], hi[:, n % KC, :], lo[:, n % KC, :]

        assert TRB[turn_no[("kvT", 0, 0)] % 2] not in SUMB
        block = ctx.enter_context(nc.Block())

        @block.sync
        def _(sp):
            for t in range(0, T - 1, 2):
                sp.dma_start(xn[:, t, :], x[t * P:(t + 1) * P, :]).then_inc(x_in[t], 16)
            sp.wait_ge(x_pad_set, 1)
            sp.dma_start(xn[0:LAST, T - 1, :], x[(T - 1) * P:N, :]).then_inc(x_in[T - 1], 16)
            sp.dma_start(wv_sb, wv).then_inc(wv_in, 16)
            sp.dma_start(wk_sb, wk).then_inc(wk_in, 16)
            for t in range(T):
                sp.wait_ge(scaled_ready[t % 2], t // 2 + 1)
                sp.dma_start(scaled_rows[t * P:(t + 1) * P, :], xn[:, t, :]).then_inc(scaled_out, 16)
            sp.wait_ge(deg_done, 1)
            sp.dma_start(wo_sb, wo).then_inc(wwo_in, 16)
            sp.dma_start(w_sb, wg_nn).then_inc(wwo_in, 16)
            sp.wait_ge(elu_done, T)
            sp.dma_start(brow_sb[:, 0, :], brow[3:4, :].to_broadcast([P, D])).then_inc(bo_in, 16)

            def load_layer(e, b, layer, parts=range(WP)):
                first, n, done = ((0, WROW1 // WP, w1_in), (WROW1, WROW2 // WP, w2_in))[layer]
                for p in parts:
                    at = first + p * n
                    sp.dma_start(ffw[:, b, at:at + n],
                                 experts[bass.ds(e, 1), :, at:at + n].rearrange("a p n -> p (a n)")).then_inc(done[b], 16)

            sp.wait_ge(mm_done, group_no[("kv", KC - 1, 0)] + 1)
            sp.dma_start(xn[:, 0:T - 1, :], x[0:(T - 1) * P, :].rearrange("(t p) n -> p t n", p=P)).then_inc(x_again, 16)
            sp.dma_start(xn[0:LAST, T - 1, :], x[(T - 1) * P:N, :]).then_inc(x_again, 16)
            for t in range(T):
                sp.wait_ge(mm_done, group_no[("outA", t, 0)] + 1)
                if t < 4 * WP:
                    load_layer(t // (2 * WP), t // (2 * WP), t // WP % 2, [t % WP])
                sp.wait_ge(rows2_ready, t + 1)
                sp.dma_start(token_rows[t * P:(t + 1) * P, :], rows2[:, t % 2, :]).then_inc(rows2_out[t % 2], 16)
            sp.wait_ge(plan_ready, 1)
            blocks = sp.value_load(plan[0:1, BLOCKS:BLOCKS + 1], min_val=MIN_BLOCKS, max_val=BLOCKS)
            for b in range(2):
                e = sp.value_load(plan[0:1, b:b + 1], min_val=0, max_val=NE - 1)
                for layer, done in enumerate((w1_in, w2_in)):
                    with sp.If(e != b):
                        sp.wait_ge(done[b], WP * 16)
                        load_layer(e, b, layer)
                    with sp.If(e == b):
                        sp.sem_inc(done[b], WP * 16)
            with sp.Fori(0, PAIRS - 1) as q:
                for b in range(2):
                    with sp.If(q * 2 + (2 + b) < blocks):
                        e = sp.value_load(plan[0:1, bass.ds(q * 2 + (2 + b), 1)], min_val=0, max_val=NE - 1)
                        sp.wait_ge(h_ready, q * (2 * HC) + (b + 1) * HC)
                        sp.sem_inc(sp_passed, 1)
                        load_layer(e, b, 0)
                        sp.wait_ge(y_ready, q * (2 * KC) + (b + 1) * KC)
                        sp.wait_ge(xg_in[b], q * 32 + 64)
                        sp.sem_inc(sp_passed, 1)
                        load_layer(e, b, 1)

        @block.scalar
        def _(act):
            act.dma_start(dst_sb, dst).then_inc(edges_in, 16)
            act.dma_start(ew_sb[:, :], ew).then_inc(edges_in, 16)
            for t in range(1, T - 1, 2):
                act.dma_start(xn[:, t, :], x[t * P:(t + 1) * P, :]).then_inc(x_in[t], 16)
            act.dma_start(wq_sb, wq).then_inc(wq_in, 16)
            act.dma_start(bq_sb[:, :], bq).then_inc(small_in, 16)
            for n in range(3):
                act.dma_start(brow_sb[:, n, :], brow[n:n + 1, :].to_broadcast([P, D])).then_inc(small_in, 16)
            act.dma_start(gw_sb[:, :, :], gate_w).then_inc(small_in, 16)
            act.dma_start(gb_sb[:, :], gate_b.to_broadcast([P, NE])).then_inc(small_in, 16)
            act.dma_start(src_sb[:, :], src).then_inc(src_in, 16)

            def empty_turn(kind, t, to):
                n = turn_no[(kind, t, 0)]
                act.wait_ge(tr_done, n + 1)
                nc.scalar.activation(to, ps[:, TRB[n % 2], :].rearrange("p (c n) -> p c n", c=KC), ACT.Copy).then_inc(tr_free, 1)

            def q_bias(m, b):
                n, e, cols = group_no[("q", m, b)], T + 3 * m + b, NB[b][1]
                act.wait_ge(mm_done, n + 1)
                act.wait_ge(elu_done, e - 1)
                nc.scalar.activation(biased[:, e % 2, 0:cols], ps[:, PRB[n % 4], 0:cols], ACT.Identity,
                                     bias=bq_sb[:, m:m + 1]).then_inc(bank_free[n % 4], 1)
                act.wait_ge(bank_free[n % 4], n // 4 + 1)
                act.sem_inc(biased_ready, 1)

            def exp_low(e):
                cols = D if e < T else NB[(e - T) % 3][1]
                act.wait_ge(low_ready, e + 1)
                if e >= 2:
                    act.wait_ge(elu_done, e - 1)
                nc.scalar.activation(expd[:, e % 2, 0:cols], low[:, e % 2, 0:cols], ACT.Exp).then_inc(exp_done, 1)

            def std2(t):
                act.wait_ge(var2_ready, t + 1)
                nc.scalar.activation(std[:, t:t + 1], veps[:, t:t + 1], ACT.Sqrt).then_inc(std2_ready, 1)

            act.wait_ge(var_ready, 1)
            nc.scalar.activation(std[:, :], veps[:, :], ACT.Sqrt).then_inc(std_ready, 1)
            act.wait_ge(rstd_ready, 1)
            for kind, m, b in order:
                if kind == "xnT":
                    if m % 2 == 0 and m + 1 < T:
                        nc.scalar.activation(xn[:, m + 1, :], xn[:, m + 1, :], ACT.Identity, bias=shift[:, m + 1:m + 2],
                                             scale=rstd[:, m + 1:m + 2]).then_inc(xn_ready[1], 1)
                    empty_turn(kind, m, xnT[:, :, m * P:(m + 1) * P])
                if kind == "q":
                    if (m, b) == (0, 0):
                        act.wait_ge(small_in, 16 * 6)
                    q_bias(m, b)
                    if 3 * m + b:
                        exp_low(T + 3 * m + b - 1)
                if kind == "k" and m:
                    exp_low(m - 1)
                if kind == "k_end":
                    exp_low(T - 1)
                if kind == "q_end":
                    exp_low(T + QG - 1)
                if kind == "deg_end":
                    act.wait_ge(root_ask, 1)
                    nc.scalar.activation(degroot[:, :], deg[:, :], ACT.Sqrt).then_inc(root_ready, 1)
                    act.wait_ge(dinv_ready, 1)
                    act.wait_ge(tr_done, T)
                    for t in range(1, T, 2):
                        nc.scalar.activation(xn[:, t, :], xn[:, t, :], ACT.Copy, scale=dinv[:, t:t + 1]).then_inc(scaled_ready[1], 1)
                if kind == "xsT":
                    empty_turn(kind, m, sumT[:, :, m * P:(m + 1) * P])
                if kind == "kvT":
                    empty_turn(kind, m, kvT)
                if kind == "split":
                    if m == 0:
                        act.wait_ge(deg_done, 1)
                        act.wait_ge(tr_free, T)
                    if m == first_out:
                        act.wait_ge(qn_ready, KC * NORMS)
                    if m == first_out + T:
                        act.wait_ge(sum_added, EG)
                        rest_end_a = act.value_load(rest_end[0:1, 0:1], min_val=0, max_val=EG * MORE)
                        act.wait_ge(rest_added, rest_end_a + 1)
                    if m >= 2:
                        act.wait_ge(mm_done, group_no[parted[m - 2]] + 1)
                    whole, hi, _ = columns(m)
                    nc.scalar.activation(hi, whole, ACT.Copy).then_inc(hi_ready, 1)
                if kind == "splitW":
                    if m == 0:
                        act.wait_ge(wv_in, 16)
                    if m == KC:
                        act.wait_ge(wk_in, 16)
                    if m == 2 * KC:
                        act.wait_ge(wwo_in, 32)
                        act.wait_ge(m_ready, KC)
                    whole, hi, _ = matrix(m)
                    nc.scalar.activation(hi, whole, ACT.Copy).then_inc(w_hi_ready, 1)
                if kind == "outA" and m == 0:
                    std2(m)
                if kind == "x2T":
                    if m >= 2:
                        act.wait_ge(logits_done, m - 1)
                    empty_turn(kind, m, x2T[:, m % 2, :, :])
                    if m + 1 < T:
                        std2(m + 1)
            act.wait_ge(plan_ready, 1)
            blocks = act.value_load(plan[0:1, BLOCKS:BLOCKS + 1], min_val=MIN_BLOCKS, max_val=BLOCKS)

            def half_turned(b):
                nc.scalar.activation(xgT[:, b, 0:2, :], ps[:, 0, 0:2 * BLK].rearrange("p (c n) -> p c n", c=2),
                                     ACT.Copy).then_inc(xgT_act, 1)

            act.wait_ge(xgT_done, 1)
            half_turned(0)
            with act.Fori(0, PAIRS) as q:
                for b in range(2):
                    with act.If(q * 2 + b < blocks):
                        act.wait_ge(w1_in[b], q * (16 * WP) + 32 * WP)
                        for m in range(HC):
                            act.wait_ge(h_done, q * (2 * HC) + (b * HC + m + 1))
                            nc.scalar.activation(hT[:, m, :], ps[:, PRB[m % 4], 0:BLK], ACT.Relu,
                                                 bias=b1[b][:, m:m + 1]).then_inc(h_ready, 1)
                    with act.If(q * 2 + (b + 1) < blocks):
                        act.wait_ge(xgT_done, q * 2 + (b + 2))
                        half_turned(1 - b)


        @block.gpsimd
        def _(pool):
            steps = [0]

            def step(ins):
                steps[0] += 1
                ins.then_inc(pool_step, 1)
                pool.wait_ge(pool_step, steps[0])

            step(nc.gpsimd.memset(xn[96:P, T - 1, :], 0.0))
            pool.sem_inc(x_pad_set, 1)
            nc.gpsimd.iota(col_i[:, :], [[1, BLK]], base=0, channel_multiplier=0)
            nc.gpsimd.iota(token_i[:, :], [[P, T]], base=0, channel_multiplier=1)
            nc.gpsimd.iota(falling_i[:, :], [[-1, NE]], base=NE, channel_multiplier=0)
            nc.gpsimd.iota(blk_i[:, :], [[1, BLOCKS]], base=0, channel_multiplier=0)
            nc.gpsimd.memset(ident[:, :], 0.0)
            nc.gpsimd.memset(before[:, :], 1.0)
            nc.gpsimd.memset(ones[:, :], 1.0)
            nc.gpsimd.memset(sumT[:, :, NP:NP + W], 0.0)
            nc.gpsimd.memset(same_head[:, :], 0.0)
            step(nc.gpsimd.memset(zero_g[:, :], 0.0))
            step(nc.gpsimd.memset(same_head[0:HEAD, 0:HEAD], 1.0))
            step(nc.gpsimd.memset(same_head[HEAD:P, HEAD:P], 1.0))
            nc.gpsimd.affine_select(out=ident[:, :], in_=ident[:, :], compare_op=ALU.not_equal, fill=1.0,
                                    base=0, pattern=[[-1, P]], channel_multiplier=1)
            step(nc.gpsimd.affine_select(out=before[:, :], in_=before[:, :], compare_op=ALU.is_gt, fill=0.0,
                                         base=0, pattern=[[1, P]], channel_multiplier=-1))
            pool.sem_inc(const_set, 1)
            step(nc.gpsimd.memset(v_sb[:, :, :, P:VW], 1.0))
            pool.sem_inc(const_set, 1)
            pool.wait_ge(edges_split, 1)
            for w in range(3):
                ins = nc.gpsimd.tensor_tensor(deg_coef[:, :, w, :], in_tile.rearrange("p t c -> p c t"),
                                              ew_h[:, w, :][:, :, None].to_broadcast([P, EC, T]), ALU.mult)
            ins.then_inc(coef_ready, 1)

            def gather(to, idx, done):
                nc.gpsimd.indirect_dma_start(
                    out=to, out_offset=None, in_=scaled_rows[:, :],
                    in_offset=bass.IndirectOffsetOnAxis(ap=idx.bitcast(U32), axis=0)).then_inc(done, 16)

            pool.wait_ge(src_in, 16)
            pool.wait_ge(scaled_out, 16 * T)
            for c in range(EG * G):
                if c >= SLOTS:
                    pool.wait_ge(sum_done, (c - SLOTS) // G + 1)
                gather(ring[:, c % SLOTS, :], src_sb[:, c:c + 1], gathered[c % SLOTS])
            pool.wait_ge(sum_done, EG)
            total = pool.value_load(rest_end[0:1, 0:1], min_val=0, max_val=EG * MORE)
            with pool.If(total > 0):
                with pool.Fori(0, EG) as g:
                    r0 = pool.value_load(rest[0:1, bass.ds(g, 1)], min_val=0, max_val=EG * MORE)
                    r1 = pool.value_load(rest[0:1, bass.ds(g + 1, 1)], min_val=0, max_val=EG * MORE)
                    with pool.If(r0 < r1):
                        with pool.Fori(r0, r1) as r:
                            pool.wait_ge(rest_done, r + 1)
                            pool.sem_inc(pool_passed, 1)
                            nc.gpsimd.tensor_copy(src_now[:, :], src_sb[:, bass.ds(g * G, G)]).then_inc(rest_now, 1)
                            pool.wait_ge(rest_now, r + 1)
                            pool.sem_inc(pool_passed, 1)
                            for j in range(G):
                                gather(ring[:, j, :], src_now[:, j:j + 1], rest_in)
            pool.wait_ge(plan_ready, 1)
            pool.wait_ge(slots_ready, 2)
            for b in range(2):
                pool.wait_ge(rows2_out[b], 16 * len(range(b, T, 2)))
            blocks = pool.value_load(plan[0:1, BLOCKS:BLOCKS + 1], min_val=MIN_BLOCKS, max_val=BLOCKS)

            def indices(i, b, use, done):
                nc.gpsimd.tensor_copy(now_a[:, use, b:b + 1], slots_a[:, bass.ds(i, 1)]).then_inc(done, 1)
                nc.gpsimd.tensor_copy(now_b[:, use, b:b + 1], slots_b[:, bass.ds(i, 1)]).then_inc(done, 1)
                pool.wait_ge(done, i * 2 + 2)
                pool.sem_inc(pool_passed, 1)

            def fetch(i, b):
                indices(i, b, 0, now_set)
                for s, now in enumerate((now_a, now_b)):
                    nc.gpsimd.indirect_dma_start(
                        out=xg[0:now.shape[0], b, s, :], out_offset=None, in_=token_rows[:, :],
                        in_offset=bass.IndirectOffsetOnAxis(ap=now[:, 0, b:b + 1].bitcast(U32), axis=0),
                    ).then_inc(xg_in[b], 16)

            fetch(0, 0)
            fetch(1, 1)
            with pool.Fori(0, PAIRS) as q:
                for b in range(2):
                    with pool.If(q * 2 + b < blocks):
                        pool.wait_ge(yo_ready, q * 4 + (2 * b + 4))
                    with pool.If(q * 2 + (b + 2) < blocks):
                        pool.wait_ge(xg_in[b], q * 32 + 32)
                        fetch(q * 2 + (b + 2), b)
                    with pool.If(q * 2 + b < blocks):
                        with pool.If(q > 0):
                            pool.wait_ge(out_done[b], q * 32)
                            pool.sem_inc(pool_passed, 1)
                        indices(q * 2 + b, b, 1, now_out)
                        for s, now in enumerate((now_a, now_b)):
                            nc.gpsimd.indirect_dma_start(
                                out=out, out_offset=bass.IndirectOffsetOnAxis(ap=now[:, 1, b:b + 1].bitcast(U32), axis=0),
                                in_=yo[0:now.shape[0], b, s, :], in_offset=None,
                                bounds_check=N - 1, oob_is_err=False).then_inc(out_done[b], 16)
            half = nc.s_assert_within(blocks >> 1, MIN_BLOCKS // 2, PAIRS)
            more_0 = nc.s_assert_within((blocks + 1) >> 1, MIN_BLOCKS // 2, PAIRS)
            pool.wait_ge(out_done[0], more_0 * 32)
            pool.wait_ge(out_done[1], half * 32)


        @block.vector
        def _(dve):
            steps = [0]

            def step(ins):
                steps[0] += 1
                ins.then_inc(dve_step, 1)
                dve.wait_ge(dve_step, steps[0])

            v = nc.vector
            dve.wait_ge(edges_in, 32)
            v.tensor_scalar(dst_hi, dst_sb, 7, None, ALU.arith_shift_right)
            v.tensor_scalar(dst_lo, dst_sb, P - 1, None, ALU.bitwise_and)
            step(v.tensor_copy(ew_h[:, 0, :], ew_sb[:, :]))
            step(v.tensor_tensor(ew_left[:, 0, :], ew_sb[:, :], ew_h[:, 0, :], ALU.subtract))
            v.tensor_copy(hi_h, dst_hi)
            v.tensor_copy(dst_lof, dst_lo)
            step(v.tensor_copy(ew_h[:, 1, :], ew_left[:, 0, :]))
            step(v.tensor_tensor(ew_left[:, 1, :], ew_left[:, 0, :], ew_h[:, 1, :], ALU.subtract))
            for t in range(T):
                v.tensor_scalar(in_tile[:, t, :], hi_h, float(t), None, ALU.is_equal)
            v.tensor_copy(ew_h[:, 2, :], ew_left[:, 1, :]).then_inc(edges_split, 1)
            dve.wait_ge(const_set, 1)
            v.tensor_copy(col_f[:, :], col_i[:, :])
            v.tensor_copy(col_h[:, :], col_i[:, 0:P])
            v.tensor_copy(token_f[:, :], token_i[:, :])
            v.tensor_copy(falling[:, :], falling_i[:, :])
            v.tensor_copy(blk_f[:, :], blk_i[:, :])
            v.tensor_copy(dst_f[:, :], dst_sb).then_inc(dst_ready, 1)
            for t in range(T):
                dve.wait_ge(x_in[t], 16)
                v.bn_stats(stat[:, t, :], xn[:, t, :]).then_inc(stats_ready, 1)
            for t in range(T):
                dve.wait_ge(stats_ready, t + 1)
                ins = v.bn_aggr(mv[:, t, :], stat[:, t, :])
            step(ins)
            v.tensor_scalar(veps[:, :], mv[:, :, 1], EPS, None, ALU.add).then_inc(var_ready, 1)
            dve.wait_ge(std_ready, 1)
            step(v.reciprocal(rstd[:, :], std[:, :]))
            v.scalar_tensor_tensor(out=shift[:, :], in0=mv[:, :, 0], scalar=-1.0, in1=rstd[:, :], op0=ALU.mult,
                                   op1=ALU.mult).then_inc(rstd_ready, 1)
            for t in range(0, T, 2):
                v.tensor_scalar(xn[:, t, :], xn[:, t, :], mv[:, t, 0:1], rstd[:, t:t + 1], ALU.subtract,
                                ALU.mult).then_inc(xn_ready[0], 1)

            def deg_hots(n):
                if n >= 2:
                    dve.wait_ge(deg_hot_used, n - 1)
                v.tensor_tensor(deg_hot[:, n % 2, :, :], col_h[:, None, :].to_broadcast([P, DG, P]),
                                dst_lof[:, n * DG:(n + 1) * DG][:, :, None].to_broadcast([P, DG, P]), ALU.is_equal).then_inc(deg_hot_ready, 1)

            deg_hots(0)
            dve.wait_ge(dst_turned, 1)
            for a, r in ((0, P), (1, EC - P)):
                v.tensor_reduce(ends[0:r, a, 0:1], ps[0:r, 7, a * P:(a + 1) * P], AX_X, ALU.min)
                ins = v.tensor_reduce(ends[0:r, a, 1:2], ps[0:r, 7, a * P:(a + 1) * P], AX_X, ALU.max)
            step(ins)
            for a, r in ((0, P), (1, EC - P)):
                for w in range(2):
                    ins = v.tensor_scalar(ends_all[0:r, 2 * a + w, :], ones[0:r, :], ends[0:r, a, w:w + 1], None, ALU.mult)
            ins.then_inc(ends_ready, 1)
            deg_hots(1)

            def windows():
                dve.wait_ge(ends_done, 1)
                v.tensor_reduce(group_lo[:, :], ps[:, 7, 0:EG * G].rearrange("p (g c) -> p g c", c=G), AX_X, ALU.min)
                step(v.tensor_reduce(group_hi[:, :], ps[:, 7, 256:256 + EG * G].rearrange("p (g c) -> p g c", c=G), AX_X, ALU.max))
                v.tensor_tensor(rel[:, 0:EG * G].rearrange("p (g c) -> p g c", c=G), dst_f[:, 0:EG * G].rearrange("p (g c) -> p g c", c=G),
                                group_lo[:, :][:, :, None].to_broadcast([P, EG, G]), ALU.subtract)
                v.tensor_copy(window[:, :], group_lo[0:1, :])
                step(v.tensor_tensor(more_i[:, :], group_hi[:, :], group_lo[:, :], ALU.subtract))
                step(v.tensor_scalar(more_i[:, :], more_i[:, :], W.bit_length() - 1, None, ALU.arith_shift_right))
                step(v.tensor_copy(more[:, :], more_i[:, :]))
                step(v.tensor_tensor_scan(after[:, :], more[:, :], zero_g[:, :], 0.0, ALU.add, ALU.add))
                v.memset(rest[:, 0:1], 0)
                v.tensor_copy(rest[:, 1:EG + 1], after[0:1, :])
                step(v.tensor_copy(rest_end[:, :], after[0:1, EG - 1:EG]))
                dve.sem_inc(windows_ready, 1)

            def degrees():
                dve.wait_ge(deg_done, 1)
                step(v.tensor_scalar(deg3[:, :], ps[:, 6, 0:T], 1.0, None, ALU.add))
                step(v.tensor_tensor(deg3[:, :], deg3[:, :], ps[:, 6, T:2 * T], ALU.add))
                step(v.tensor_tensor(deg3[:, :], deg3[:, :], ps[:, 6, 2 * T:3 * T], ALU.add))
                v.tensor_scalar(degpos[:, :], deg3[:, :], 0.0, None, ALU.is_gt)
                v.tensor_scalar(deg[:, :], deg3[:, :], 1e-37, None, ALU.max).then_inc(root_ask, 1)
                dve.wait_ge(root_ready, 1)
                step(v.reciprocal(dinv[:, :], degroot[:, :]))
                step(v.tensor_tensor(dinv[:, :], dinv[:, :], degpos[:, :], ALU.mult))
                dve.sem_inc(dinv_ready, 1)
                dve.wait_ge(tr_done, T)
                for t in range(0, T, 2):
                    v.tensor_scalar(xn[:, t, :], xn[:, t, :], dinv[:, t:t + 1], None, ALU.mult).then_inc(scaled_ready[0], 1)

            def bank_of(kind, m, b=0):
                n = group_no[(kind, m, b)]
                dve.wait_ge(mm_done, n + 1)
                return bank_free[n % 4], ps[:, PRB[n % 4], :]

            def low_of(e, y, cols):
                if e >= 2:
                    dve.wait_ge(exp_done, e - 1)
                v.tensor_scalar(low[:, e % 2, 0:cols], y, 0.0, None, ALU.min).then_inc(low_ready, 1)

            def q_low(m, b):
                e, cols = T + 3 * m + b, NB[b][1]
                dve.wait_ge(biased_ready, 3 * m + b + 1)
                low_of(e, biased[:, e % 2, 0:cols], cols)

            def k_low(t):
                if t == 0:
                    dve.wait_ge(scaled_out, 16 * T)
                    dve.wait_ge(tr_done, turn_no[("xsT", T - 1, 0)] + 1)
                free, bank = bank_of("k", t)
                step(v.tensor_tensor(k_sb[:, t, :], bank, brow_sb[:, 0, :], ALU.add))
                dve.sem_inc(free, 1)
                low_of(t, k_sb[:, t, :], D)

            def elu(e):
                if e >= T:
                    first, cols = NB[(e - T) % 3]
                    y, to = biased[:, e % 2, 0:cols], qT[:, (e - T) // 3, first:first + cols]
                else:
                    cols = D
                    y = to = k_sb[:, e, :]
                dve.wait_ge(exp_done, e + 1)
                v.scalar_tensor_tensor(out=to, in0=y, scalar=0.0, in1=expd[:, e % 2, 0:cols],
                                       op0=ALU.max, op1=ALU.add).then_inc(elu_done, 1)

            def hots(g):
                if g >= EG:
                    return
                if g >= SLOTS // G:
                    dve.wait_ge(sum_done, g - SLOTS // G + 1)
                for c in range(g * G, (g + 1) * G):
                    ins = v.tensor_scalar(hot[:, c % SLOTS, :], col_f[:, 0:W], rel[:, c:c + 1], ew_sb[:, c:c + 1],
                                          ALU.is_equal, ALU.mult)
                ins.then_inc(hot_ready, 1)

            def add_window(bank, start):
                to = sumT[:, :, bass.ds(start, W)]
                return v.tensor_tensor(to, ps[:, bank, 0:KC * W].rearrange("p (c n) -> p c n", c=KC), to, ALU.add)

            def rest_windows():
                total = dve.value_load(rest_end[0:1, 0:1], min_val=0, max_val=EG * MORE)
                dve.sem_inc(rest_hot, 1)
                dve.sem_inc(rest_set, 1)
                dve.sem_inc(rest_added, 1)
                dve.wait_ge(sum_added, EG)
                with dve.If(total > 0):
                    with dve.Fori(0, EG) as g:
                        r0 = dve.value_load(rest[0:1, bass.ds(g, 1)], min_val=0, max_val=EG * MORE)
                        r1 = dve.value_load(rest[0:1, bass.ds(g + 1, 1)], min_val=0, max_val=EG * MORE)
                        start = dve.value_load(window[0:1, bass.ds(g, 1)], min_val=0, max_val=NP - 1)
                        dve.wait_ge(rest_hot, r0 + 1)
                        dve.wait_ge(rest_set, r0 + g + 1)
                        v.tensor_copy(edge_now[:, 0, :], rel[:, bass.ds(g * G, G)])
                        v.tensor_copy(edge_now[:, 1, :], ew_sb[:, bass.ds(g * G, G)]).then_inc(rest_set, 1)
                        with dve.If(r0 < r1):
                            with dve.Fori(r0, r1) as r:
                                dve.wait_ge(rest_hot, r + 1)
                                dve.wait_ge(rest_set, r + g + 2)
                                v.tensor_scalar(edge_now[:, 0, :], edge_now[:, 0, :], float(-W), None, ALU.add).then_inc(rest_set, 1)
                                dve.wait_ge(rest_set, r + g + 3)
                                for j in range(G):
                                    ins = v.tensor_scalar(hot[:, j, :], col_f[:, 0:W], edge_now[:, 0, j:j + 1],
                                                          edge_now[:, 1, j:j + 1], ALU.is_equal, ALU.mult)
                                ins.then_inc(rest_hot, 1)
                                dve.wait_ge(rest_done, r + 2)
                                dve.wait_ge(rest_added, r + 1)
                                at = nc.s_assert_within(start + (r - r0 + 1) * W, 0, NP - 1,
                                                        skip_runtime_bounds_check_because="further windows start at or before the group's greatest destination")
                                add_window(6, at).then_inc(rest_added, 1)

            def out_rows(t):
                b = t % 2
                free, bank = bank_of("outA", t)
                if t >= 2:
                    dve.wait_ge(rows2_out[b], 16 * (t // 2))
                    dve.wait_ge(tr_done, turn_no[("x2T", t - 2, 0)] + 1)
                step(v.scalar_tensor_tensor(out=rows2[:, b, 0:D], in0=bank, scalar=dinv[:, t:t + 1], in1=xn[:, t, :],
                                            op0=ALU.mult, op1=ALU.add))
                dve.sem_inc(free, 1)
                step(v.bn_stats(stat[:, t, :], rows2[:, b, 0:D]))
                step(v.bn_aggr(mv[:, t, :], stat[:, t, :]))
                v.tensor_scalar(veps[:, t:t + 1], mv[:, t, 1:2], EPS, None, ALU.add).then_inc(var2_ready, 1)
                dve.wait_ge(std2_ready, t + 1)
                step(v.reciprocal(rstd[:, t:t + 1], std[:, t:t + 1]))
                v.tensor_scalar(rows2[:, b, D:2 * D], rows2[:, b, 0:D], mv[:, t, 0:1], rstd[:, t:t + 1],
                                ALU.subtract, ALU.mult).then_inc(rows2_ready, 1)

            dve.wait_ge(small_in, 16 * 6)
            dve.wait_ge(const_set, 2)
            dve_order = list(order)
            for i, item in enumerate(order):
                if item[0] == "v" and order[i + 1][0] == "deg":
                    dve_order[i:i + 2] = [order[i + 1], item]
            for kind, m, b in dve_order:
                if kind == "q":
                    q_low(m, b)
                    if 3 * m + b:
                        elu(T + 3 * m + b - 1)
                if kind == "deg":
                    if m + 2 < EC // DG:
                        deg_hots(m + 2)
                if kind == "deg_end":
                    degrees()
                    windows()
                if kind == "k":
                    k_low(m)
                    if m:
                        elu(m - 1)
                if kind == "k_end":
                    elu(T - 1)
                if kind == "q_end":
                    elu(T + QG - 1)
                if kind == "v":
                    free, bank = bank_of(kind, m)
                    v.tensor_tensor(v_sb[:, m, :, 0:P], bank.rearrange("p (c n) -> p c n", c=KC),
                                    brow_sb[:, 1, :].rearrange("p (c n) -> p c n", c=KC), ALU.add).then_inc(free, 1)
                if kind == "kv":
                    free, bank = bank_of(kind, m)
                    v.tensor_tensor(kvm[:, m, :], bank[:, 0:P], same_head[:, :], ALU.mult)
                    step(v.tensor_scalar(ksm[:, m, :], same_head[:, :], bank[:, P:P + 1], None, ALU.mult))
                    dve.sem_inc(free, 1)
                    dve.sem_inc(kv_masked, 1)
                if kind == "m":
                    free, bank = bank_of(kind, m)
                    step(v.tensor_copy(m_hi[:, m, :], bank))
                    step(v.tensor_tensor(m_lo[:, m, :], bank, m_hi[:, m, :], ALU.subtract))
                    dve.sem_inc(free, 1)
                    dve.sem_inc(m_ready, 1)
                if kind == "norm":
                    first, cols = b * 256, 256
                    free, bank = bank_of(kind, m, b)
                    step(v.tensor_scalar(inv_norm[:, b % 2, 0:cols], bank[:, 0:cols], 1e-6, None, ALU.add))
                    dve.sem_inc(free, 1)
                    step(v.reciprocal(inv_norm[:, b % 2, 0:cols], inv_norm[:, b % 2, 0:cols]))
                    step(v.tensor_tensor(qT[:, m, first:first + cols], qT[:, m, first:first + cols], inv_norm[:, b % 2, 0:cols], ALU.mult))
                    dve.sem_inc(qn_ready, 1)
                if kind == "agg":
                    if m == 0:
                        for g in range(SLOTS // G - 1):
                            hots(g)
                        dve.wait_ge(tr_free, turn_no[("xsT", T - 1, 0)] + 1)
                    hots(m + SLOTS // G - 1)
                    start = dve.value_load(window[0:1, m:m + 1], min_val=0, max_val=NP - 1)
                    dve.wait_ge(sum_done, m + 1)
                    if m:
                        dve.wait_ge(sum_added, m)
                    add_window(SUMB[m % len(SUMB)], start).then_inc(sum_added, 1)
                if kind == "rest":
                    rest_windows()
                if kind == "split":
                    dve.wait_ge(hi_ready, m + 1)
                    whole, hi, lo = columns(m)
                    v.tensor_tensor(lo, whole, hi, ALU.subtract).then_inc(lo_ready, 1)
                if kind == "splitW":
                    dve.wait_ge(w_hi_ready, m + 1)
                    whole, hi, lo = matrix(m)
                    v.tensor_tensor(lo, whole, hi, ALU.subtract).then_inc(w_lo_ready, 1)
                if kind == "outB":
                    if m == 0:
                        dve.wait_ge(bo_in, 16)
                        step(v.tensor_tensor(brow_sb[:, 2, :], brow_sb[:, 2, :], brow_sb[:, 0, :], ALU.add))
                        dve.wait_ge(x_again, 32)
                    free, bank = bank_of(kind, m)
                    step(v.tensor_tensor(xn[:, m, :], bank, xn[:, m, :], ALU.add))
                    dve.sem_inc(free, 1)
                    step(v.tensor_tensor(xn[:, m, :], xn[:, m, :], brow_sb[:, 2, :], ALU.add))
                if kind == "outA":
                    out_rows(m)
            v.tensor_scalar(blk_slots[:, :], blk_f[:, :], float(BLK), None, ALU.mult)
            v.tensor_scalar(id_t[:, :], token_f[:, :], float(N), 0.0, ALU.subtract, ALU.min)
            v.tensor_scalar(valid[:, :], token_f[:, :], float(N), None, ALU.is_lt)
            dve.wait_ge(logits_done, T)
            step(v.tensor_tensor(logit[:, :, :], ps[:, 6, 0:T * NE].rearrange("p (t e) -> p t e", t=T),
                                 gb_sb[:, None, :].to_broadcast([P, T, NE]), ALU.add))
            step(v.tensor_reduce(best[:, :], logit[:, :, :], AX_X, ALU.max))
            step(v.tensor_tensor(top[:, :, :], logit[:, :, :], best[:, :][:, :, None].to_broadcast([P, T, NE]), ALU.is_equal))
            step(v.tensor_tensor(top[:, :, :], top[:, :, :], falling[:, None, :].to_broadcast([P, T, NE]), ALU.mult))
            step(v.tensor_reduce(best[:, :], top[:, :, :], AX_X, ALU.max))
            step(v.tensor_tensor(choice[:, :, :], best[:, :][:, :, None].to_broadcast([P, T, NE]),
                                 falling[:, None, :].to_broadcast([P, T, NE]), ALU.is_equal))
            v.tensor_tensor(choice[:, :, :], choice[:, :, :], valid[:, :][:, :, None].to_broadcast([P, T, NE]), ALU.mult).then_inc(choice_ready, 1)
            dve.wait_ge(rank_done, 1)
            step(v.memset(count[:, :], 0.0))
            for t in range(T):
                v.tensor_tensor(rank[:, t, :], ps[:, 7, t * NE:(t + 1) * NE], count[:, :], ALU.add)
                step(v.tensor_tensor(count[:, :], ps[:, 7, 256 + t * NE:256 + (t + 1) * NE], count[:, :], ALU.add))
            step(v.tensor_tensor(full_e[:, :, :], count[:, :, None].to_broadcast([P, NE, MIN_BLOCKS]),
                                 blk_slots[:, None, 0:MIN_BLOCKS].to_broadcast([P, NE, MIN_BLOCKS]), ALU.is_gt))
            step(v.tensor_reduce(nblk[:, :], full_e[:, :, :], AX_X, ALU.add))
            step(v.tensor_tensor_scan(blk_end[:, :], nblk[:, :], zero_g[:, 0:NE], 0.0, ALU.add, ALU.add))
            v.tensor_tensor(pick[:, :, :], choice[:, :, :], rank[:, :, :], ALU.mult)
            step(v.tensor_tensor(blk_start[:, :], blk_end[:, :], nblk[:, :], ALU.subtract))
            step(v.tensor_reduce(rank_t[:, :], pick[:, :, :], AX_X, ALU.add))
            v.tensor_tensor(over_all[:, :, :], rank_t[:, :, None].to_broadcast([P, T, MIN_BLOCKS - 1]),
                            blk_slots[:, None, 1:MIN_BLOCKS].to_broadcast([P, T, MIN_BLOCKS - 1]), ALU.is_ge)
            step(v.tensor_tensor(pick[:, :, :], choice[:, :, :], blk_start[:, None, :].to_broadcast([P, T, NE]), ALU.mult))
            v.tensor_reduce(over_t[:, :], over_all[:, :, :], AX_X, ALU.add)
            step(v.tensor_reduce(start_t[:, :], pick[:, :, :], AX_X, ALU.add))
            v.tensor_tensor(start_t[:, :], start_t[:, :], over_t[:, :], ALU.add)
            step(v.scalar_tensor_tensor(out=place_t[:, :], in0=over_t[:, :], scalar=float(-BLK), in1=rank_t[:, :],
                                        op0=ALU.mult, op1=ALU.add))
            v.tensor_tensor(in_place[:, :, :], place_t[:, :, None].to_broadcast([P, T, BLK]),
                            col_f[:, None, :].to_broadcast([P, T, BLK]), ALU.is_equal)
            step(v.tensor_tensor(in_block[:, :, :], start_t[:, :, None].to_broadcast([P, T, BLOCKS]),
                                 blk_f[:, None, :].to_broadcast([P, T, BLOCKS]), ALU.is_equal))
            v.tensor_tensor(in_block[:, :, :], in_block[:, :, :], id_t[:, :, None].to_broadcast([P, T, BLOCKS]), ALU.mult).then_inc(slots_asked, 1)
            step(v.tensor_tensor(blk_over[:, :, :], blk_f[0:1, :, None].to_broadcast([1, BLOCKS, NE - 1]),
                                 blk_end[0:1, None, 0:NE - 1].to_broadcast([1, BLOCKS, NE - 1]), ALU.is_ge))
            step(v.tensor_reduce(blk_e[:, :], blk_over[:, :, :], AX_X, ALU.add))
            v.tensor_copy(plan[:, 0:BLOCKS], blk_e[:, :])
            step(v.tensor_copy(plan[:, BLOCKS:BLOCKS + 1], blk_end[0:1, NE - 1:NE]))
            dve.sem_inc(plan_ready, 1)
            dve.wait_ge(slots_done, 1)
            v.tensor_scalar(slots_a[:, 0:BLOCKS], ps[:, 7, 0:BLOCKS], float(N), None, ALU.add).then_inc(slots_ready, 1)
            v.tensor_scalar(slots_b[:, 0:BLOCKS], ps[0:B2ND, 6, 0:BLOCKS], float(N), None, ALU.add).then_inc(slots_ready, 1)
            blk0 = blk_f[0:1, :, None].to_broadcast([1, BLOCKS, NE])
            step(v.scalar_tensor_tensor(out=size_end[:, :], in0=blk_start[0:1, :], scalar=float(BLK), in1=count[0:1, :],
                                        op0=ALU.mult, op1=ALU.add))
            v.tensor_tensor(size_on[:, :, :], blk0, blk_start[0:1, None, :].to_broadcast([1, BLOCKS, NE]), ALU.is_ge)
            step(v.scalar_tensor_tensor(out=size_e[:, :, :], in0=blk0, scalar=float(-BLK),
                                        in1=size_end[:, None, :].to_broadcast([1, BLOCKS, NE]), op0=ALU.mult, op1=ALU.add))
            step(v.tensor_tensor(size_e[:, :, :], size_e[:, :, :], size_on[:, :, :], ALU.mult))
            step(v.tensor_reduce(size_f[:, :], size_e[:, :, :], AX_X, ALU.max))
            step(v.tensor_scalar(size_f[:, :], size_f[:, :], float(BLK), 0.0, ALU.min, ALU.max))
            v.tensor_copy(size[:, :], size_f[:, :]).then_inc(size_ready, 1)
            def half_turned(b):
                v.tensor_copy(xgT[:, b, 2:4, :], ps[:, 1, 0:2 * BLK].rearrange("p (c n) -> p c n", c=2)).then_inc(xgT_dve, 1)

            dve.sem_inc(yo_ready, 2)
            blocks = dve.value_load(plan[0:1, BLOCKS:BLOCKS + 1], min_val=MIN_BLOCKS, max_val=BLOCKS)
            dve.wait_ge(xgT_done, 1)
            half_turned(0)
            with dve.Fori(0, PAIRS) as q:
                for b in range(2):
                    with dve.If(q * 2 + (b + 1) < blocks):
                        dve.wait_ge(xgT_done, q * 2 + (b + 2))
                        half_turned(1 - b)
                    with dve.If(q * 2 + b < blocks):
                        dve.wait_ge(w2_in[b], q * (16 * WP) + 32 * WP)
                        for j in range(KC):
                            dve.wait_ge(y_done, q * (2 * KC) + (b * KC + j + 1))
                            v.tensor_scalar(yT[:, j, :], ps[:, 6 + j % 2, 0:BLK], b2[b][:, j:j + 1], None, ALU.add).then_inc(y_ready, 1)
                        with dve.If(q > 0):
                            dve.wait_ge(out_done[b], q * 32)
                            dve.sem_inc(dve_passed, 1)
                        dve.wait_ge(xg_in[b], q * 32 + 32)
                        dve.wait_ge(yr_done, q * 2 + (b + 1))
                        v.tensor_tensor(yo[:, b, 0, :], ps[:, 0, :], xg[:, b, 0, 0:D], ALU.add).then_inc(yo_ready, 1)
                        v.tensor_tensor(yo[0:B2ND, b, 1, :], ps[0:B2ND, 1, :], xg[0:B2ND, b, 1, 0:D], ALU.add).then_inc(yo_ready, 1)

        @block.tensor
        def _(pe):
            mm = nc.tensor.matmul

            def in_parts(kind, t, b_hi, b_lo):
                n = parted.index((kind, t, 0))
                pe.wait_ge(w_lo_ready, KC * {"v": 1, "k": 2, "outB": 2, "outA": 3}[kind])
                pe.wait_ge(lo_ready, n + 1)
                _, a_hi, a_lo = columns(n)
                return [part for c in range(KC) for part in
                        ((a_lo[:, c, :], b_hi[:, c, :]), (a_hi[:, c, :], b_lo[:, c, :]), (a_hi[:, c, :], b_hi[:, c, :]))]

            def turn(kind, t, block_of):
                n = turn_no[(kind, t, 0)]
                if n >= 2:
                    pe.wait_ge(tr_free, n - 1)
                for c in range(KC):
                    ins = nc.tensor.transpose(ps[:, TRB[n % 2], c * P:(c + 1) * P], block_of(c), ident[:, :])
                ins.then_inc(tr_done, 1)

            def group(kind, m, b, cols, parts):
                n = group_no[(kind, m, b)]
                if n >= 4:
                    pe.wait_ge(bank_free[n % 4], n // 4)
                for i, (left, right) in enumerate(parts):
                    ins = mm(ps[:, PRB[n % 4], 0:cols], left, right, start=(i == 0), stop=(i == len(parts) - 1))
                ins.then_inc(mm_done, 1)

            def window_sum(bank, rows, hots, done):
                for c in range(KC):
                    for j in range(G):
                        ins = mm(ps[:, bank, c * W:(c + 1) * W], rows[j][:, c * P:(c + 1) * P], hots[j],
                                 start=(j == 0), stop=(j == G - 1))
                ins.then_inc(done, 1)

            def gate(t):
                pe.wait_ge(tr_free, turn_no[("x2T", t, 0)] + 1)
                for c in range(KC):
                    ins = mm(ps[:, 6, t * NE:(t + 1) * NE], x2T[:, t % 2, c, :], gw_sb[:, c, :], start=(c == 0), stop=(c == KC - 1))
                ins.then_inc(logits_done, 1)

            pe.wait_ge(const_set, 1)
            pe.wait_ge(dst_ready, 1)
            nc.tensor.transpose(ps[:, 7, 0:P], dst_f[:, 0:P], ident[:, :])
            nc.tensor.transpose(ps[0:EC - P, 7, P:2 * P], dst_f[:, P:EC], ident[:, :]).then_inc(dst_turned, 1)
            for kind, m, b in order:
                if kind == "xnT":
                    pe.wait_ge(xn_ready[m % 2], m // 2 + 1)
                    turn(kind, m, lambda c: xn[:, m, c * P:(c + 1) * P])
                if kind == "q":
                    first, cols = NB[b]
                    pe.wait_ge(wq_in, 16)
                    group(kind, m, b, cols, [(wq_sb[:, c, m * P:(m + 1) * P], xnT[:, c, first:first + cols]) for c in range(KC)])
                if kind == "deg":
                    if m == 0:
                        pe.wait_ge(ends_ready, 1)
                        for w in range(2):
                            mm(ps[:, 7, w * 256:w * 256 + P], ends_all[:, w, :], ident[:, :], start=True, stop=True)
                            ins = mm(ps[:, 7, w * 256 + P:w * 256 + EC], ends_all[0:EC - P, 2 + w, :], ident[0:EC - P, 0:EC - P],
                                     start=True, stop=True)
                        ins.then_inc(ends_done, 1)
                        pe.wait_ge(coef_ready, 1)
                    pe.wait_ge(deg_hot_ready, m + 1)
                    for c in range(DG):
                        ins = mm(ps[:, 6, 0:3 * T], deg_hot[:, m % 2, c, :], deg_coef[:, m * DG + c, :, :].rearrange("p w t -> p (w t)"),
                                 start=(m == 0 and c == 0), stop=(m == EC // DG - 1 and c == DG - 1), skip_group_check=True)
                    ins.then_inc(deg_hot_used, 1)
                if kind == "deg_end":
                    pe.wait_ge(deg_hot_used, EC // DG)
                    pe.sem_inc(deg_done, 1)
                if kind == "xsT":
                    pe.wait_ge(scaled_ready[m % 2], m // 2 + 1)
                    turn(kind, m, lambda c: xn[:, m, c * P:(c + 1) * P])
                if kind == "k":
                    pe.wait_ge(wk_in, 16)
                    group(kind, m, b, D, in_parts(kind, m, wk_hi, wk_lo))
                if kind == "v":
                    pe.wait_ge(wv_in, 16)
                    pe.wait_ge(tr_free, m + 1)
                    if m < PLAIN_V:
                        group(kind, m, b, D, [(xnT[:, c, m * P:(m + 1) * P], wv_sb[:, c, :]) for c in range(KC)])
                    else:
                        group(kind, m, b, D, in_parts(kind, m, wv_hi, wv_lo))
                if kind == "kv":
                    if m == 0:
                        pe.wait_ge(elu_done, T)
                        n = group_no[("v", T - 1, 0)]
                        for last in range(n - 3, n + 1):
                            pe.wait_ge(bank_free[last % 4], last // 4 + 1)
                    rows = [P] * (T - 1) + [LAST]
                    group(kind, m, b, VW, [(k_sb[0:r, t, m * P:(m + 1) * P], v_sb[0:r, t, m, :]) for t, r in enumerate(rows)])
                if kind == "kvT":
                    pe.wait_ge(kv_masked, KC)
                    turn(kind, m, lambda c: kvm[:, c, :])
                if kind == "m":
                    if m == 0:
                        pe.wait_ge(wwo_in, 32)
                        pe.wait_ge(tr_free, turn_no[("kvT", 0, 0)] + 1)
                    group(kind, m, b, D, [(kvT[:, m, :], wo_sb[:, m, :])])
                if kind == "norm":
                    first, cols = b * 256, 256
                    pe.wait_ge(elu_done, T + 3 * m + first // 512 + 1)
                    group(kind, m, b, cols, [(ksm[:, m, :], qT[:, m, first:first + cols])])
                if kind == "agg":
                    if m == 0:
                        pe.wait_ge(tr_free, 2 * T)
                    if m >= len(SUMB):
                        pe.wait_ge(sum_added, m - len(SUMB) + 1)
                    pe.wait_ge(hot_ready, m + 1)
                    slots = [(m * G + j) % SLOTS for j in range(G)]
                    for s in slots:
                        pe.wait_ge(gathered[s], 16 * (m * G // SLOTS + 1))
                    window_sum(SUMB[m % len(SUMB)], [ring[:, s, :] for s in slots], [hot[:, s, :] for s in slots], sum_done)
                if kind == "rest":
                    pe.wait_ge(sum_added, EG)
                    pe.wait_ge(windows_ready, 1)
                    total = pe.value_load(rest_end[0:1, 0:1], min_val=0, max_val=EG * MORE)
                    pe.sem_inc(rest_done, 1)
                    with pe.If(total > 0):
                        with pe.Fori(0, total) as r:
                            pe.wait_ge(rest_in, r * (16 * G) + 16 * G)
                            pe.wait_ge(rest_hot, r + 2)
                            pe.wait_ge(rest_added, r + 1)
                            window_sum(6, [ring[:, j, :] for j in range(G)], [hot[:, j, :] for j in range(G)], rest_done)
                    pe.wait_ge(rest_added, total + 1)
                if kind == "outA":
                    group(kind, m, b, D, in_parts(kind, m, w_hi, w_lo))
                    if m >= 2:
                        gate(m - 2)
                if kind == "outB":
                    if m == 0:
                        pe.wait_ge(m_ready, KC)
                        pe.wait_ge(qn_ready, KC * NORMS)
                    group(kind, m, b, D, in_parts(kind, m, m_hi, m_lo))
                if kind == "x2T":
                    pe.wait_ge(rows2_ready, m + 1)
                    turn(kind, m, lambda c: rows2[:, m % 2, D + c * P:D + (c + 1) * P])
            gate(T - 2)
            gate(T - 1)
            pe.wait_ge(choice_ready, 1)
            every = choice[:, :, :].rearrange("p t e -> p (t e)")
            mm(ps[:, 7, 0:T * NE], before[:, :], every, start=True, stop=True)
            mm(ps[:, 7, 256:256 + T * NE], ones[:, :], every, start=True, stop=True).then_inc(rank_done, 1)
            pe.wait_ge(slots_asked, 1)
            for t in range(T):
                mm(ps[:, 7, 0:BLOCKS], in_place[:, t, 0:P], in_block[:, t, :], start=(t == 0), stop=(t == T - 1))
            for t in range(T):
                ins = mm(ps[0:B2ND, 6, 0:BLOCKS], in_place[:, t, P:BLK], in_block[:, t, :], start=(t == 0), stop=(t == T - 1))
            ins.then_inc(slots_done, 1)
            pe.wait_ge(plan_ready, 1)
            blocks = pe.value_load(plan[0:1, BLOCKS:BLOCKS + 1], min_val=MIN_BLOCKS, max_val=BLOCKS)

            def turn_rows(b):
                for c in range(KC):
                    at = (c % 2) * BLK
                    nc.tensor.transpose(ps[:, c // 2, at:at + P], xg[:, b, 0, D + c * P:D + (c + 1) * P], ident[:, :])
                    ins = nc.tensor.transpose(ps[:, c // 2, at + P:at + BLK],
                                              xg[0:B2ND, b, 1, D + c * P:D + (c + 1) * P], ident[0:B2ND, 0:B2ND])
                ins.then_inc(xgT_done, 1)

            def turn_results(i):
                pe.wait_ge(y_ready, i * KC)
                for j in range(KC):
                    nc.tensor.transpose(ps[:, 0, j * P:(j + 1) * P], yT[:, j, 0:P], ident[:, :])
                    ins = nc.tensor.transpose(ps[0:B2ND, 1, j * P:(j + 1) * P], yT[:, j, P:BLK], ident[:, :])
                ins.then_inc(yr_done, 1)

            def layers(q, b, width):
                for m in range(HC):
                    if m == 2 and b:
                        turn_results(q * 2 + 1)
                    elif m == 2:
                        with pe.If(q > 0):
                            turn_results(q * 2)
                    if m >= 4:
                        pe.wait_ge(h_ready, q * (2 * HC) + (b * HC + m - 3))
                    for c in range(KC):
                        ins = mm(ps[:, PRB[m % 4], 0:width], w1[b][:, c, m * P:(m + 1) * P], xgT[:, b, c, 0:width],
                                 start=(c == 0), stop=(c == KC - 1))
                    ins.then_inc(h_done, 1)
                with pe.If(q * 2 + (b + 1) < blocks):
                    pe.wait_ge(xg_in[1 - b], q * 32 + (32 + 32 * b))
                    pe.wait_ge(yo_ready, q * 4 + (2 * b + 2))
                    turn_rows(1 - b)
                pe.wait_ge(w2_in[b], q * (16 * WP) + 32 * WP)
                for j in range(KC):
                    if j >= 2:
                        pe.wait_ge(y_ready, q * (2 * KC) + (b * KC + j - 1))
                    for m in range(HC):
                        if j == 0:
                            pe.wait_ge(h_ready, q * (2 * HC) + (b * HC + m + 1))
                        ins = mm(ps[:, 6 + j % 2, 0:width], w2[b][:, m, j * P:(j + 1) * P], hT[:, m, 0:width],
                                 start=(m == 0), stop=(m == HC - 1))
                    ins.then_inc(y_done, 1)

            pe.wait_ge(xg_in[0], 32)
            turn_rows(0)
            pe.wait_ge(size_ready, 1)
            with pe.Fori(0, PAIRS) as q:
                for b in range(2):
                    with pe.If(q * 2 + b < blocks):
                        tokens = pe.value_load(size[0:1, bass.ds(q * 2 + b, 1)], min_val=0, max_val=BLK)
                        pe.wait_ge(w1_in[b], q * (16 * WP) + 32 * WP)
                        pe.wait_ge(xgT_act, q * 2 + (b + 1))
                        pe.wait_ge(xgT_dve, q * 2 + (b + 1))
                        with pe.If(tokens <= WIDTHS[0]):
                            layers(q, b, WIDTHS[0])
                        for less, width in zip(WIDTHS, WIDTHS[1:]):
                            with pe.If(tokens > less):
                                with pe.If(tokens <= width):
                                    layers(q, b, width)
            turn_results(blocks)


def kernel(**inputs):
    import numpy as np
    import concourse.bacc as bacc
    from concourse.bass_utils import run_bass_kernel_spmd

    a = {k: np.asarray(v) for k, v in inputs.items()}

    def chunks(e):
        return np.ascontiguousarray(e.reshape(EC, P).T)

    def rows(w):
        return np.ascontiguousarray(w.reshape(-1, P, w.shape[-1]).transpose(1, 0, 2))

    pad = EC * P - E
    experts = np.concatenate([
        a["L0_ffn_W1"].reshape(NE, KC, P, H).transpose(0, 2, 1, 3).reshape(NE, P, KC * H),
        a["L0_ffn_b1"].reshape(NE, HC, P).transpose(0, 2, 1),
        a["L0_ffn_W2"].reshape(NE, HC, P, D).transpose(0, 2, 1, 3).reshape(NE, P, HC * D),
        a["L0_ffn_b2"].reshape(NE, KC, P).transpose(0, 2, 1)], axis=2)
    arrays = {
        "x": a["x"],
        "src": chunks(np.concatenate([a["src"], np.zeros(pad, a["src"].dtype)])),
        "dst": chunks(np.concatenate([a["dst"], np.full(pad, NP - 1, a["dst"].dtype)])),
        "ew": chunks(np.concatenate([a["edge_weight"], np.zeros(pad, a["edge_weight"].dtype)])),
        "wq": rows(a["L0_mix_Wq"].T), "wk": rows(a["L0_mix_Wk"].T), "wv": rows(a["L0_mix_Wv"].T), "wo": rows(a["L0_mix_Wo"].T),
        "wg_nn": rows(a["L0_gnn_W"]),
        "bq": np.ascontiguousarray(a["L0_mix_bq"].reshape(KC, P).T),
        "brow": np.stack([a["L0_mix_bk"], a["L0_mix_bv"], a["L0_gnn_b"], a["L0_mix_bo"]]),
        "gate_w": rows(a["L0_ffn_Wg"]),
        "gate_b": a["L0_ffn_bg"].reshape(1, NE),
        "experts": np.ascontiguousarray(experts),
    }
    nc = bacc.Bacc("TRN2", target_bir_lowering=False, num_devices=1)
    args = {k: nc.dram_tensor(f"in_{k}", v.shape, mybir.dt.from_np(v.dtype), kind="ExternalInput").ap() for k, v in arrays.items()}
    out = nc.dram_tensor("out_x", (N, D), F32, kind="ExternalOutput").ap()
    transformer_layer(nc, **args, out=out)
    r = run_bass_kernel_spmd(nc, [{f"in_{k}": v for k, v in arrays.items()}], core_ids=[0])
    return r.results[0]["out_x"]
```
